# Optimizing a Trainium2 kernel written in Bass

```python
import numpy as np
import jax
import jax.numpy as jnp

def _softmax(x, axis=-1):
    return jax.nn.softmax(x, axis=axis)

def _gelu(x):
    return jax.nn.gelu(x, approximate=True)

def _silu(x):
    return jax.nn.silu(x)

def _sigmoid(x):
    return jax.nn.sigmoid(x)

def _layernorm(x, axis=-1, eps=1e-05):
    m = jnp.mean(x, axis=axis, keepdims=True)
    v = jnp.var(x, axis=axis, keepdims=True)
    return (x - m) / jnp.sqrt(v + eps)

def _scatter_add(tgt, idx, src, axis=0):
    return tgt.at[idx].add(src)

def _segment_sum(src, seg, n):
    return jax.ops.segment_sum(src, seg, n)
kernel_name = 'mk_adaln_ffn_d2_seqx_r4_64c977'

def setup_inputs(seed: int=0):
    np.random.seed(seed)
    _w = jnp.asarray

    def _rec_inputs():
        import jax
        import jax.numpy as jnp
        _rk = jax.random.key(seed)
        x = -0.000125 + 0.9999 * jax.random.normal(jax.random.fold_in(_rk, 1), (64, 64, 256), jnp.float32)
        _lenS = 64 - jax.random.randint(jax.random.fold_in(_rk, 7), (64,), 0, max(1, 64 // 4) + 1, jnp.int32)
        _lenS2 = 64 - jax.random.randint(jax.random.fold_in(_rk, 8), (64,), 0, max(1, 64 // 4) + 1, jnp.int32)
        cond_1024 = 0.00782532 + 1.00527 * jax.random.normal(jax.random.fold_in(_rk, 11), (64, 256), jnp.float32)
        return (x, cond_1024)
    x, cond_1024 = _rec_inputs()

    def _L0_cond_setup():
        import jax, jax.numpy as jnp
        import numpy as np
        NHID = 256
        NHEAD = 16
        HEAD_DIM = 64
        B, L = (8, 1024)
        key = jax.random.key(seed)
        ks = jax.random.split(key, 12)
        s_in = 1.0 / np.sqrt(NHID)
        s_o = 1.0 / np.sqrt(NHEAD * HEAD_DIM)
        return {'x': jax.random.normal(ks[0], (B, L, NHID), dtype=jnp.float32), 'ax': jax.random.normal(ks[1], (B, NHID), dtype=jnp.float32), 'WQ_w': jax.random.normal(ks[2], (NHID, NHEAD * HEAD_DIM), dtype=jnp.float32) * s_in, 'WQ_b': jnp.zeros((NHEAD * HEAD_DIM,), dtype=jnp.float32), 'WK_w': jax.random.normal(ks[3], (NHID, NHEAD * HEAD_DIM), dtype=jnp.float32) * s_in, 'WK_b': jnp.zeros((NHEAD * HEAD_DIM,), dtype=jnp.float32), 'WV_w': jax.random.normal(ks[4], (NHID, NHEAD * HEAD_DIM), dtype=jnp.float32) * s_in, 'WV_b': jnp.zeros((NHEAD * HEAD_DIM,), dtype=jnp.float32), 'WO_w': jax.random.normal(ks[5], (NHEAD * HEAD_DIM, NHID), dtype=jnp.float32) * s_o, 'WO_b': jnp.zeros((NHID,), dtype=jnp.float32)}
    _L0_cond_all = _L0_cond_setup()
    _L0_cond_in = {k: v for k, v in _L0_cond_all.items() if k in ('WQ_w', 'WQ_b', 'WK_w', 'WK_b', 'WV_w', 'WV_b', 'WO_w', 'WO_b')}
    del _L0_cond_all

    def _L0_ffn_setup():
        import jax, jax.numpy as jnp
        import numpy as np
        B, N, C, H, REG = (1, 2309, 256, 16, 5)
        D = C // H
        key = jax.random.key(seed)
        k0, k1, k2, k3 = jax.random.split(key, 4)
        x = jax.random.normal(k0, (B, N, C), dtype=jnp.float32)
        g_info = jax.random.normal(k1, (12, 2, C), dtype=jnp.float32)
        W_qkv = jax.random.normal(k2, (C, 3 * C), dtype=jnp.float32) * 0.02
        W_proj = jax.random.normal(k3, (C, C), dtype=jnp.float32) * 0.02
        b_proj = jnp.zeros((C,), dtype=jnp.float32)
        return {'x': x, 'g_info': g_info, 'W_qkv': W_qkv, 'W_proj': W_proj, 'b_proj': b_proj}
    _L0_ffn_all = _L0_ffn_setup()
    _L0_ffn_in = {k: v for k, v in _L0_ffn_all.items() if k in ('g_info', 'W_qkv', 'W_proj', 'b_proj')}
    del _L0_ffn_all

    def _L1_cond_setup():
        import jax, jax.numpy as jnp
        import numpy as np
        N, T, D, H = (64, 128, 256, 256)
        key = jax.random.key(seed)
        k1, k2, k3, k4 = jax.random.split(key, 4)
        x = jax.random.normal(k1, (N, T, D), dtype=jnp.float32)
        h0 = jax.random.normal(k2, (N, H), dtype=jnp.float32)
        Wx = jax.random.normal(k3, (D, H), dtype=jnp.float32) / np.sqrt(D)
        Wh = jax.random.normal(k4, (H, H), dtype=jnp.float32) / np.sqrt(H)
        b = jnp.zeros((H,), dtype=jnp.float32)
        return {'x': x, 'h0': h0, 'Wx': Wx, 'Wh': Wh, 'b': b}
    _L1_cond_all = _L1_cond_setup()
    _L1_cond_in = {k: v for k, v in _L1_cond_all.items() if k in ('Wx', 'Wh', 'b')}
    del _L1_cond_all

    def _L1_ffn_setup():
        import jax, jax.numpy as jnp
        import numpy as np
        E = 8
        C = 320
        D = 256
        H = 1024
        B, S = (4, 512)
        key = jax.random.key(seed)
        ks = jax.random.split(key, 12)
        sc = 0.02
        return {'input': jax.random.normal(ks[0], (B, S, D), jnp.float32), 'router_w': jax.random.normal(ks[1], (D, E), jnp.float32) * sc, 'router_b': jnp.zeros((E,), jnp.float32), 'w1': jax.random.normal(ks[2], (E, D, H), jnp.float32) * sc, 'b1': jnp.zeros((E, H), jnp.float32), 'w2': jax.random.normal(ks[3], (E, H, D), jnp.float32) * sc, 'b2': jnp.zeros((E, D), jnp.float32), 'ow1': jax.random.normal(ks[4], (D, H), jnp.float32) * sc, 'ob1': jnp.zeros((H,), jnp.float32), 'ow2': jax.random.normal(ks[5], (H, D), jnp.float32) * sc, 'ob2': jnp.zeros((D,), jnp.float32)}
    _L1_ffn_all = _L1_ffn_setup()
    _L1_ffn_in = {k: v for k, v in _L1_ffn_all.items() if k in ('router_w', 'router_b', 'w1', 'b1', 'w2', 'b2', 'ow1', 'ob1', 'ow2', 'ob2')}
    del _L1_ffn_all
    return {'x': x, 'cond_1024': cond_1024, 'L0_cond_WQ_w': _L0_cond_in['WQ_w'], 'L0_cond_WQ_b': _L0_cond_in['WQ_b'], 'L0_cond_WK_w': _L0_cond_in['WK_w'], 'L0_cond_WK_b': _L0_cond_in['WK_b'], 'L0_cond_WV_w': _L0_cond_in['WV_w'], 'L0_cond_WV_b': _L0_cond_in['WV_b'], 'L0_cond_WO_w': _L0_cond_in['WO_w'], 'L0_cond_WO_b': _L0_cond_in['WO_b'], 'L0_ffn_g_info': _L0_ffn_in['g_info'], 'L0_ffn_W_qkv': _L0_ffn_in['W_qkv'], 'L0_ffn_W_proj': _L0_ffn_in['W_proj'], 'L0_ffn_b_proj': _L0_ffn_in['b_proj'], 'L1_cond_Wx': _L1_cond_in['Wx'], 'L1_cond_Wh': _L1_cond_in['Wh'], 'L1_cond_b': _L1_cond_in['b'], 'L1_ffn_router_w': _L1_ffn_in['router_w'], 'L1_ffn_router_b': _L1_ffn_in['router_b'], 'L1_ffn_w1': _L1_ffn_in['w1'], 'L1_ffn_b1': _L1_ffn_in['b1'], 'L1_ffn_w2': _L1_ffn_in['w2'], 'L1_ffn_b2': _L1_ffn_in['b2'], 'L1_ffn_ow1': _L1_ffn_in['ow1'], 'L1_ffn_ob1': _L1_ffn_in['ob1'], 'L1_ffn_ow2': _L1_ffn_in['ow2'], 'L1_ffn_ob2': _L1_ffn_in['ob2']}

def reference(x, cond_1024, L0_cond_WQ_w, L0_cond_WQ_b, L0_cond_WK_w, L0_cond_WK_b, L0_cond_WV_w, L0_cond_WV_b, L0_cond_WO_w, L0_cond_WO_b, L0_ffn_g_info, L0_ffn_W_qkv, L0_ffn_W_proj, L0_ffn_b_proj, L1_cond_Wx, L1_cond_Wh, L1_cond_b, L1_ffn_router_w, L1_ffn_router_b, L1_ffn_w1, L1_ffn_b1, L1_ffn_w2, L1_ffn_b2, L1_ffn_ow1, L1_ffn_ob1, L1_ffn_ow2, L1_ffn_ob2):
    import jax
    import jax.numpy as jnp

    def _L0_cond_ref(x, ax, WQ_w, WQ_b, WK_w, WK_b, WV_w, WV_b, WO_w, WO_b):
        import jax, jax.numpy as jnp
        import numpy as np
        NHID = 256
        NHEAD = 16
        HEAD_DIM = 64
        B, L = (8, 1024)
        Bx, Lx, H = x.shape
        nh, d = (NHEAD, HEAD_DIM)
        q = (x @ WQ_w + WQ_b).reshape(Bx, Lx, nh, d)
        k = (x @ WK_w + WK_b).reshape(Bx, Lx, nh, d)
        ak = (ax @ WK_w + WK_b).reshape(Bx, 1, nh, d)
        av = (ax @ WV_w + WV_b).reshape(Bx, 1, nh, d)
        pad_k = jnp.pad(k, ((0, 0), (1, 1), (0, 0), (0, 0)))
        k_shift = jnp.stack([pad_k[:, t:Lx + t] for t in range(3)], axis=3)
        akb = jnp.broadcast_to(ak, (Bx, Lx, nh, d))[:, :, :, None, :]
        avb = jnp.broadcast_to(av, (Bx, Lx, nh, d))[:, :, :, None, :]
        K = jnp.concatenate([akb, k_shift], axis=3)
        V = jnp.concatenate([avb, k_shift], axis=3)
        scores = jnp.einsum('blhd,blhjd->blhj', q, K) / jnp.sqrt(jnp.float32(d))
        alphas = jax.nn.softmax(scores, axis=-1)
        att = jnp.einsum('blhj,blhjd->blhd', alphas, V).reshape(Bx, Lx, nh * d)
        return att @ WO_w + WO_b

    def _L0_ffn_ref(x, g_info, W_qkv, W_proj, b_proj):
        import jax, jax.numpy as jnp
        import numpy as np
        B, N, C, H, REG = (1, 2309, 256, 16, 5)
        D = C // H
        Bx, Nx, Cx = x.shape
        scale = D ** (-0.5)
        qkv = (x @ W_qkv).reshape(Bx, Nx, 3, H, D)
        q, k, v = (qkv[:, :, 0], qkv[:, :, 1], qkv[:, :, 2])
        g_layer = g_info[0].reshape(-1, H, D)
        q_g = g_layer[0]
        q_pure = q[:, REG:]
        q_n = q_pure / jnp.linalg.norm(q_pure, axis=-1, keepdims=True)
        qg_n = q_g / jnp.linalg.norm(q_g, axis=-1, keepdims=True)
        sim = (qg_n[None, None] * q_n).sum(-1).mean(-1)
        sim = (sim - sim.min()) / (sim.max() - sim.min())
        pos = sim > 0.9
        logits = jnp.einsum('bqhd,bkhd->bhqk', q * scale, k)

        def masked_attn(tok_mask):
            key_mask = jnp.concatenate([jnp.ones((Bx, REG), bool), tok_mask], axis=1)
            l = jnp.where(key_mask[:, None, None, :], logits, -jnp.inf)
            a = jax.nn.softmax(l, axis=-1)
            return jnp.einsum('bhqk,bkhd->bqhd', a, v)
        x_pos = masked_attn(pos)
        x_neg = masked_attn(~pos)
        reg_out = (x_pos[:, :REG] + x_neg[:, :REG]) * 0.5
        tok_out = jnp.where(pos[:, :, None, None], x_pos[:, REG:], x_neg[:, REG:])
        out = jnp.concatenate([reg_out, tok_out], axis=1).reshape(Bx, Nx, Cx)
        return out @ W_proj + b_proj

    def _L1_cond_ref(x, h0, Wx, Wh, b):
        import jax, jax.numpy as jnp
        import numpy as np
        N, T, D, H = (64, 128, 256, 256)
        xW = jnp.einsum('ntd,dh->nth', x, Wx) + b
        xW_t = jnp.swapaxes(xW, 0, 1)

        def step(prev_h, xw):
            next_h = jnp.tanh(prev_h @ Wh + xw)
            return (next_h, next_h)
        _, h_t = jax.lax.scan(step, h0, xW_t)
        return jnp.swapaxes(h_t, 0, 1)

    def _L1_ffn_ref(input, router_w, router_b, w1, b1, w2, b2, ow1, ob1, ow2, ob2):
        import jax, jax.numpy as jnp
        import numpy as np
        E = 8
        C = 320
        D = 256
        H = 1024
        B, S = (4, 512)
        Bq, Sq, Dq = input.shape
        N = Bq * Sq
        xf = input.reshape(N, Dq)
        probs = jax.nn.softmax(xf @ router_w + router_b, axis=-1)
        eid = jnp.argmax(probs, axis=-1)
        onehot = jax.nn.one_hot(eid, E, dtype=xf.dtype)
        rank = (jnp.cumsum(onehot, axis=0)[jnp.arange(N), eid] - 1.0).astype(jnp.int32)
        valid = rank < C
        pos = jnp.where(valid, rank, 0)
        vmask = valid.astype(xf.dtype)[:, None]
        buf = jnp.zeros((E, C, Dq), xf.dtype).at[eid, pos].add(xf * vmask)
        h = jax.nn.relu(jnp.einsum('ecd,edh->ech', buf, w1) + b1[:, None, :])
        y = jnp.einsum('ech,ehd->ecd', h, w2) + b2[:, None, :]
        y_tok = y[eid, pos] * vmask
        yov = jax.nn.relu(xf @ ow1 + ob1) @ ow2 + ob2
        out = y_tok + yov * (1.0 - vmask)
        return out.reshape(Bq, Sq, Dq)
    x = x + _L0_ffn_ref(_L0_cond_ref(x, cond_1024, L0_cond_WQ_w, L0_cond_WQ_b, L0_cond_WK_w, L0_cond_WK_b, L0_cond_WV_w, L0_cond_WV_b, L0_cond_WO_w, L0_cond_WO_b), L0_ffn_g_info, L0_ffn_W_qkv, L0_ffn_W_proj, L0_ffn_b_proj)
    x = x + _L1_ffn_ref(_L1_cond_ref(x, cond_1024, L1_cond_Wx, L1_cond_Wh, L1_cond_b), L1_ffn_router_w, L1_ffn_router_b, L1_ffn_w1, L1_ffn_b1, L1_ffn_w2, L1_ffn_b2, L1_ffn_ow1, L1_ffn_ob1, L1_ffn_ow2, L1_ffn_ob2)
    return x

_drawn_inputs = setup_inputs


def setup_inputs(seed=0):
    import zlib

    import numpy as np

    out = dict(_drawn_inputs(seed))
    spreads = {'L0_cond_WQ_b': (0.0, 0.8),
     'L0_cond_WK_b': (0.0, 0.45),
     'L0_cond_WV_b': (0.0, 0.729),
     'L0_cond_WO_b': (0.0, 0.395),
     'L0_ffn_b_proj': (0.0, 0.1),
     'L1_cond_b': (0.0, 0.1),
     'L1_ffn_router_b': (0.0, 0.1),
     'L1_ffn_b1': (0.0, 0.1),
     'L1_ffn_b2': (0.0, 0.1),
     'L1_ffn_ob1': (0.0, 0.27),
     'L1_ffn_ob2': (0.0, 0.1)}
    factors = {'L0_cond_WQ_w': 3.906, 'L0_cond_WK_w': 2.812, 'L0_ffn_g_info': 8.0}
    for name, (base, spread) in spreads.items():
        noise = np.random.default_rng([zlib.crc32(name.encode()), seed]).standard_normal(out[name].shape)
        drawn = base * np.exp(spread * noise) if base else spread * noise
        out[name] = jnp.asarray(drawn.astype(out[name].dtype))
    for name, factor in factors.items():
        out[name] = (out[name] * factor).astype(out[name].dtype)
    return out
```

```python
from contextlib import ExitStack

import numpy as np

import concourse.bass as bass
from concourse import mybir

ALU = mybir.AluOpType
ACT = mybir.ActivationFunctionType
F32 = mybir.dt.float32
BF16 = mybir.dt.bfloat16
U32 = mybir.dt.uint32
X = mybir.AxisListType.X

P = 128
B, L, D = 64, 64, 256
KT = D // P
PAIRS = B // 2
H0, HD0 = 16, 64
HT = H0 * HD0 // P
H1, HD1 = 16, 16
REG = 5
W0 = L + 2
SPB = 4
NSLOT = H1 + 2
E, CAP, HID = 8, 320, 1024
FT = HID // P
STEPS2 = L // 2
XROWS = E * CAP
NEG = -1.0e30
CAPT = [(0, 128), (128, 128), (256, 64)]


def shape_constants():
    p = np.arange(P)
    ident = np.eye(P, dtype=np.float32)
    band = np.full((P, 2, W0), NEG, np.float32)
    for q in range(P):
        for head, first, extra in ((0, 1, 0), (1, 0, L)):
            for j in (q % L - 1, q % L, q % L + 1):
                if 0 <= j < L:
                    band[q, head, first + j] = 0.0
            band[q, head, extra] = 0.0
            if q % L in (0, L - 1):
                band[q, head, L + 1] = 0.0
    band = band.reshape(P, -1)
    head8 = (p[:, None] // HD1 == np.arange(8)[None]).astype(np.float32)
    head16 = np.zeros((P, KT, H1), np.float32)
    for t in range(KT):
        head16[:, t, 8 * t:8 * t + 8] = head8
    same_head = (p[:, None] // HD1 == p[None] // HD1).astype(np.float32)
    same_seq = (p[:, None] // L == p[None] // L).astype(np.float32)
    key_diag = (p[:, None] % L == np.arange(L)[None]).astype(np.float32)
    tok_row = np.tile((np.arange(L) >= REG).astype(np.float32)[None], (P, 1))
    is_tok = ((p % L) >= REG).astype(np.float32)[:, None]
    par, b = p // B, p % B
    same_b = (b[:, None] == b[None]).astype(np.float32)
    drop = -same_b * ((par[:, None] == 1) | (par[None] == 0))
    before = (b[:, None] < b[None]).astype(np.float32)
    e_minus = np.tile(np.arange(E, dtype=np.float32)[None] - E, (P, 1))
    own = (XROWS + np.arange(STEPS2)[None] * P + p[:, None]).astype(np.float32)
    parts = dict(ident=ident, band=band, head8=head8, head16=head16.reshape(P, -1), same_head=same_head,
                 same_seq=same_seq, key_diag=key_diag, tok_row=tok_row, is_tok=is_tok, same_b=same_b,
                 drop=drop.astype(np.float32), before=before, e_minus=e_minus, own=own)
    at, cols = {}, 0
    for name, a in parts.items():
        at[name] = (cols, a.shape[1])
        cols += a.shape[1]
    return np.concatenate(list(parts.values()), 1), at


def bc(ap, shape):
    return ap.unsqueeze(len(ap.shape)).broadcast_to(shape)


def build(nc, t, CONST_AT):
    with ExitStack() as outer:
        def sbuf(ctx, name, shape, dt=F32):
            return ctx.enter_context(nc.sbuf_tensor(name, shape, dt))

        def sem(ctx, name):
            return ctx.enter_context(nc.semaphore(name))

        consts = sbuf(outer, "consts", [P, sum(w for _, w in CONST_AT.values())])
        ident_h = sbuf(outer, "ident_h", [P, P], BF16)

        def const(name):
            o, w = CONST_AT[name]
            return consts[:, o:o + w]

        ident = const("ident")
        avw_d = nc.dram_tensor("avw_d", [B * H0, D], F32).ap()
        x1_d = nc.dram_tensor("x1_d", [B, L, D], F32).ap()
        xtab_d = nc.dram_tensor("xtab_d", [XROWS + B * L, D], F32).ap()
        ytab_d = nc.dram_tensor("ytab_d", [XROWS + B * L, D], F32).ap()

        fq = sbuf(outer, "fq", [P, KT, B * L])
        fk = sbuf(outer, "fk", [P, KT, B * L])
        fv = sbuf(outer, "fv", [P, PAIRS, D])
        with ExitStack() as c:
            qgblk = sbuf(outer, "qgblk", [P, KT, H1])
            sims = sbuf(outer, "sims", [P, PAIRS, 2 * H1])
            star_pass(nc, c, sbuf, sem, t, const, ident, ident_h, consts, qgblk, fq, fk, fv, sims, avw_d, xtab_d)
        x1T = sbuf(outer, "x1T", [P, KT, L, B])
        with ExitStack() as l0:
            key_bias = sbuf(l0, "key_bias", [P, PAIRS, L], BF16)
            reg_bias = sbuf(l0, "reg_bias", [P, PAIRS, 2, L], BF16)
            with ExitStack() as c:
                classes(nc, c, sbuf, sem, const, ident, sims, key_bias, reg_bias)
            with ExitStack() as c:
                masked_pass(nc, c, sbuf, sem, t, const, ident, ident_h, fq, fk, fv, key_bias, reg_bias, x1T, x1_d)
        h_rows = fv
        room = fk[:].rearrange("p k n -> p (k n)")
        ew1 = [room[:, u * 4096:u * 4096 + 2048].rearrange("p (k n) -> p k n", k=KT) for u in range(2)]
        ew2 = [room[:, u * 4096 + 2048:u * 4096 + 4096].rearrange("p (k n) -> p k n", k=FT) for u in range(2)]
        with ExitStack() as l1:
            logits = sbuf(l1, "logits", [P, STEPS2, E])
            eb1 = [sbuf(l1, f"eb1_{u}", [P, FT]) for u in range(2)]
            e_loaded = [sem(l1, f"e_loaded{u}") for u in range(2)]
            with ExitStack() as c:
                recurrence(nc, c, sbuf, sem, t, const, ident, x1T, h_rows, logits, ytab_d,
                           ew1, ew2, eb1, e_loaded)
            with ExitStack() as c:
                experts(nc, c, sbuf, sem, t, const, ident, h_rows, logits, x1_d, xtab_d, ytab_d,
                        ew1, ew2, eb1, e_loaded)


def star_pass(nc, c, sbuf, sem, t, const, ident, ident_h, consts, qgblk, fq, fk, fv, sims, avw_d, xtab_d):
    wq = sbuf(c, "wq", [P, KT, H0 * HD0])
    wk = sbuf(c, "wk", [P, KT, H0 * HD0])
    wo = sbuf(c, "wo", [P, HT, D])
    wqkv = sbuf(c, "wqkv", [P, KT, 3 * D])
    bq, bk, bv = (sbuf(c, n, [P, HT]) for n in ("bq", "bk", "bv"))
    bo = sbuf(c, "bo", [P, KT])
    akT = sbuf(c, "akT", [P, HT, B])
    headones = const("head16").rearrange("p (t h) -> p t h", t=KT)
    band_h = sbuf(c, "band_h", [P, SPB // 2, 2 * W0], BF16)
    xrow = sbuf(c, "xrow", [P, D])
    avw = sbuf(c, "avw", [2 * H0, D])
    kblk = sbuf(c, "kblk", [P, HT, 2, 2 * (L + 1)])
    prob = sbuf(c, "prob", [P, H0, W0])
    pkey = sbuf(c, "pkey", [P, H0, L])
    acond = sbuf(c, "acond", [P, 2 * H0])
    mx, sm, aw = (sbuf(c, n, [P, H0]) for n in ("mx", "sm", "aw"))

    with ExitStack() as s:
        cond = sbuf(s, "cond", [B, D])
        condT = sbuf(s, "condT", [P, KT, B])
        avT = sbuf(s, "avT", [P, HT, B])
        wv = fk[:, :, 0:H0 * HD0]
        avw_rows = fv[0:B, 0:H0]
        g, g2, gn = (sbuf(s, n, [P, KT]) for n in ("g", "g2", "gn"))
        zero = sbuf(s, "zero", [P, 4 * D])
        pst = s.enter_context(nc.psum_tensor("pst", [P, 2, 512], F32))
        psa = s.enter_context(nc.psum_tensor("psa", [P, 2, 512], F32))
        psv = s.enter_context(nc.psum_tensor("psv", [B, 4, 512], F32))
        loaded, wv_loaded, zero_set, zeroed, avw_stored = (sem(s, n) for n in (
            "p_loaded", "p_wv_loaded", "p_zero_set", "p_zeroed", "p_avw_stored"))
        condT_ps, condT_done, ak_ps, ak_done, av_ps, av_done, avw_ps, avw_done = (sem(s, n) for n in (
            "p_condT_ps", "p_condT_done", "p_ak_ps", "p_ak_done", "p_av_ps", "p_av_done", "p_avw_ps", "p_avw_done"))
        g2_done, gs_ps, gs_root, gs_inv, gn_done, pad_set = (sem(s, n) for n in (
            "p_g2_done", "p_gs_ps", "p_gs_root", "p_gs_inv", "p_gn_done", "p_pad_set"))
        block = s.enter_context(nc.Block())
        loads = [
            (consts[:], t["consts"]), (cond[:], t["cond_1024"]),
            (bk[:], t["L0_cond_WK_b"].rearrange("(m p) -> p m", p=P)),
            (bv[:], t["L0_cond_WV_b"].rearrange("(m p) -> p m", p=P)),
            (bq[:], t["L0_cond_WQ_b"].rearrange("(m p) -> p m", p=P)),
            (bo[:], t["L0_cond_WO_b"].rearrange("(m p) -> p m", p=P)),
            (g[:], t["L0_ffn_g_info"][0, 0].rearrange("(m p) -> p m", p=P)),
            (wk[:], t["L0_cond_WK_w"].rearrange("(k p) n -> p k n", p=P)),
            (wq[:], t["L0_cond_WQ_w"].rearrange("(k p) n -> p k n", p=P)),
            (wo[:], t["L0_cond_WO_w"].rearrange("(k p) n -> p k n", p=P)),
            (wqkv[:], t["L0_ffn_W_qkv"].rearrange("(k p) n -> p k n", p=P)),
        ]

        @block.sync
        def _(sp):
            for dst, src in loads:
                with nc.allow_non_contiguous_dma(reason="bias columns"):
                    sp.dma_start(dst, src).then_inc(loaded, 16)
            sp.dma_start(wv, t["L0_cond_WV_w"].rearrange("(k p) n -> p k n", p=P)).then_inc(wv_loaded, 16)
            sp.wait_ge(zero_set, 1)
            rows = XROWS // P // 4
            for n in range(rows):
                sp.dma_start(xtab_d[n * 4 * P:(n + 1) * 4 * P].rearrange("(p r) d -> p (r d)", p=P),
                             zero[:]).then_inc(zeroed, 16)
            sp.wait_ge(avw_done, H0 // 2)
            sp.dma_start(avw_d.rearrange("(b h) d -> b h d", h=H0), avw_rows).then_inc(avw_stored, 16)
            sp.wait_ge(zeroed, 16 * rows)
            sp.wait_ge(avw_stored, 16)

        @block.tensor
        def _(pe):
            pe.wait_ge(loaded, 16 * len(loads))
            for k in range(KT):
                m = pe.transpose(pst[:, 0, k * B:(k + 1) * B], cond[:, k * P:(k + 1) * P], ident[0:B, 0:B])
            m.then_inc(condT_ps, 1)
            pe.wait_ge(condT_done, 1)
            for w, out, ready in ((wk, psa[:, 0], ak_ps), (wv, psa[:, 1], av_ps)):
                if w is wv:
                    pe.wait_ge(wv_loaded, 16)
                for n in range(HT):
                    for k in range(KT):
                        m = pe.matmul(out[:, n * B:(n + 1) * B], w[:, k, n * P:(n + 1) * P], condT[:, k],
                                      start=(k == 0), stop=(k == KT - 1))
                m.then_inc(ready, 1)
            pe.wait_ge(g2_done, 1)
            pe.matmul(pst[:, 1, 0:KT], const("same_head"), g2[:], start=True, stop=True).then_inc(gs_ps, 1)
            pe.wait_ge(av_done, 1)
            for n in range(H0 // 2):
                if n >= 2:
                    pe.wait_ge(avw_done, n - 1)
                for a in range(2):
                    m = pe.matmul(psv[:, 2 * (n % 2) + a, 0:D], avT[64 * a:64 * a + 64, n],
                                  wo[64 * a:64 * a + 64, n], start=True, stop=True)
                m.then_inc(avw_ps, 1)

        @block.vector
        def _(dve):
            dve.memset(zero[:], 0.0).then_inc(zero_set, 1)
            dve.memset(kblk[:], 0.0)
            dve.memset(acond[:], 0.0).then_inc(pad_set, 1)
            dve.wait_ge(loaded, 16 * len(loads))
            dve.tensor_copy(ident_h[:], ident)
            for n in range(SPB // 2):
                dve.tensor_copy(band_h[:, n], const("band"))
            dve.tensor_tensor(g2[:], g[:], g[:], ALU.mult).then_inc(g2_done, 1)
            dve.wait_ge(condT_ps, 1)
            dve.tensor_copy(condT[:].rearrange("p k b -> p (k b)"), pst[:, 0, 0:KT * B]).then_inc(condT_done, 1)
            dve.wait_ge(ak_ps, 1)
            dve.tensor_tensor(akT[:], psa[:, 0].rearrange("p (m b) -> p m b", b=B), bc(bk[:], [P, HT, B]),
                              ALU.add).then_inc(ak_done, 1)
            dve.wait_ge(av_ps, 1)
            dve.tensor_tensor(avT[:], psa[:, 1].rearrange("p (m b) -> p m b", b=B), bc(bv[:], [P, HT, B]),
                              ALU.add).then_inc(av_done, 1)
            dve.wait_ge(gs_root, 1)
            dve.reciprocal(g2[:], gn[:]).then_inc(gs_inv, 1)
            dve.wait_ge(gs_inv, 1)
            dve.tensor_tensor(gn[:], g2[:], g[:], ALU.mult).then_inc(gn_done, 1)
            dve.wait_ge(gn_done, 1)
            dve.tensor_tensor(qgblk[:], headones, bc(gn[:], [P, KT, H1]), ALU.mult)
            for n in range(H0 // 2):
                dve.wait_ge(avw_ps, n + 1)
                dve.tensor_copy(avw_rows[:, 2 * n:2 * n + 2], psv[:, 2 * (n % 2):2 * (n % 2) + 2, 0:D]).then_inc(avw_done, 1)

        @block.scalar
        def _(act):
            act.wait_ge(gs_ps, 1)
            act.activation(gn[:], pst[:, 1, 0:KT], ACT.Sqrt).then_inc(gs_root, 1)

    with ExitStack() as s:
        xT = sbuf(s, "xT", [P, KT, P])
        qT = sbuf(s, "qT", [P, HT, P])
        vblk = sbuf(s, "vblk", [P, HT, 2, P])
        probT = sbuf(s, "probT", [P, HT, P])
        acondT = sbuf(s, "acondT", [2 * H0, P])
        attT = sbuf(s, "attT", [P, HT, P])
        yT = sbuf(s, "yT", [P, KT, P])
        qs = sbuf(s, "qs", [P, KT, P])
        qq = sbuf(s, "qq", [P, KT, P])
        score = s.enter_context(nc.psum_tensor("score", [P, 4, 512], F32))
        bank = [s.enter_context(nc.psum_tensor(f"bank{n}", [P, 512], F32)) for n in range(4)]
        names = ("x_loaded avw_loaded xT_ps xT_done q_ps q_done k_ps k_done ak_set s_ps max_done sub_done exp_done "
                 "sum_done inv_done prob_done aw_done acond_done pT_ps pT_done aT_ps aT_done att_ps att_done y_ps y_done "
                 "f_ps fq_done fk_done qq_done fv_ps fv_done v_ps v_done sim_ps sim_done fq_kept")
        S = {n: sem(s, "a_" + n) for n in names.split()}
        block = s.enter_context(nc.Block())
        s4 = score[:].rearrange("p n c -> p (n c)")

        def slots(half):
            return score[:, 2 * half:2 * half + 2, 0:SPB * W0].rearrange("p n (s w) -> p n s w", w=W0)

        def half_of(ap, half):
            return ap[:, 8 * half:8 * half + 8]

        def prob4(half):
            return prob[:, 8 * half:8 * half + 8].rearrange("p (n s) w -> p n s w", s=SPB)

        @block.sync
        def _(sp):
            def load(i, first=False):
                if not first:
                    sp.wait_ge(S["xT_ps"], i)
                sp.dma_start(xrow[:], t["x"][bass.ds(i * 2, 2)].rearrange("b l d -> (b l) d")).then_inc(S["x_loaded"], 16)
                if not first:
                    sp.wait_ge(S["y_ps"], i)
                sp.dma_start(avw[:], avw_d[bass.ds(i * 2 * H0, 2 * H0)]).then_inc(S["avw_loaded"], 16)
            load(0, True)
            with sp.Fori(1, PAIRS) as i:
                load(i)

        @block.tensor
        def _(pe):
            def project(i, first=False):
                pe.wait_ge(S["x_loaded"], i * 16 + 16)
                if not first:
                    pe.wait_ge(S["v_done"], i * 4)
                for k in range(KT):
                    m = pe.transpose(bank[2][:, k * P:(k + 1) * P], xrow[:, k * P:(k + 1) * P], ident)
                m.then_inc(S["xT_ps"], 1)
                if not first:
                    pe.wait_ge(S["sim_done"], i - 1)
                pe.wait_ge(S["xT_done"], i + 1)
                for half in range(2):
                    for n in range(4):
                        for k in range(KT):
                            m = pe.matmul(bank[half][:, n * P:(n + 1) * P], wq[:, k, (4 * half + n) * P:(4 * half + n + 1) * P],
                                          xT[:, k], start=(k == 0), stop=(k == KT - 1))
                    m.then_inc(S["q_ps"], 1)
                for half in range(2):
                    for n in range(4):
                        for k in range(KT):
                            m = pe.matmul(bank[3 - half][:, n * P:(n + 1) * P], wk[:, k, (4 * half + n) * P:(4 * half + n + 1) * P],
                                          xT[:, k], start=(k == 0), stop=(k == KT - 1))
                    m.then_inc(S["k_ps"], 1)

            def attend(i, last=False):
                if last:
                    pe.wait_ge(S["v_done"], i * 4 + 4)
                    pe.wait_ge(S["sim_done"], i)
                else:
                    pe.wait_ge(S["q_done"], i * 2 + 4)
                for half in range(2):
                    pe.wait_ge(S["prob_done"], i * 2 + half + 1)
                    for n in range(4):
                        p = 4 * half + n
                        m = pe.transpose(bank[half][:, n * P:(n + 1) * P], pkey[:, 2 * p:2 * p + 2].rearrange("p a k -> p (a k)"), ident)
                    m.then_inc(S["pT_ps"], 1)
                pe.wait_ge(S["acond_done"], i + 1)
                if not last:
                    pe.wait_ge(S["k_done"], i * 2 + 4)
                pe.transpose(bank[3][0:2 * H0, 0:P], acond[:], ident).then_inc(S["aT_ps"], 1)
                for half in range(2):
                    pe.wait_ge(S["v_done"], i * 4 + 2 * half + 2)
                    pe.wait_ge(S["pT_done"], i * 2 + half + 1)
                    out = bank[2] if half == 0 else bank[0]
                    for n in range(4):
                        p = 4 * half + n
                        for q in range(2):
                            for a in range(2):
                                m = pe.matmul(out[64 * a:64 * a + 64, n * P + q * L:n * P + (q + 1) * L],
                                              vblk[:, p, q, 64 * a:64 * a + 64], probT[:, p, q * L:(q + 1) * L],
                                              start=True, stop=True)
                    m.then_inc(S["att_ps"], 1)
                pe.wait_ge(S["att_done"], i * 2 + 2)
                pe.wait_ge(S["aT_done"], i + 1)
                pe.wait_ge(S["avw_loaded"], i * 16 + 16)
                for n in range(KT):
                    for p in range(HT):
                        pe.matmul(bank[1][:, n * P:(n + 1) * P], wo[:, p, n * P:(n + 1) * P], attT[:, p],
                                  start=(p == 0), stop=False)
                    m = pe.matmul(bank[1][:, n * P:(n + 1) * P], avw[:, n * P:(n + 1) * P], acondT[:],
                                  start=False, stop=True)
                m.then_inc(S["y_ps"], 1)

            def scores(i, first=False):
                if not first:
                    pe.wait_ge(S["sub_done"], i * 2)
                for n in range(4):
                    pe.matmul(score[:, n, 0:SPB * W0], ident_h[:], band_h[:].rearrange("p n w -> p (n w)"),
                              start=True, stop=True)
                pe.wait_ge(S["q_done"], i * 2 + 2)
                pe.wait_ge(S["k_done"], i * 2 + 2)
                pe.wait_ge(S["ak_set"], i + 1)
                for p in range(HT):
                    for q in range(2):
                        o = (p % 2) * 2 * W0
                        out = score[64 * q:64 * q + 64, p // 2, o:o + 2 * W0].rearrange("p (s w) -> p s w", w=W0)[:, :, 0:L + 1]
                        m = pe.matmul(out, qT[:, p, q * L:(q + 1) * L], kblk[:, p, q].rearrange("p (s w) -> p s w", s=2), start=False,
                                      stop=True, skip_group_check=True)
                    if p % 4 == 3:
                        m.then_inc(S["s_ps"], 1)

            def masked_qkv(i):
                pe.wait_ge(S["y_done"], i + 1)
                for n in range(4):
                    for k in range(KT):
                        m = pe.matmul(bank[3][:, n * P:(n + 1) * P], wqkv[:, k, n * P:(n + 1) * P], yT[:, k],
                                      start=(k == 0), stop=(k == KT - 1))
                m.then_inc(S["f_ps"], 1)
                for k in range(KT):
                    m = pe.matmul(bank[2][:, 0:D], yT[:, k], wqkv[:, k, 2 * D:3 * D],
                                  start=(k == 0), stop=(k == KT - 1))
                m.then_inc(S["fv_ps"], 1)

            def values(i, after):
                order = (0, 1, 3, 2)
                for n in range(4):
                    after(n)
                    for j in range(4):
                        p, q = 2 * n + j // 2, j % 2
                        m = pe.transpose(bank[order[n]][:, j * P:(j + 1) * P], kblk[:, p, q, 1:1 + 2 * L], ident)
                    m.then_inc(S["v_ps"], 1)

            def similarity(i, last=False):
                pe.wait_ge(S["fq_done"], i + 1)
                pe.wait_ge(S["qq_done"], i + 1)
                if last:
                    pe.wait_ge(S["att_done"], i * 2 + 2)
                else:
                    pe.wait_ge(S["v_done"], i * 4 + 5)
                for o, src, w in ((0, qs, qgblk), (H1, qq, headones)):
                    for k in range(KT):
                        m = pe.matmul(bank[0][:, o:o + H1], src[:, k], w[:, k], start=(k == 0), stop=(k == KT - 1))
                m.then_inc(S["sim_ps"], 1)

            def first_values(n):
                if n == 0:
                    pe.wait_ge(S["q_done"], 2)
                if n == 2:
                    pe.wait_ge(S["k_done"], 2)

            project(0, True)
            scores(0, True)
            values(0, first_values)
            def step(i):
                project(i + 1)
                attend(i)
                scores(i + 1)
                masked_qkv(i)

                def after(n):
                    if n == 0:
                        pe.wait_ge(S["att_done"], i * 2 + 2)
                    if n == 1:
                        pe.wait_ge(S["y_done"], i + 1)
                    if n == 2:
                        pe.wait_ge(S["fk_done"], i + 1)
                        pe.wait_ge(S["fv_done"], i + 1)
                values(i + 1, after)
                similarity(i)

            step(0)
            with pe.Fori(1, PAIRS - 1) as i:
                step(i)
            attend(PAIRS - 1, True)
            masked_qkv(PAIRS - 1)
            similarity(PAIRS - 1, True)

        @block.vector
        def _(dve):
            def bias_out(i):
                for half in range(2):
                    dve.wait_ge(S["q_ps"], i * 2 + half + 1)
                    dve.tensor_tensor(qT[:, 4 * half:4 * half + 4], bank[half][:].rearrange("p (m n) -> p m n", n=P),
                                      bc(bq[:, 4 * half:4 * half + 4], [P, 4, P]), ALU.add).then_inc(S["q_done"], 1)
                for half in range(2):
                    dve.wait_ge(S["k_ps"], i * 2 + half + 1)
                    for a in range(2):
                        r = slice(64 * a, 64 * a + 64)
                        src = bank[3 - half][r].rearrange("p (m q n) -> p m q n", q=2, n=L)
                        b4 = bc(bc(bk[r, 4 * half:4 * half + 4], [64, 4, 2]), [64, 4, 2, L])
                        m = dve.tensor_tensor(kblk[r, 4 * half:4 * half + 4, :, 1 + a * L:1 + (a + 1) * L], src, b4, ALU.add)
                    m.then_inc(S["k_done"], 1)

            def softmax(i):
                for half in range(2):
                    dve.wait_ge(S["s_ps"], i * 2 + half + 1)
                    dve.tensor_reduce(half_of(mx, half).rearrange("p (n s) -> p n s", s=SPB), slots(half), X,
                                      ALU.max).then_inc(S["max_done"], 1)
                    dve.wait_ge(S["max_done"], i * 2 + half + 1)
                    dve.wait_ge(S["acond_done"], i)
                    dve.tensor_tensor(prob4(half), slots(half),
                                      bc(half_of(mx, half).rearrange("p (n s) -> p n s", s=SPB), [P, 2, SPB, W0]),
                                      ALU.subtract).then_inc(S["sub_done"], 1)
                for half in range(2):
                    dve.wait_ge(S["exp_done"], i * 2 + half + 1)
                    dve.tensor_reduce(half_of(sm, half), prob[:, 8 * half:8 * half + 8], X, ALU.add).then_inc(S["sum_done"], 1)
                    dve.wait_ge(S["sum_done"], i * 2 + half + 1)
                    dve.reciprocal(half_of(sm, half), half_of(sm, half)).then_inc(S["inv_done"], 1)

            def sim_out(i):
                dve.wait_ge(S["sim_ps"], i + 1)
                dve.tensor_copy(sims[:, bass.ds(i, 1)].rearrange("p a b -> p (a b)"),
                                bank[0][:, 0:2 * H1]).then_inc(S["sim_done"], 1)

            bias_out(0)
            softmax(0)
            with dve.Fori(0, PAIRS - 1) as i:
                bias_out(i + 1)
                softmax(i + 1)
                sim_out(i)
            sim_out(PAIRS - 1)

        @block.scalar
        def _(act):
            def xT_out(i):
                act.wait_ge(S["xT_ps"], i + 1)
                act.copy(xT[:].rearrange("p k n -> p (k n)"), bank[2][:, 0:KT * P]).then_inc(S["xT_done"], 1)

            def attend_out(i):
                for half in range(2):
                    act.wait_ge(S["pT_ps"], i * 2 + half + 1)
                    act.copy(probT[:, 4 * half:4 * half + 4].rearrange("p m n -> p (m n)"), bank[half][:]).then_inc(S["pT_done"], 1)
                act.wait_ge(S["aT_ps"], i + 1)
                act.copy(acondT[:], bank[3][0:2 * H0, 0:P]).then_inc(S["aT_done"], 1)
                for half in range(2):
                    act.wait_ge(S["att_ps"], i * 2 + half + 1)
                    act.copy(attT[:, 4 * half:4 * half + 4].rearrange("p m n -> p (m n)"),
                             bank[2 if half == 0 else 0][:]).then_inc(S["att_done"], 1)
                act.wait_ge(S["y_ps"], i + 1)
                for n in range(KT):
                    m = act.activation(yT[:, n], bank[1][:, n * P:(n + 1) * P], ACT.Identity, bias=bo[:, n:n + 1])
                m.then_inc(S["y_done"], 1)

            def exps(i):
                for half in range(2):
                    act.wait_ge(S["sub_done"], i * 2 + half + 1)
                    act.activation(prob[:, 8 * half:8 * half + 8], prob[:, 8 * half:8 * half + 8], ACT.Exp,
                                   scale=HD0 ** -0.5).then_inc(S["exp_done"], 1)

            def masked_out(i):
                act.wait_ge(S["f_ps"], i + 1)
                act.wait_ge(S["fq_kept"], i)
                act.wait_ge(S["sim_ps"], i)
                qp = bank[3][:, 0:KT * P].rearrange("p (k n) -> p k n", n=P)
                act.copy(qs[:], qp).then_inc(S["fq_done"], 1)
                act.activation(qq[:], qp, ACT.Square).then_inc(S["qq_done"], 1)
                act.copy(fk[:, :, bass.ds(i * P, P)], bank[3][:, KT * P:].rearrange("p (k n) -> p k n", n=P)).then_inc(S["fk_done"], 1)
                act.wait_ge(S["fv_ps"], i + 1)
                act.copy(fv[:, bass.ds(i, 1)].rearrange("p a b -> p (a b)"), bank[2][:, 0:D]).then_inc(S["fv_done"], 1)

            def values_out(i):
                order = (0, 1, 3, 2)
                for n in range(4):
                    act.wait_ge(S["v_ps"], i * 4 + n + 1)
                    act.copy(vblk[:, 2 * n:2 * n + 2].rearrange("p m q n -> p (m q n)"), bank[order[n]][:]).then_inc(S["v_done"], 1)

            xT_out(0)
            exps(0)
            values_out(0)
            def step(i):
                xT_out(i + 1)
                attend_out(i)
                masked_out(i)
                exps(i + 1)
                values_out(i + 1)

            step(0)
            with act.Fori(1, PAIRS - 1) as i:
                step(i)
            attend_out(PAIRS - 1)
            masked_out(PAIRS - 1)

        upper_lower = [const("same_seq")[:, 64 * q:64 * q + 1] for q in range(2)]

        @block.gpsimd
        def _(pool):
            def condition_keys(i, first=False):
                if not first:
                    pool.wait_ge(S["v_ps"], i * 4)
                for a in range(2):
                    m = pool.tensor_tensor(kblk[:, :, :, a * (2 * L + 1)], akT[:, :, bass.ds(i * 2, 2)],
                                           bc(upper_lower[a].broadcast_to([P, HT]), [P, HT, 2]), ALU.mult)
                m.then_inc(S["ak_set"], 1)

            def normalise(i):
                for half in range(2):
                    pool.wait_ge(S["inv_done"], i * 2 + half + 1)
                    pool.wait_ge(S["pT_ps"], i * 2)
                    for a in range(2):
                        heads = slice(8 * half + a, 8 * half + 8, 2)
                        m = pool.tensor_tensor(pkey[:, heads], prob[:, heads, 1 - a:1 - a + L], bc(sm[:, heads], [P, 4, L]), ALU.mult)
                    m.then_inc(S["prob_done"], 1)
                pool.wait_ge(S["aT_ps"], i)
                for a in range(2):
                    m = pool.tensor_tensor(aw[:, a::2], prob[:, a::2, a * L], sm[:, a::2], ALU.mult)
                m.then_inc(S["aw_done"], 1)
                pool.wait_ge(S["aw_done"], i + 1)
                for q in range(2):
                    m = pool.tensor_tensor(acond[:, q * H0:(q + 1) * H0], aw[:], upper_lower[q].broadcast_to([P, H0]), ALU.mult)
                m.then_inc(S["acond_done"], 1)

            def keep_q(i):
                pool.wait_ge(S["fq_done"], i + 1)
                pool.tensor_copy(fq[:, :, bass.ds(i * P, P)], qs[:]).then_inc(S["fq_kept"], 1)

            condition_keys(0, True)
            normalise(0)
            with pool.Fori(0, PAIRS - 1) as i:
                condition_keys(i + 1)
                normalise(i + 1)
                keep_q(i)
            keep_q(PAIRS - 1)




def classes(nc, c, sbuf, sem, const, ident, sims, key_bias, reg_bias):
    n16 = [P, PAIRS, H1]
    root, inv = sbuf(c, "root", n16), sbuf(c, "inv", n16)
    sim, low, high, scaled, cls = (sbuf(c, n, [P, PAIRS]) for n in ("sim", "low", "high", "scaled", "cls"))
    ext, extT, both, span = sbuf(c, "ext", [P, 2]), sbuf(c, "extT", [2, P]), sbuf(c, "both", [P, 2]), sbuf(c, "span", [P, 2])
    ends, endrow = sbuf(c, "ends", [2, 1]), sbuf(c, "endrow", [2, 2])
    ones2 = sbuf(c, "ones2", [2, P])
    far = sbuf(c, "far", [P, 1])
    diag = sbuf(c, "diag", [P, PAIRS, L], BF16)
    seq_h = sbuf(c, "seq_h", [P, P], BF16)
    allow, slope, offset, tmp = (sbuf(c, n, [P, PAIRS, L]) for n in ("allow", "slope", "offset", "tmp"))
    first_h = sbuf(c, "first_h", [P, 2, P], BF16)
    ps = c.enter_context(nc.psum_tensor("cls_ps", [P, 4, 512], F32))
    ps_reg = c.enter_context(nc.psum_tensor("cls_reg", [P, 2, 512], F32))
    ps_s = c.enter_context(nc.psum_tensor("cls_s", [P, 512], F32))
    rooted, ext_done, extT_ps, end_set, end_ps, diag_done, key_ps, reg_ps, reg_done = (sem(c, "c_" + n) for n in (
        "rooted", "ext_done", "extT_ps", "end_set", "end_ps", "diag_done", "key_ps", "reg_ps", "reg_done"))
    step = sem(c, "c_step")
    block = c.enter_context(nc.Block())

    @block.scalar
    def _(act):
        act.activation(root[:], sims[:, :, H1:2 * H1], ACT.Sqrt).then_inc(rooted, 1)

    @block.tensor
    def _(pe):
        pe.wait_ge(ext_done, 1)
        pe.transpose(ps_s[0:2, 0:P], ext[:], ident).then_inc(extT_ps, 1)
        pe.wait_ge(end_set, 1)
        pe.matmul(ps_s[:, P:P + 2], ones2[:], endrow[:], start=True, stop=True).then_inc(end_ps, 1)
        pe.wait_ge(diag_done, 1)
        for n in range(4):
            m = pe.matmul(ps[:, n], seq_h[:], diag[:, 8 * n:8 * n + 8].rearrange("p a b -> p (a b)"), start=True, stop=True)
        m.then_inc(key_ps, 1)
        for n in range(8):
            if n >= 1:
                pe.wait_ge(reg_done, n)
            for q in range(2):
                m = pe.matmul(ps_reg[:, q, 0:4 * L], first_h[:, q],
                              diag[:, 4 * n:4 * n + 4].rearrange("p a b -> p (a b)"), start=True, stop=True)
            m.then_inc(reg_ps, 1)

    @block.vector
    def _(dve):
        done = 0

        def then(ins):
            nonlocal done
            done += 1
            ins.then_inc(step, 1)
            dve.wait_ge(step, done)

        dve.memset(endrow[:], 0.0)
        dve.memset(ones2[:], 1.0)
        dve.memset(allow[:], 0.0)
        dve.tensor_copy(seq_h[:], const("same_seq"))
        for q in range(2):
            then(dve.tensor_scalar(first_h[:, q], const("same_seq")[:, 64 * q:64 * q + 1].broadcast_to([P, P]), 1.0, None, ALU.mult))
        then(dve.tensor_scalar(far[:], const("is_tok"), -NEG, NEG, ALU.mult, ALU.add))
        dve.wait_ge(rooted, 1)
        then(dve.reciprocal(inv[:], root[:]))
        then(dve.tensor_tensor(root[:], sims[:, :, 0:H1], inv[:], ALU.mult))
        then(dve.tensor_reduce(low[:], root[:], X, ALU.add))
        then(dve.tensor_scalar(sim[:], low[:], 1.0 / H1, None, ALU.mult))
        then(dve.tensor_scalar(high[:], sim[:], far[:], None, ALU.add))
        then(dve.tensor_scalar(low[:], sim[:], -1.0, far[:], ALU.mult, ALU.add))
        dve.tensor_reduce(ext[:, 0:1], low[:], X, ALU.max)
        dve.tensor_reduce(ext[:, 1:2], high[:], X, ALU.max).then_inc(ext_done, 1)
        dve.wait_ge(extT_ps, 1)
        then(dve.tensor_reduce(ends[:], ps_s[0:2, 0:P], X, ALU.max))
        dve.tensor_tensor(endrow[:], ident[0:2, 0:2], ends[:].broadcast_to([2, 2]), ALU.mult).then_inc(end_set, 1)
        dve.wait_ge(end_ps, 1)
        then(dve.tensor_copy(both[:], ps_s[:, P:P + 2]))
        then(dve.tensor_tensor(span[:, 0:1], both[:, 0:1], both[:, 1:2], ALU.add))
        then(dve.reciprocal(span[:, 1:2], span[:, 0:1]))
        then(dve.tensor_scalar(scaled[:], sim[:], both[:, 0:1], span[:, 1:2], ALU.add, ALU.mult))
        then(dve.tensor_scalar(low[:], scaled[:], 0.9, const("is_tok"), ALU.is_gt, ALU.mult))
        dve.tensor_tensor(diag[:], bc(low[:], [P, PAIRS, L]),
                          const("key_diag").unsqueeze(1).broadcast_to([P, PAIRS, L]), ALU.mult).then_inc(diag_done, 1)
        then(dve.tensor_scalar(far[:], const("is_tok"), -1.0, 1.0, ALU.mult, ALU.add))
        then(dve.tensor_scalar(cls[:], low[:], far[:], None, ALU.add))
        dve.tensor_scalar(high[:], cls[:], -2.0, 1.0, ALU.mult, ALU.add)
        then(dve.tensor_tensor(offset[:], bc(cls[:], [P, PAIRS, L]),
                               const("tok_row").unsqueeze(1).broadcast_to([P, PAIRS, L]), ALU.mult))
        dve.wait_ge(key_ps, 1)
        then(dve.tensor_tensor(slope[:], ps[:].rearrange("p n (a b) -> p (n a) b", b=L), bc(high[:], [P, PAIRS, L]), ALU.mult))
        then(dve.tensor_tensor(tmp[:], slope[:], offset[:], ALU.add))
        dve.tensor_scalar(key_bias[:], tmp[:], NEG, None, ALU.mult)
        for n in range(8):
            dve.wait_ge(reg_ps, n + 1)
            dve.tensor_scalar(reg_bias[:, 4 * n:4 * n + 4].rearrange("p a q b -> p q a b"),
                              ps_reg[:, :, 0:4 * L].rearrange("p q (a b) -> p q a b", b=L), NEG, None,
                              ALU.mult).then_inc(reg_done, 1)


def masked_pass(nc, c, sbuf, sem, t, const, ident, ident_h, fq, fk, fv, key_bias, reg_bias, x1T, x1_d):
    wp = sbuf(c, "wp", [P, KT, D])
    bp = sbuf(c, "bp", [P, D])
    xrow = sbuf(c, "mxrow", [P, D])
    xb = sbuf(c, "xb", [P, D])
    x1 = sbuf(c, "x1", [P, D])
    q = sbuf(c, "q_pair", [P, KT, P])
    v = sbuf(c, "v_pair", [P, D])
    kb = sbuf(c, "k_pair", [P, KT, P])
    mask = sbuf(c, "mask_pair", [P, L + 2 * L], BF16)
    rq = sbuf(c, "rq", [P, KT, 2, L])
    kblk = sbuf(c, "mkblk", [P, KT, 2, 8, L])
    vblk = sbuf(c, "mvblk", [P, 2, 8, 2 * HD1])
    prob = sbuf(c, "mprob", [P, NSLOT, L])
    probT = sbuf(c, "mprobT", [P, NSLOT // 2, P])
    oT = sbuf(c, "oT", [P, KT, P])
    mx, sm = sbuf(c, "mmx", [P, NSLOT]), sbuf(c, "msm", [P, NSLOT])
    regh = sbuf(c, "regh", [P, 2 * KT, 8, REG])
    reg = sbuf(c, "reg", [P, KT, 2, REG])
    score = c.enter_context(nc.psum_tensor("mscore", [P, 3, 512], F32))
    pt = [c.enter_context(nc.psum_tensor(f"mpt{n}", [P, 512], F32)) for n in range(2)]
    pr = c.enter_context(nc.psum_tensor("mpr", [P, 512], F32))
    po = c.enter_context(nc.psum_tensor("mpo", [P, 512], F32))
    px = c.enter_context(nc.psum_tensor("mpx", [P, 512], F32))
    names = ("w_loaded x_loaded stored pads q_set k_set v_set mask_set rq_set kblk_set vblk_set s_ps max_done sub_done exp_done "
             "sum_done inv_done prob_done pT_ps pT_done o_ps o_done r_ps rmul_done rsum_done radd_done reg_done "
             "xb_done x_ps x1_done x1T_ps x1T_done")
    S = {n: sem(c, "m_" + n) for n in names.split()}
    block = c.enter_context(nc.Block())
    head8 = const("head8")
    sflat = score[:].rearrange("p n c -> p (n c)")[:, 0:NSLOT * L].rearrange("p (s k) -> p s k", k=L)

    @block.sync
    def _(sp):
        sp.dma_start(wp[:], t["L0_ffn_W_proj"].rearrange("(k p) n -> p k n", p=P)).then_inc(S["w_loaded"], 16)
        sp.dma_start(bp[:], t["L0_ffn_b_proj"].partition_broadcast(P)).then_inc(S["w_loaded"], 16)
        def step(i):
            sp.wait_ge(S["xb_done"], i)
            sp.dma_start(xrow[:], t["x"][bass.ds(i * 2, 2)].rearrange("b l d -> (b l) d")).then_inc(S["x_loaded"], 16)
            sp.wait_ge(S["x1_done"], i + 1)
            sp.dma_start(x1_d[bass.ds(i * 2, 2)].rearrange("b l d -> (b l) d"), x1[:]).then_inc(S["stored"], 16)

        step(0)
        with sp.Fori(1, PAIRS) as i:
            step(i)
        sp.wait_ge(S["stored"], 16 * PAIRS)

    @block.gpsimd
    def _(pool):
        def stage(i):
            pool.wait_ge(S["s_ps"], i)
            pool.tensor_copy(q[:], fq[:, :, bass.ds(i * P, P)]).then_inc(S["q_set"], 1)
            pool.tensor_copy(kb[:], fk[:, :, bass.ds(i * P, P)]).then_inc(S["k_set"], 1)
            pool.tensor_copy(mask[:, 0:L], key_bias[:, bass.ds(i, 1)].rearrange("p a b -> p (a b)"))
            pool.tensor_copy(mask[:, L:], reg_bias[:, bass.ds(i, 1)].rearrange("p a q b -> p (a q b)")).then_inc(S["mask_set"], 1)
            pool.wait_ge(S["q_set"], i + 1)
            for k in range(KT):
                for s in range(2):
                    m = pool.tensor_tensor(rq[:, k, s, 0:8 * REG].rearrange("p (h r) -> p h r", r=REG), bc(head8, [P, 8, REG]),
                                           q[:, k, s * L:s * L + REG].unsqueeze(1).broadcast_to([P, 8, REG]), ALU.mult)
            m.then_inc(S["rq_set"], 1)
            pool.wait_ge(S["k_set"], i + 1)
            for s in range(2):
                m = pool.tensor_tensor(kblk[:, 1, s], bc(head8, [P, 8, L]),
                                       kb[:, 1, s * L:(s + 1) * L].unsqueeze(1).broadcast_to([P, 8, L]), ALU.mult)
            m.then_inc(S["kblk_set"], 1)

        def stage_v(i):
            pool.wait_ge(S["r_ps"], i)
            pool.tensor_copy(v[:], fv[:, bass.ds(i, 1)].rearrange("p a b -> p (a b)")).then_inc(S["v_set"], 1)

        def normalise(i):
            pool.wait_ge(S["inv_done"], i + 1)
            pool.tensor_tensor(prob[:], prob[:], bc(sm[:], [P, NSLOT, L]), ALU.mult).then_inc(S["prob_done"], 1)

        def residual(i):
            pool.wait_ge(S["x_loaded"], i * 16 + 16)
            pool.wait_ge(S["x1_done"], i)
            pool.tensor_tensor(xb[:], xrow[:], bp[:], ALU.add).then_inc(S["xb_done"], 1)

        pool.memset(rq[:], 0.0).then_inc(S["pads"], 1)
        pool.memset(vblk[:], 0.0).then_inc(S["pads"], 1)
        pool.wait_ge(S["pads"], 2)
        pool.wait_ge(S["w_loaded"], 32)
        stage(0)
        stage_v(0)
        def step(i):
            normalise(i)
            stage(i + 1)
            residual(i)
            stage_v(i + 1)

        step(0)
        with pool.Fori(1, PAIRS - 1) as i:
            step(i)
        normalise(PAIRS - 1)
        residual(PAIRS - 1)

    @block.tensor
    def _(pe):
        def scores(i):
            pe.wait_ge(S["mask_set"], i + 1)
            pe.wait_ge(S["sub_done"], i)
            for n in range(2):
                pe.matmul(score[:, n], ident_h[:], mask[:, 0:L].unsqueeze(1).broadcast_to([P, 8, L]), start=True, stop=True)
            pe.matmul(score[:, 2, 0:2 * L], ident_h[:], mask[:, L:], start=True, stop=True)
            pe.wait_ge(S["rq_set"], i + 1)
            for k in range(KT):
                for s in range(2):
                    pe.matmul(score[64 * k:64 * k + 64, 2, s * L:(s + 1) * L], rq[:, k, s], kb[:, k, s * L:(s + 1) * L],
                              start=False, stop=True, skip_group_check=True)
            pe.wait_ge(S["kblk_set"], i * 2 + 2)
            for k in range(KT):
                for s in range(2):
                    m = pe.matmul(score[64 * s:64 * s + 64, k], q[:, k, s * L:(s + 1) * L],
                                  kblk[:, k, s].rearrange("p h n -> p (h n)"), start=False, stop=True, skip_group_check=True)
            m.then_inc(S["s_ps"], 1)

        def transposed(i):
            pe.wait_ge(S["prob_done"], i + 1)
            pe.wait_ge(S["x1T_done"], i)
            pe.wait_ge(S["rmul_done"], i)
            for n in range(NSLOT // 2):
                out = (pt[0], pt[1], px)[n // 4]
                if n == 8:
                    pe.wait_ge(S["x1_done"], i)
                m = pe.transpose(out[:, (n % 4) * P:(n % 4 + 1) * P], prob[:, 2 * n:2 * n + 2].rearrange("p a k -> p (a k)"), ident)
                if n in (3, 7, 8):
                    m.then_inc(S["pT_ps"], 1)

        def weigh(i):
            pe.wait_ge(S["pT_done"], i * 3 + 3)
            pe.wait_ge(S["vblk_set"], i + 1)
            pe.wait_ge(S["o_done"], i)
            for s in range(2):
                for p in range(8):
                    r = 32 * (p % 4)
                    m = pe.matmul(po[r:r + 32, (p // 4) * P + s * L:(p // 4) * P + (s + 1) * L], vblk[:, s, p],
                                  probT[:, p, s * L:(s + 1) * L], start=True, stop=True, tile_position=(0, r))
            m.then_inc(S["o_ps"], 1)
            for k in range(KT):
                for s in range(2):
                    out = (pr[:, 0:KT * L], pt[0][:, 0:KT * L])[s]
                    m = pe.matmul(out[:, k * L:(k + 1) * L], v[64 * s:64 * s + 64, k * P:(k + 1) * P],
                                  probT[64 * s:64 * s + 64, 8, k * L:(k + 1) * L], start=True, stop=True)
            m.then_inc(S["r_ps"], 1)

        def projected(i):
            pe.wait_ge(S["reg_done"], i + 1)
            for k in range(KT):
                m = pe.matmul(px[:, 0:D], oT[:, k], wp[:, k], start=(k == 0), stop=(k == KT - 1))
            m.then_inc(S["x_ps"], 1)

        def turned(i):
            pe.wait_ge(S["x1_done"], i + 1)
            for k in range(KT):
                m = pe.transpose(pt[1][:, k * P:(k + 1) * P], x1[:, k * P:(k + 1) * P], ident)
            m.then_inc(S["x1T_ps"], 1)

        pe.wait_ge(S["w_loaded"], 32)
        scores(0)
        def step(i):
            transposed(i)
            weigh(i)
            scores(i + 1)
            projected(i)
            turned(i)

        step(0)
        with pe.Fori(1, PAIRS - 1) as i:
            step(i)
        transposed(PAIRS - 1)
        weigh(PAIRS - 1)
        projected(PAIRS - 1)
        turned(PAIRS - 1)

    @block.vector
    def _(dve):
        def blocks(i):
            dve.wait_ge(S["k_set"], i + 1)
            for s in range(2):
                m = dve.tensor_tensor(kblk[:, 0, s], bc(head8, [P, 8, L]),
                                      kb[:, 0, s * L:(s + 1) * L].unsqueeze(1).broadcast_to([P, 8, L]), ALU.mult)
            m.then_inc(S["kblk_set"], 1)

        def softmax_top(i):
            dve.wait_ge(S["s_ps"], i + 1)
            dve.tensor_reduce(mx[:], sflat, X, ALU.max).then_inc(S["max_done"], 1)
            dve.wait_ge(S["max_done"], i + 1)
            dve.tensor_tensor(prob[:], sflat, bc(mx[:], [P, NSLOT, L]), ALU.subtract).then_inc(S["sub_done"], 1)

        def softmax_sum(i):
            dve.wait_ge(S["exp_done"], i + 1)
            dve.tensor_reduce(sm[:], prob[:], X, ALU.add).then_inc(S["sum_done"], 1)
            dve.wait_ge(S["sum_done"], i + 1)
            dve.reciprocal(sm[:], sm[:]).then_inc(S["inv_done"], 1)

        def registers(i):
            dve.wait_ge(S["r_ps"], i + 1)
            for s, src in enumerate((pr[:, 0:KT * L], pt[0][:, 0:KT * L])):
                for k in range(KT):
                    m = dve.tensor_tensor(regh[:, 2 * k + s], src[:, k * L:k * L + 8 * REG].rearrange("p (h r) -> p h r", r=REG),
                                          bc(head8, [P, 8, REG]), ALU.mult)
            m.then_inc(S["rmul_done"], 1)
            dve.wait_ge(S["rmul_done"], i + 1)
            dve.tensor_reduce(reg[:].rearrange("p k s r -> p (k s) r"), regh[:].rearrange("p n h r -> p n r h"), X,
                              ALU.add).then_inc(S["rsum_done"], 1)
            dve.wait_ge(S["rsum_done"], i + 1)
            dve.wait_ge(S["o_done"], i + 1)
            o = oT[:].rearrange("p k (s n) -> p k s n", s=2)[:, :, :, 0:REG]
            dve.tensor_tensor(reg[:], reg[:], o, ALU.add).then_inc(S["radd_done"], 1)
            dve.wait_ge(S["radd_done"], i + 1)
            dve.tensor_scalar(o, reg[:], 0.5, None, ALU.mult).then_inc(S["reg_done"], 1)

        def residual(i):
            dve.wait_ge(S["x_ps"], i + 1)
            dve.wait_ge(S["xb_done"], i + 1)
            dve.wait_ge(S["x1T_ps"], i)
            dve.wait_ge(S["stored"], i * 16)
            dve.tensor_tensor(x1[:], px[:, 0:D], xb[:], ALU.add).then_inc(S["x1_done"], 1)

        blocks(0)
        softmax_top(0)
        softmax_sum(0)
        def step(i):
            blocks(i + 1)
            registers(i)
            softmax_top(i + 1)
            residual(i)
            softmax_sum(i + 1)

        step(0)
        with dve.Fori(1, PAIRS - 1) as i:
            step(i)
        registers(PAIRS - 1)
        residual(PAIRS - 1)

    @block.scalar
    def _(act):
        def exps(i):
            act.wait_ge(S["sub_done"], i + 1)
            act.activation(prob[:], prob[:], ACT.Exp, scale=HD1 ** -0.5).then_inc(S["exp_done"], 1)

        def values(i):
            act.wait_ge(S["v_set"], i + 1)
            for s in range(2):
                src = v[64 * s:64 * s + 64].rearrange("p (n a d) -> p n a d", a=2, d=HD1)
                for a in range(2):
                    m = act.copy(vblk[64 * a:64 * a + 64, s, :, a * HD1:(a + 1) * HD1], src[:, :, a])
            m.then_inc(S["vblk_set"], 1)

        def weights(i):
            for n in range(3):
                act.wait_ge(S["pT_ps"], i * 3 + n + 1)
                w = 4 if n < 2 else 1
                act.copy(probT[:, 4 * n:4 * n + w].rearrange("p m n -> p (m n)"),
                         (pt[0], pt[1], px)[n][:, 0:w * P]).then_inc(S["pT_done"], 1)

        def out(i):
            act.wait_ge(S["o_ps"], i + 1)
            act.wait_ge(S["x_ps"], i)
            act.copy(oT[:].rearrange("p k n -> p (k n)"), po[:, 0:KT * P]).then_inc(S["o_done"], 1)

        def turned(i):
            act.wait_ge(S["x1T_ps"], i + 1)
            for k in range(KT):
                m = act.copy(x1T[:, k, :, bass.ds(i * 2, 2)].rearrange("p t s -> p s t"),
                             pt[1][:, k * P:(k + 1) * P].rearrange("p (s t) -> p s t", s=2))
            m.then_inc(S["x1T_done"], 1)

        act.wait_ge(S["pads"], 2)
        exps(0)
        def step(i):
            values(i)
            weights(i)
            out(i)
            exps(i + 1)
            turned(i)

        step(0)
        with act.Fori(1, PAIRS - 1) as i:
            step(i)
        values(PAIRS - 1)
        weights(PAIRS - 1)
        out(PAIRS - 1)
        turned(PAIRS - 1)


def recurrence(nc, c, sbuf, sem, t, const, ident, x1T, h_rows, logits, ytab_d, ew1, ew2, eb1, e_loaded):
    wx, wh = sbuf(c, "wx", [P, KT, D]), sbuf(c, "wh", [P, KT, D])
    b, ob1 = sbuf(c, "rb", [P, KT]), sbuf(c, "ob1", [P, FT])
    ow1, ow2 = sbuf(c, "ow1", [P, KT, HID]), sbuf(c, "ow2", [P, FT, D])
    rw = sbuf(c, "rw", [P, KT, E])
    rbias, ob2 = sbuf(c, "rbias", [P, E]), sbuf(c, "ob2", [P, D])
    cond = sbuf(c, "rcond", [B, D])
    h = [sbuf(c, f"h{u}", [P, KT, 2 * B]) for u in range(2)]
    hid = sbuf(c, "ohid", [P, FT, P])
    y = sbuf(c, "oy", [P, D])
    ph = [[c.enter_context(nc.psum_tensor(f"ph{u}{m}", [P, 512], F32)) for m in range(KT)] for u in range(2)]
    pm = [c.enter_context(nc.psum_tensor(f"pm{n}", [P, 512], F32)) for n in range(2)]
    py = c.enter_context(nc.psum_tensor("py", [P, 512], F32))
    pr = c.enter_context(nc.psum_tensor("prow", [P, 512], F32))
    names = ("loaded condT_ps h0_done h_ps h_done hid_ps hid_done y_ps y_done stored row_ps row_done logit_ps logit_done")
    S = {n: sem(c, "r_" + n) for n in names.split()}
    block = c.enter_context(nc.Block())
    ytok = ytab_d[XROWS:].rearrange("(j p) d -> j p d", p=P)

    @block.sync
    def _(sp):
        loads = [
            (cond[:], t["cond_1024"]), (wx[:], t["L1_cond_Wx"].rearrange("(k p) n -> p k n", p=P)),
            (wh[:], t["L1_cond_Wh"].rearrange("(k p) n -> p k n", p=P)),
            (b[:], t["L1_cond_b"].rearrange("(m p) -> p m", p=P)),
            (ob1[:], t["L1_ffn_ob1"].rearrange("(m p) -> p m", p=P)),
            (rw[:], t["L1_ffn_router_w"].rearrange("(k p) n -> p k n", p=P)),
            (rbias[:], t["L1_ffn_router_b"].partition_broadcast(P)), (ob2[:], t["L1_ffn_ob2"].partition_broadcast(P)),
            (ow1[:], t["L1_ffn_ow1"].rearrange("(k p) n -> p k n", p=P)),
            (ow2[:], t["L1_ffn_ow2"].rearrange("(k p) n -> p k n", p=P)),
        ]
        for dst, src in loads:
            with nc.allow_non_contiguous_dma(reason="bias columns"):
                sp.dma_start(dst, src).then_inc(S["loaded"], 16)
        for e in range(2):
            load_expert(nc, sp, t, e, ew1[e], ew2[e], eb1[e], e_loaded[e])
        with sp.Fori(0, STEPS2) as j:
            sp.wait_ge(S["y_done"], j + 1)
            sp.dma_start(ytok[bass.ds(j, 1)].rearrange("a p d -> p (a d)"), y[:]).then_inc(S["stored"], 16)
        sp.wait_ge(S["stored"], 16 * STEPS2)

    @block.tensor
    def _(pe):
        def inputs(j, u):
            for m in range(KT):
                for k in range(KT):
                    pe.matmul(ph[u][m][:, 0:P], wx[:, k, m * P:(m + 1) * P],
                              x1T[:, k, bass.ds(j * 2, 2)].rearrange("p t b -> p (t b)"),
                              start=(k == 0), stop=(k == KT - 1), skip_group_check=True)

        def step(j, u, par, first=False):
            src, o = (h[1 - u], B) if par == 0 else (h[u], 0)
            if first:
                pe.wait_ge(S["h0_done"], 1)
            else:
                pe.wait_ge(S["h_done"], j * 4 + 2 * par)
            for k in range(KT):
                for m in range(KT):
                    ins = pe.matmul(ph[u][m][:, par * B:(par + 1) * B], wh[:, k, m * P:(m + 1) * P], src[:, k, o:o + B],
                                    start=False, stop=True, skip_group_check=True)
                    if k == KT - 1:
                        ins.then_inc(S["h_ps"], 1)

        def mlp_up(j, u):
            pe.wait_ge(S["h_done"], j * 4 + 4)
            pe.wait_ge(S["hid_done"], j * 8)
            for half in range(2):
                for n in range(4):
                    for k in range(KT):
                        f = 4 * half + n
                        m = pe.matmul(pm[half][:, n * P:(n + 1) * P], ow1[:, k, f * P:(f + 1) * P], h[u][:, k],
                                      start=(k == 0), stop=(k == KT - 1))
                m.then_inc(S["hid_ps"], 1)

        def rows_and_logits(j, u):
            pe.wait_ge(S["row_done"], j)
            for k in range(KT):
                m = pe.transpose(pr[:, k * P:(k + 1) * P], h[u][:, k], ident)
            m.then_inc(S["row_ps"], 1)
            pe.wait_ge(S["logit_done"], j)
            pe.wait_ge(S["y_done"], j)
            for k in range(KT):
                m = pe.matmul(py[:, 0:E], h[u][:, k], rw[:, k], start=(k == 0), stop=(k == KT - 1))
            m.then_inc(S["logit_ps"], 1)

        def mlp_down(j):
            pe.wait_ge(S["hid_done"], j * 8 + 8)
            pe.wait_ge(S["logit_done"], j + 1)
            for f in range(FT):
                m = pe.matmul(py[:, 0:D], hid[:, f], ow2[:, f], start=(f == 0), stop=(f == FT - 1))
            m.then_inc(S["y_ps"], 1)

        pe.wait_ge(S["loaded"], 160)
        for k in range(KT):
            m = pe.transpose(py[:, k * B:(k + 1) * B], cond[:, k * P:(k + 1) * P], ident[0:B, 0:B])
        m.then_inc(S["condT_ps"], 1)
        inputs(0, 0)
        step(0, 0, 0, True)
        step(0, 0, 1)

        def pair(j, u):
            inputs(j, u)
            step(j, u, 0)
            mlp_up(j - 1, 1 - u)
            step(j, u, 1)
            rows_and_logits(j - 1, 1 - u)
            mlp_down(j - 1)
        pair(1, 1)
        with pe.Fori(1, STEPS2 // 2) as n:
            for u in range(2):
                pair(n * 2 + u, u)
        mlp_up(STEPS2 - 1, 1)
        rows_and_logits(STEPS2 - 1, 1)
        mlp_down(STEPS2 - 1)

    @block.scalar
    def _(act):
        act.wait_ge(S["condT_ps"], 1)
        act.copy(h[1][:, :, B:], py[:, 0:KT * B].rearrange("p (k b) -> p k b", b=B)).then_inc(S["h0_done"], 1)
        with act.Fori(0, STEPS2 // 2) as n:
            for u in range(2):
                for par in range(2):
                    for m in range(KT):
                        act.wait_ge(S["h_ps"], n * 8 + (4 * u + 2 * par + m + 1))
                        act.activation(h[u][:, m, par * B:(par + 1) * B], ph[u][m][:, par * B:(par + 1) * B], ACT.Tanh,
                                       bias=b[:, m:m + 1]).then_inc(S["h_done"], 1)

    @block.vector
    def _(dve):
        dve.wait_ge(S["loaded"], 160)
        def two_steps(j):
            for half in range(2):
                dve.wait_ge(S["hid_ps"], j * 2 + half + 1)
                for n in range(4):
                    f = 4 * half + n
                    dve.tensor_scalar(hid[:, f], pm[half][:, n * P:(n + 1) * P], ob1[:, f:f + 1], 0.0,
                                      ALU.add, ALU.max).then_inc(S["hid_done"], 1)
            dve.wait_ge(S["row_ps"], j + 1)
            dve.tensor_copy(h_rows[:, bass.ds(j, 1)].rearrange("p a d -> p (a d)"), pr[:, 0:D]).then_inc(S["row_done"], 1)
            dve.wait_ge(S["logit_ps"], j + 1)
            dve.tensor_tensor(logits[:, bass.ds(j, 1)].rearrange("p a e -> p (a e)"), py[:, 0:E], rbias[:],
                              ALU.add).then_inc(S["logit_done"], 1)
            dve.wait_ge(S["y_ps"], j + 1)
            dve.wait_ge(S["stored"], j * 16)
            dve.tensor_tensor(y[:], py[:, 0:D], ob2[:], ALU.add).then_inc(S["y_done"], 1)

        two_steps(0)
        with dve.Fori(1, STEPS2) as j:
            two_steps(j)


def load_expert(nc, eng, t, e, w1, w2, b1, loaded):
    eng.dma_start(w1, t["L1_ffn_w1"][bass.ds(e, 1)].rearrange("a (k p) n -> p (a k) n", p=P)).then_inc(loaded, 16)
    eng.dma_start(w2, t["L1_ffn_w2"][bass.ds(e, 1)].rearrange("a (k p) n -> p (a k) n", p=P)).then_inc(loaded, 16)
    with nc.allow_non_contiguous_dma(reason="bias columns"):
        eng.dma_start(b1[:], t["L1_ffn_b1"][bass.ds(e, 1)].rearrange("a (m p) -> p (a m)", p=P)).then_inc(loaded, 16)


def experts(nc, c, sbuf, sem, t, const, ident, h_rows, logits, x1_d, xtab_d, ytab_d, ew1, ew2, eb1, e_loaded):
    big = [P, STEPS2, E]
    eq, cand, hot, count, rank = (sbuf(c, n, big) for n in ("eq", "cand", "hot", "count", "rank"))
    top, eid, pos, ok, slot, gap = (sbuf(c, n, [P, STEPS2]) for n in ("top", "eid", "pos", "ok", "slot", "gap"))
    ones = sbuf(c, "ones", [P, STEPS2])
    idx = sbuf(c, "idx", [P, STEPS2], U32)
    b2 = sbuf(c, "b2", [P, E, D])
    xe = [sbuf(c, f"xe{u}", [P, 3, D]) for u in range(2)]
    xeT = sbuf(c, "xeT", [P, KT, CAP])
    hT = sbuf(c, "ehT", [P, FT, CAP])
    ye = [sbuf(c, f"ye{u}", [P, 3, D]) for u in range(2)]
    got = [sbuf(c, f"got{u}", [P, 4, D]) for u in range(2)]
    res = [sbuf(c, f"res{u}", [P, 4, D]) for u in range(2)]
    pxT = c.enter_context(nc.psum_tensor("pxT", [P, KT, 512], F32))
    phid = [c.enter_context(nc.psum_tensor(f"phid{n}", [P, 512], F32)) for n in range(4)]
    pyo = [c.enter_context(nc.psum_tensor(f"pyo{n}", [P, 512], F32)) for n in range(2)]
    names = "b2_loaded hot_done rank_ps idx_done scattered xT_ps xT_done hid_ps hid_act hid_dve y_ps y_done"
    S = {n: sem(c, "e_" + n) for n in names.split()}
    step = sem(c, "e_step")
    x_loaded = [sem(c, f"e_x_loaded{u}") for u in range(2)]
    y_stored = [sem(c, f"e_y_stored{u}") for u in range(2)]
    res_loaded = [sem(c, f"e_res_loaded{u}") for u in range(2)]
    gathered = [sem(c, f"e_gathered{u}") for u in range(2)]
    out_stored = [sem(c, f"e_out_stored{u}") for u in range(2)]
    summed = sem(c, "e_summed")
    block = c.enter_context(nc.Block())
    GROUPS = STEPS2 // 4

    def by_parity(ap, g, par):
        return ap.rearrange("b (j r) d -> b j r d", r=2)[:, bass.ds(g * 4, 4), par]

    @block.sync
    def _(sp):
        sp.dma_start(b2[:].rearrange("p e d -> p (e d)"),
                     t["L1_ffn_b2"].rearrange("e d -> (e d)").partition_broadcast(P)).then_inc(S["b2_loaded"], 16)
        sp.wait_ge(S["scattered"], 16 * STEPS2)

        def load_rows(e, u):
            sp.dma_start(xe[u][:, 0:2], xtab_d[bass.ds(e * CAP, 2 * P)].rearrange("(n p) d -> p n d", p=P)).then_inc(x_loaded[u], 16)
            sp.dma_start(xe[u][0:64, 2], xtab_d[bass.ds(e * CAP + 2 * P, 64)]).then_inc(x_loaded[u], 16)

        def store(e, u):
            sp.wait_ge(S["y_done"], e * 3 + 3)
            sp.dma_start(ytab_d[bass.ds(e * CAP, 2 * P)].rearrange("(n p) d -> p n d", p=P), ye[u][:, 0:2]).then_inc(y_stored[u], 16)
            sp.dma_start(ytab_d[bass.ds(e * CAP + 2 * P, 64)], ye[u][0:64, 2]).then_inc(y_stored[u], 16)

        for u in range(2):
            load_rows(u, u)
        for u in range(2):
            for par in range(2):
                sp.dma_start(res[u][64 * par:64 * par + 64], by_parity(x1_d, u, par)).then_inc(res_loaded[u], 16)
        with sp.Fori(0, E // 2 - 1) as n:
            for u in range(2):
                e = n * 2 + u
                store(e, u)
                load_rows(e + 2, u)
                load_expert(nc, sp, t, e + 2, ew1[u], ew2[u], eb1[u], e_loaded[u])
        for u in range(2):
            store(E - 2 + u, u)
        with sp.Fori(0, GROUPS // 2 - 1) as n:
            for u in range(2):
                g = n * 2 + u
                sp.wait_ge(summed, g + 1)
                for par in range(2):
                    sp.dma_start(by_parity(t["out"], g, par), got[u][64 * par:64 * par + 64]).then_inc(out_stored[u], 16)
                for par in range(2):
                    sp.dma_start(res[u][64 * par:64 * par + 64], by_parity(x1_d, g + 2, par)).then_inc(res_loaded[u], 16)
        for u in range(2):
            g = GROUPS - 2 + u
            sp.wait_ge(summed, g + 1)
            for par in range(2):
                sp.dma_start(by_parity(t["out"], g, par), got[u][64 * par:64 * par + 64]).then_inc(out_stored[u], 16)
        for u in range(2):
            sp.wait_ge(out_stored[u], 32 * (GROUPS // 2))

    @block.gpsimd
    def _(pool):
        pool.wait_ge(S["idx_done"], 1)
        for j in range(STEPS2):
            pool.indirect_dma_start(xtab_d, bass.IndirectOffsetOnAxis(idx[:, j:j + 1], 0), h_rows[:, j], None).then_inc(S["scattered"], 16)
        for u in range(2):
            pool.wait_ge(y_stored[u], 32 * E // 2)
        for g in range(GROUPS):
            u = g % 2
            pool.wait_ge(out_stored[u], g // 2 * 32)
            for i in range(4):
                pool.indirect_dma_start(got[u][:, i], None, ytab_d,
                                        bass.IndirectOffsetOnAxis(idx[:, g * 4 + i:g * 4 + i + 1], 0)).then_inc(gathered[u], 16)

    @block.tensor
    def _(pe):
        pe.wait_ge(S["hot_done"], 1)
        flat = "p j e -> p (j e)"
        pe.matmul(pxT[:, 0, 0:STEPS2 * E], const("same_b"), count[:].rearrange(flat), start=True, stop=False)
        pe.matmul(pxT[:, 0, 0:STEPS2 * E], const("drop"), hot[:].rearrange(flat), start=False, stop=False)
        pe.matmul(pxT[:, 0, 0:STEPS2 * E], const("before"),
                  count[:, STEPS2 - 1].unsqueeze(1).broadcast_to(big), start=False, stop=True).then_inc(S["rank_ps"], 1)
        pe.wait_ge(S["idx_done"], 1)

        def turn(e, n, u):
            pe.wait_ge(x_loaded[u], n * 32 + 32)
            pe.wait_ge(S["xT_done"], e)
            for k in range(KT):
                for i, (o, w) in enumerate(CAPT):
                    m = pe.transpose(pxT[:, k, o:o + w], xe[u][0:w, i, k * P:(k + 1) * P], ident[0:w, 0:w])
            m.then_inc(S["xT_ps"], 1)

        def up(e, n, u):
            pe.wait_ge(S["xT_done"], e + 1)
            pe.wait_ge(e_loaded[u], n * 48 + 48)
            for f in range(FT):
                pe.wait_ge(S["hid_act"] if f % 2 == 0 else S["hid_dve"], e * 4 + max(f // 2 - 1, 0))
                for k in range(KT):
                    m = pe.matmul(phid[f % 4][:, 0:CAP], ew1[u][:, k, f * P:(f + 1) * P], xeT[:, k], start=(k == 0), stop=(k == KT - 1))
                m.then_inc(S["hid_ps"], 1)

        def down(e, u):
            pe.wait_ge(S["hid_act"], e * 4 + 4)
            pe.wait_ge(S["hid_dve"], e * 4 + 4)
            for i, (o, w) in enumerate(CAPT):
                pe.wait_ge(S["y_done"], e * 3 + max(i - 1, 0))
                for f in range(FT):
                    m = pe.matmul(pyo[0 if i != 1 else 1][0:w, 0:D], hT[:, f, o:o + w], ew2[u][:, f], start=(f == 0), stop=(f == FT - 1))
                m.then_inc(S["y_ps"], 1)

        turn(0, 0, 0)
        def two(n):
            for u in range(2):
                up(n * 2 + u, n, u)
                turn(n * 2 + u + 1, n + u, 1 - u)
                down(n * 2 + u, u)

        two(0)
        with pe.Fori(1, E // 2 - 1) as n:
            two(n)
        up(E - 2, E // 2 - 1, 0)
        turn(E - 1, E // 2 - 1, 1)
        down(E - 2, 0)
        up(E - 1, E // 2 - 1, 1)
        down(E - 1, 1)

    @block.scalar
    def _(act):
        def two(n):
            for u in range(2):
                e = n * 2 + u
                act.wait_ge(S["xT_ps"], e + 1)
                act.wait_ge(S["hid_ps"], e * FT)
                act.copy(xeT[:], pxT[:, :, 0:CAP]).then_inc(S["xT_done"], 1)
                for f in range(0, FT, 2):
                    act.wait_ge(S["hid_ps"], e * FT + (f + 1))
                    act.activation(hT[:, f], phid[f % 4][:, 0:CAP], ACT.Relu, bias=eb1[u][:, f:f + 1]).then_inc(S["hid_act"], 1)

        two(0)
        with act.Fori(1, E // 2) as n:
            two(n)

    @block.vector
    def _(dve):
        done = 0

        def then(ins):
            nonlocal done
            done += 1
            ins.then_inc(step, 1)
            dve.wait_ge(step, done)

        e_minus = const("e_minus").unsqueeze(1).broadcast_to(big)
        dve.memset(ones[:], 1.0)
        then(dve.tensor_reduce(top[:], logits[:], X, ALU.max))
        then(dve.tensor_tensor(eq[:], logits[:], bc(top[:], big), ALU.is_equal))
        then(dve.tensor_tensor(cand[:], eq[:], e_minus, ALU.mult))
        then(dve.tensor_reduce(eid[:], cand[:], X, ALU.min))
        then(dve.tensor_tensor(hot[:], e_minus, bc(eid[:], big), ALU.is_equal))
        for n in range(E):
            m = dve.tensor_tensor_scan(count[:, :, n], ones[:], hot[:, :, n], 0.0, ALU.mult, ALU.add)
        m.then_inc(S["hot_done"], 1)
        dve.wait_ge(S["rank_ps"], 1)
        then(dve.tensor_tensor(rank[:], hot[:], pxT[:, 0, 0:STEPS2 * E].rearrange("p (j e) -> p j e", e=E), ALU.mult))
        then(dve.tensor_reduce(pos[:], rank[:], X, ALU.add))
        then(dve.tensor_scalar(ok[:], pos[:], float(CAP), None, ALU.is_lt))
        then(dve.tensor_scalar(slot[:], eid[:], float(E), float(CAP), ALU.add, ALU.mult))
        then(dve.tensor_tensor(slot[:], slot[:], pos[:], ALU.add))
        then(dve.tensor_tensor(gap[:], slot[:], const("own"), ALU.subtract))
        then(dve.tensor_tensor(gap[:], gap[:], ok[:], ALU.mult))
        dve.tensor_tensor(idx[:], gap[:], const("own"), ALU.add).then_inc(S["idx_done"], 1)
        dve.wait_ge(S["b2_loaded"], 16)

        def two(n):
            for u in range(2):
                e = n * 2 + u
                for f in range(1, FT, 2):
                    dve.wait_ge(S["hid_ps"], e * FT + (f + 1))
                    dve.tensor_scalar(hT[:, f], phid[f % 4][:, 0:CAP], eb1[u][:, f:f + 1], 0.0, ALU.add, ALU.max).then_inc(S["hid_dve"], 1)
                for i, (o, w) in enumerate(CAPT):
                    dve.wait_ge(S["y_ps"], e * 3 + (i + 1))
                    dve.wait_ge(y_stored[u], n * 32)
                    dve.tensor_tensor(ye[u][0:w, i], pyo[0 if i != 1 else 1][0:w, 0:D],
                                      b2[0:w, bass.ds(e, 1)].rearrange("p a d -> p (a d)"), ALU.add).then_inc(S["y_done"], 1)

        two(0)
        with dve.Fori(1, E // 2) as n:
            two(n)
        with dve.Fori(0, GROUPS // 2) as n:
            for u in range(2):
                dve.wait_ge(gathered[u], n * 64 + 64)
                dve.wait_ge(res_loaded[u], n * 32 + 32)
                dve.tensor_tensor(got[u][:], got[u][:], res[u][:], ALU.add).then_inc(summed, 1)


_NAMES = ["x", "cond_1024", "L0_cond_WQ_w", "L0_cond_WQ_b", "L0_cond_WK_w", "L0_cond_WK_b", "L0_cond_WV_w",
          "L0_cond_WV_b", "L0_cond_WO_w", "L0_cond_WO_b", "L0_ffn_g_info", "L0_ffn_W_qkv", "L0_ffn_W_proj",
          "L0_ffn_b_proj", "L1_cond_Wx", "L1_cond_Wh", "L1_cond_b", "L1_ffn_router_w", "L1_ffn_router_b", "L1_ffn_w1",
          "L1_ffn_b1", "L1_ffn_w2", "L1_ffn_b2", "L1_ffn_ow1", "L1_ffn_ob1", "L1_ffn_ow2", "L1_ffn_ob2"]


def kernel(**inputs):
    import concourse.bacc as bacc
    from concourse.bass_utils import run_bass_kernel_spmd as run

    nc = bacc.Bacc("TRN2", target_bir_lowering=False, num_devices=1)
    arrays, tensors = {}, {}
    table, const_at = shape_constants()
    given = {n: np.ascontiguousarray(inputs[n]) for n in _NAMES}
    given["consts"] = table
    for name, a in given.items():
        arrays["in_" + name] = a
        tensors[name] = nc.dram_tensor("in_" + name, a.shape, mybir.dt.from_np(a.dtype), kind="ExternalInput").ap()
    tensors["out"] = nc.dram_tensor("out_0", (B, L, D), F32, kind="ExternalOutput").ap()
    build(nc, tensors, const_at)
    return run(nc, [arrays], core_ids=[0]).results[0]["out_0"]
```

```python
from contextlib import ExitStack

import numpy as np

import concourse.bass as bass
from concourse import mybir

ALU = mybir.AluOpType
ACT = mybir.ActivationFunctionType
F32 = mybir.dt.float32
F32R = mybir.dt.float32r
BF16 = mybir.dt.bfloat16
U32 = mybir.dt.uint32
X = mybir.AxisListType.X

P = 128
B, L, D = 64, 64, 256
KT = D // P
PAIRS = B // 2
H0, HD0 = 16, 64
HT = H0 * HD0 // P
H1, HD1 = 16, 16
REG = 5
W0 = L + 2
SPB = 4
NSLOT = H1 + 2
E, CAP, HID = 8, 320, 1024
FT = HID // P
STEPS2 = L // 2
XROWS = E * CAP
NEG = -1.0e30
CAPT = [(0, 128), (128, 128), (256, 64)]


def shape_constants():
    p = np.arange(P)
    ident = np.eye(P, dtype=np.float32)
    band = np.full((P, 2, W0), NEG, np.float32)
    for q in range(P):
        for head, first, extra in ((0, 1, 0), (1, 0, L)):
            for j in (q % L - 1, q % L, q % L + 1):
                if 0 <= j < L:
                    band[q, head, first + j] = 0.0
            band[q, head, extra] = 0.0
            if q % L in (0, L - 1):
                band[q, head, L + 1] = 0.0
    band = band.reshape(P, -1)
    head8 = (p[:, None] // HD1 == np.arange(8)[None]).astype(np.float32)
    head16 = np.zeros((P, KT, H1), np.float32)
    for t in range(KT):
        head16[:, t, 8 * t:8 * t + 8] = head8
    same_head = (p[:, None] // HD1 == p[None] // HD1).astype(np.float32)
    same_seq = (p[:, None] // L == p[None] // L).astype(np.float32)
    key_diag = (p[:, None] % L == np.arange(L)[None]).astype(np.float32)
    tok_row = np.tile((np.arange(L) >= REG).astype(np.float32)[None], (P, 1))
    is_tok = ((p % L) >= REG).astype(np.float32)[:, None]
    par, b = p // B, p % B
    same_b = (b[:, None] == b[None]).astype(np.float32)
    drop = -same_b * ((par[:, None] == 1) | (par[None] == 0))
    before = (b[:, None] < b[None]).astype(np.float32)
    e_minus = np.tile(np.arange(E, dtype=np.float32)[None] - E, (P, 1))
    own = (XROWS + np.arange(STEPS2)[None] * P + p[:, None]).astype(np.float32)
    parts = dict(ident=ident, band=band, head8=head8, head16=head16.reshape(P, -1), same_head=same_head,
                 same_seq=same_seq, key_diag=key_diag, tok_row=tok_row, is_tok=is_tok, same_b=same_b,
                 drop=drop.astype(np.float32), before=before, e_minus=e_minus, own=own)
    at, cols = {}, 0
    for name, a in parts.items():
        at[name] = (cols, a.shape[1])
        cols += a.shape[1]
    return np.concatenate(list(parts.values()), 1), at


def bc(ap, shape):
    return ap.unsqueeze(len(ap.shape)).broadcast_to(shape)


def build(nc, t, CONST_AT):
    with ExitStack() as outer:
        def sbuf(ctx, name, shape, dt=F32):
            return ctx.enter_context(nc.sbuf_tensor(name, shape, dt))

        def sem(ctx, name):
            return ctx.enter_context(nc.semaphore(name))

        consts = sbuf(outer, "consts", [P, sum(w for _, w in CONST_AT.values())])
        ident_h = sbuf(outer, "ident_h", [P, P], BF16)

        def const(name):
            o, w = CONST_AT[name]
            return consts[:, o:o + w]

        ident = const("ident")
        avw_d = nc.dram_tensor("avw_d", [B * H0, D], F32).ap()
        x1_d = nc.dram_tensor("x1_d", [B, L, D], F32).ap()
        xtab_d = nc.dram_tensor("xtab_d", [XROWS + B * L, D], F32).ap()
        ytab_d = nc.dram_tensor("ytab_d", [XROWS + B * L, D], F32).ap()

        fq = sbuf(outer, "fq", [P, KT, B * L])
        fk = sbuf(outer, "fk", [P, KT, B * L])
        fv = sbuf(outer, "fv", [P, PAIRS, D])
        with ExitStack() as c:
            qgblk = sbuf(outer, "qgblk", [P, KT, H1])
            sims = sbuf(outer, "sims", [P, PAIRS, 2 * H1])
            star_pass(nc, c, sbuf, sem, t, const, ident, ident_h, consts, qgblk, fq, fk, fv, sims, avw_d, xtab_d)
        x1T = sbuf(outer, "x1T", [P, KT, L, B])
        with ExitStack() as l0:
            key_bias = sbuf(l0, "key_bias", [P, PAIRS, L], BF16)
            reg_bias = sbuf(l0, "reg_bias", [P, PAIRS, 2, L], BF16)
            with ExitStack() as c:
                classes(nc, c, sbuf, sem, const, ident, sims, key_bias, reg_bias)
            with ExitStack() as c:
                masked_pass(nc, c, sbuf, sem, t, const, ident, ident_h, fq, fk, fv, key_bias, reg_bias, x1T, x1_d)
        h_rows = fv
        room = fk[:].rearrange("p k n -> p (k n)")
        ew1 = [room[:, u * 4096:u * 4096 + 2048].rearrange("p (k n) -> p k n", k=KT) for u in range(2)]
        ew2 = [room[:, u * 4096 + 2048:u * 4096 + 4096].rearrange("p (k n) -> p k n", k=FT) for u in range(2)]
        with ExitStack() as l1:
            logits = sbuf(l1, "logits", [P, STEPS2, E])
            eb1 = [sbuf(l1, f"eb1_{u}", [P, FT]) for u in range(2)]
            e_loaded = [sem(l1, f"e_loaded{u}") for u in range(2)]
            with ExitStack() as c:
                recurrence(nc, c, sbuf, sem, t, const, ident, x1T, h_rows, logits, ytab_d,
                           ew1, ew2, eb1, e_loaded)
            with ExitStack() as c:
                experts(nc, c, sbuf, sem, t, const, ident, h_rows, logits, x1_d, xtab_d, ytab_d,
                        ew1, ew2, eb1, e_loaded)


def star_pass(nc, c, sbuf, sem, t, const, ident, ident_h, consts, qgblk, fq, fk, fv, sims, avw_d, xtab_d):
    wq = sbuf(c, "wq", [P, KT, H0 * HD0])
    wk = sbuf(c, "wk", [P, KT, H0 * HD0])
    wo = sbuf(c, "wo", [P, HT, D])
    wqkv = sbuf(c, "wqkv", [P, KT, 3 * D])
    bq, bk, bv = (sbuf(c, n, [P, HT]) for n in ("bq", "bk", "bv"))
    bo = sbuf(c, "bo", [P, KT])
    akT = sbuf(c, "akT", [P, HT, B])
    headones = const("head16").rearrange("p (t h) -> p t h", t=KT)
    band_h = sbuf(c, "band_h", [P, SPB // 2, 2 * W0], BF16)
    xrow = sbuf(c, "xrow", [P, D])
    avw = sbuf(c, "avw", [2 * H0, D])
    kblk = sbuf(c, "kblk", [P, HT, 2, 2 * (L + 1)])
    prob = sbuf(c, "prob", [P, H0, W0])
    pkey = sbuf(c, "pkey", [P, H0, L])
    acond = sbuf(c, "acond", [P, 2 * H0])
    mx, sm, aw = (sbuf(c, n, [P, H0]) for n in ("mx", "sm", "aw"))

    with ExitStack() as s:
        cond = sbuf(s, "cond", [B, D])
        condT = sbuf(s, "condT", [P, KT, B])
        avT = sbuf(s, "avT", [P, HT, B])
        wv = fk[:, :, 0:H0 * HD0]
        avw_rows = fv[0:B, 0:H0]
        g, g2, gn = (sbuf(s, n, [P, KT]) for n in ("g", "g2", "gn"))
        zero = sbuf(s, "zero", [P, 4 * D])
        pst = s.enter_context(nc.psum_tensor("pst", [P, 2, 512], F32))
        psa = s.enter_context(nc.psum_tensor("psa", [P, 2, 512], F32))
        psv = s.enter_context(nc.psum_tensor("psv", [B, 4, 512], F32))
        loaded, wv_loaded, zero_set, zeroed, avw_stored = (sem(s, n) for n in (
            "p_loaded", "p_wv_loaded", "p_zero_set", "p_zeroed", "p_avw_stored"))
        condT_ps, condT_done, ak_ps, ak_done, av_ps, av_done, avw_ps, avw_done = (sem(s, n) for n in (
            "p_condT_ps", "p_condT_done", "p_ak_ps", "p_ak_done", "p_av_ps", "p_av_done", "p_avw_ps", "p_avw_done"))
        g2_done, gs_ps, gs_root, gs_inv, gn_done, pad_set = (sem(s, n) for n in (
            "p_g2_done", "p_gs_ps", "p_gs_root", "p_gs_inv", "p_gn_done", "p_pad_set"))
        block = s.enter_context(nc.Block())
        loads = [
            (consts[:], t["consts"]), (cond[:], t["cond_1024"]),
            (bk[:], t["L0_cond_WK_b"].rearrange("(m p) -> p m", p=P)),
            (bv[:], t["L0_cond_WV_b"].rearrange("(m p) -> p m", p=P)),
            (bq[:], t["L0_cond_WQ_b"].rearrange("(m p) -> p m", p=P)),
            (bo[:], t["L0_cond_WO_b"].rearrange("(m p) -> p m", p=P)),
            (g[:], t["L0_ffn_g_info"][0, 0].rearrange("(m p) -> p m", p=P)),
            (wk[:], t["L0_cond_WK_w"].rearrange("(k p) n -> p k n", p=P)),
            (wq[:], t["L0_cond_WQ_w"].rearrange("(k p) n -> p k n", p=P)),
            (wo[:], t["L0_cond_WO_w"].rearrange("(k p) n -> p k n", p=P)),
            (wqkv[:], t["L0_ffn_W_qkv"].rearrange("(k p) n -> p k n", p=P)),
        ]

        @block.sync
        def _(sp):
            for dst, src in loads:
                with nc.allow_non_contiguous_dma(reason="bias columns"):
                    sp.dma_start(dst, src).then_inc(loaded, 16)
            sp.dma_start(wv, t["L0_cond_WV_w"].rearrange("(k p) n -> p k n", p=P)).then_inc(wv_loaded, 16)
            sp.wait_ge(zero_set, 1)
            rows = XROWS // P // 4
            for n in range(rows):
                sp.dma_start(xtab_d[n * 4 * P:(n + 1) * 4 * P].rearrange("(p r) d -> p (r d)", p=P),
                             zero[:]).then_inc(zeroed, 16)
            sp.wait_ge(avw_done, H0 // 2)
            sp.dma_start(avw_d.rearrange("(b h) d -> b h d", h=H0), avw_rows).then_inc(avw_stored, 16)
            sp.wait_ge(zeroed, 16 * rows)
            sp.wait_ge(avw_stored, 16)

        @block.tensor
        def _(pe):
            pe.wait_ge(loaded, 16 * len(loads))
            for k in range(KT):
                m = pe.transpose(pst[:, 0, k * B:(k + 1) * B], cond[:, k * P:(k + 1) * P], ident[0:B, 0:B])
            m.then_inc(condT_ps, 1)
            pe.wait_ge(condT_done, 1)
            for w, out, ready in ((wk, psa[:, 0], ak_ps), (wv, psa[:, 1], av_ps)):
                if w is wv:
                    pe.wait_ge(wv_loaded, 16)
                for n in range(HT):
                    for k in range(KT):
                        m = pe.matmul(out[:, n * B:(n + 1) * B], w[:, k, n * P:(n + 1) * P], condT[:, k],
                                      start=(k == 0), stop=(k == KT - 1))
                m.then_inc(ready, 1)
            pe.wait_ge(g2_done, 1)
            pe.matmul(pst[:, 1, 0:KT], const("same_head"), g2[:], start=True, stop=True).then_inc(gs_ps, 1)
            pe.wait_ge(av_done, 1)
            for n in range(H0 // 2):
                if n >= 2:
                    pe.wait_ge(avw_done, n - 1)
                for a in range(2):
                    m = pe.matmul(psv[:, 2 * (n % 2) + a, 0:D], avT[64 * a:64 * a + 64, n],
                                  wo[64 * a:64 * a + 64, n], start=True, stop=True)
                m.then_inc(avw_ps, 1)

        @block.vector
        def _(dve):
            dve.memset(zero[:], 0.0).then_inc(zero_set, 1)
            dve.memset(kblk[:], 0.0)
            dve.memset(acond[:], 0.0).then_inc(pad_set, 1)
            dve.wait_ge(loaded, 16 * len(loads))
            dve.tensor_copy(ident_h[:], ident)
            for n in range(SPB // 2):
                dve.tensor_copy(band_h[:, n], const("band"))
            dve.tensor_tensor(g2[:], g[:], g[:], ALU.mult).then_inc(g2_done, 1)
            dve.wait_ge(condT_ps, 1)
            dve.tensor_copy(condT[:].rearrange("p k b -> p (k b)"), pst[:, 0, 0:KT * B]).then_inc(condT_done, 1)
            dve.wait_ge(ak_ps, 1)
            dve.tensor_tensor(akT[:], psa[:, 0].rearrange("p (m b) -> p m b", b=B), bc(bk[:], [P, HT, B]),
                              ALU.add).then_inc(ak_done, 1)
            dve.wait_ge(av_ps, 1)
            dve.tensor_tensor(avT[:], psa[:, 1].rearrange("p (m b) -> p m b", b=B), bc(bv[:], [P, HT, B]),
                              ALU.add).then_inc(av_done, 1)
            dve.wait_ge(gs_root, 1)
            dve.reciprocal(g2[:], gn[:]).then_inc(gs_inv, 1)
            dve.wait_ge(gs_inv, 1)
            dve.tensor_tensor(gn[:], g2[:], g[:], ALU.mult).then_inc(gn_done, 1)
            dve.wait_ge(gn_done, 1)
            dve.tensor_tensor(qgblk[:], headones, bc(gn[:], [P, KT, H1]), ALU.mult)
            for n in range(H0 // 2):
                dve.wait_ge(avw_ps, n + 1)
                dve.tensor_copy(avw_rows[:, 2 * n:2 * n + 2], psv[:, 2 * (n % 2):2 * (n % 2) + 2, 0:D]).then_inc(avw_done, 1)

        @block.scalar
        def _(act):
            act.wait_ge(gs_ps, 1)
            act.activation(gn[:], pst[:, 1, 0:KT], ACT.Sqrt).then_inc(gs_root, 1)

    with ExitStack() as s:
        xT = sbuf(s, "xT", [P, KT, P])
        qT = sbuf(s, "qT", [P, HT, P])
        vblk = sbuf(s, "vblk", [P, HT, 2, P])
        probT = sbuf(s, "probT", [P, HT, P])
        acondT = sbuf(s, "acondT", [2 * H0, P])
        attT = sbuf(s, "attT", [P, HT, P])
        yT = sbuf(s, "yT", [P, KT, P])
        qs = sbuf(s, "qs", [P, KT, P])
        qq = sbuf(s, "qq", [P, KT, P])
        score = s.enter_context(nc.psum_tensor("score", [P, 4, 512], F32))
        bank = [s.enter_context(nc.psum_tensor(f"bank{n}", [P, 512], F32)) for n in range(4)]
        names = ("x_loaded avw_loaded xT_ps xT_done q_ps q_done k_ps k_done ak_set s_ps max_done sub_done exp_done "
                 "sum_done inv_done prob_done aw_done acond_done pT_ps pT_done aT_ps aT_done att_ps att_done y_ps y_done "
                 "f_ps fq_done fk_done qq_done fv_ps fv_done v_ps v_done sim_ps sim_done fq_kept")
        S = {n: sem(s, "a_" + n) for n in names.split()}
        block = s.enter_context(nc.Block())
        s4 = score[:].rearrange("p n c -> p (n c)")

        def slots(half):
            return score[:, 2 * half:2 * half + 2, 0:SPB * W0].rearrange("p n (s w) -> p n s w", w=W0)

        def half_of(ap, half):
            return ap[:, 8 * half:8 * half + 8]

        def prob4(half):
            return prob[:, 8 * half:8 * half + 8].rearrange("p (n s) w -> p n s w", s=SPB)

        @block.sync
        def _(sp):
            def load(i, first=False):
                if not first:
                    sp.wait_ge(S["xT_ps"], i)
                sp.dma_start(xrow[:], t["x"][bass.ds(i * 2, 2)].rearrange("b l d -> (b l) d")).then_inc(S["x_loaded"], 16)
                if not first:
                    sp.wait_ge(S["y_ps"], i)
                sp.dma_start(avw[:], avw_d[bass.ds(i * 2 * H0, 2 * H0)]).then_inc(S["avw_loaded"], 16)
            load(0, True)
            with sp.Fori(1, PAIRS) as i:
                load(i)

        Q_BANK, K_BANK = (1, 3), (2, 0)
        W_BANK, A_BANK, ATT_BANK, Y_BANK = (1, 3), 2, (1, 3), 0
        V_BANK, F_BANK, FV_BANK, X_BANK, SIM_BANK = (2, 1, 3, 2), 0, 1, 3, 2

        @block.tensor
        def _(pe):
            def turn_x(i):
                pe.wait_ge(S["x_loaded"], i * 16 + 16)
                for k in range(KT):
                    m = pe.transpose(bank[X_BANK][:, k * P:(k + 1) * P], xrow[:, k * P:(k + 1) * P], ident)
                m.then_inc(S["xT_ps"], 1)

            def project(i, first=False):
                pe.wait_ge(S["xT_done"], i + 1)
                if not first:
                    pe.wait_ge(S["fv_done"], i - 1)
                for half in range(2):
                    for n in range(4):
                        for k in range(KT):
                            m = pe.matmul(bank[Q_BANK[half]][:, n * P:(n + 1) * P],
                                          wq[:, k, (4 * half + n) * P:(4 * half + n + 1) * P],
                                          xT[:, k], start=(k == 0), stop=(k == KT - 1))
                    m.then_inc(S["q_ps"], 1)
                if not first:
                    pe.wait_ge(S["sim_done"], i - 1)
                for half in range(2):
                    for n in range(4):
                        for k in range(KT):
                            m = pe.matmul(bank[K_BANK[half]][:, n * P:(n + 1) * P],
                                          wk[:, k, (4 * half + n) * P:(4 * half + n + 1) * P],
                                          xT[:, k], start=(k == 0), stop=(k == KT - 1))
                    m.then_inc(S["k_ps"], 1)

            def weights(i, last=False):
                if last:
                    pe.wait_ge(S["xT_done"], i + 1)
                    pe.wait_ge(S["fv_done"], i)
                    pe.wait_ge(S["sim_done"], i)
                else:
                    pe.wait_ge(S["q_done"], i * 2 + 4)
                for half in range(2):
                    pe.wait_ge(S["prob_done"], i * 2 + half + 1)
                    for n in range(4):
                        p = 4 * half + n
                        m = pe.transpose(bank[W_BANK[half]][:, n * P:(n + 1) * P],
                                         pkey[:, 2 * p:2 * p + 2].rearrange("p a k -> p (a k)"), ident)
                    m.then_inc(S["pT_ps"], 1)
                pe.wait_ge(S["acond_done"], i + 1)
                if not last:
                    pe.wait_ge(S["k_done"], i * 2 + 3)
                pe.transpose(bank[A_BANK][0:2 * H0, 0:P], acond[:], ident).then_inc(S["aT_ps"], 1)

            def attend(i):
                pe.wait_ge(S["v_done"], i * 4 + 4)
                for half in range(2):
                    pe.wait_ge(S["pT_done"], i * 2 + half + 1)
                    for n in range(4):
                        p = 4 * half + n
                        for q in range(2):
                            for a in range(2):
                                m = pe.matmul(bank[ATT_BANK[half]][64 * a:64 * a + 64, n * P + q * L:n * P + (q + 1) * L],
                                              vblk[:, p, q, 64 * a:64 * a + 64], probT[:, p, q * L:(q + 1) * L],
                                              start=True, stop=True)
                    m.then_inc(S["att_ps"], 1)

            def mask_scores(i):
                pe.wait_ge(S["sub_done"], i * 2)
                for n in range(4):
                    pe.matmul(score[:, n, 0:SPB * W0], ident_h[:], band_h[:].rearrange("p n w -> p (n w)"),
                              start=True, stop=True)

            def scores(i):
                pe.wait_ge(S["q_done"], i * 2 + 2)
                pe.wait_ge(S["k_done"], i * 2 + 2)
                pe.wait_ge(S["ak_set"], i + 1)
                for p in range(HT):
                    for q in range(2):
                        o = (p % 2) * 2 * W0
                        out = score[64 * q:64 * q + 64, p // 2, o:o + 2 * W0].rearrange("p (s w) -> p s w", w=W0)[:, :, 0:L + 1]
                        m = pe.matmul(out, qT[:, p, q * L:(q + 1) * L], kblk[:, p, q].rearrange("p (s w) -> p s w", s=2),
                                      start=False, stop=True, skip_group_check=True)
                    if p % 4 == 3:
                        m.then_inc(S["s_ps"], 1)

            def through_wo(i):
                pe.wait_ge(S["att_done"], i * 2 + 2)
                pe.wait_ge(S["aT_done"], i + 1)
                pe.wait_ge(S["avw_loaded"], i * 16 + 16)
                for n in range(KT):
                    for p in range(HT):
                        pe.matmul(bank[Y_BANK][:, n * P:(n + 1) * P], wo[:, p, n * P:(n + 1) * P], attT[:, p],
                                  start=(p == 0), stop=False)
                    m = pe.matmul(bank[Y_BANK][:, n * P:(n + 1) * P], avw[:, n * P:(n + 1) * P], acondT[:],
                                  start=False, stop=True)
                m.then_inc(S["y_ps"], 1)

            def values(i, first=False):
                for n in range(4):
                    if n == 3 or first:
                        pe.wait_ge(S["v_done"], i * 4 + (1 if n == 3 else 0))
                    for j in range(4):
                        p, q = 2 * n + j // 2, j % 2
                        m = pe.transpose(bank[V_BANK[n]][:, j * P:(j + 1) * P], kblk[:, p, q, 1:1 + 2 * L], ident)
                    m.then_inc(S["v_ps"], 1)

            def masked_qkv(i, last=False):
                pe.wait_ge(S["y_done"], i + 1)
                for n in range(4):
                    for k in range(KT):
                        m = pe.matmul(bank[F_BANK][:, n * P:(n + 1) * P], wqkv[:, k, n * P:(n + 1) * P], yT[:, k],
                                      start=(k == 0), stop=(k == KT - 1))
                m.then_inc(S["f_ps"], 1)
                if not last:
                    pe.wait_ge(S["v_done"], i * 4 + 6)
                for k in range(KT):
                    m = pe.matmul(bank[FV_BANK][:, 0:D], yT[:, k], wqkv[:, k, 2 * D:3 * D],
                                  start=(k == 0), stop=(k == KT - 1))
                m.then_inc(S["fv_ps"], 1)

            def similarity(i, last=False):
                pe.wait_ge(S["fq_done"], i + 1)
                pe.wait_ge(S["qq_done"], i + 1)
                if not last:
                    pe.wait_ge(S["v_done"], i * 4 + 8)
                for o, src, w in ((0, qs, qgblk), (H1, qq, headones)):
                    for k in range(KT):
                        m = pe.matmul(bank[SIM_BANK][:, o:o + H1], src[:, k], w[:, k], start=(k == 0), stop=(k == KT - 1))
                m.then_inc(S["sim_ps"], 1)

            turn_x(0)
            project(0, True)
            mask_scores(0)
            scores(0)
            pe.wait_ge(S["q_done"], 2)
            values(0, True)
            pe.wait_ge(S["v_done"], 3)
            turn_x(1)
            pe.wait_ge(S["v_done"], 4)

            def step(i, last=False):
                project(i + 1, isinstance(i, int) and i == 0)
                weights(i)
                mask_scores(i + 1)
                attend(i)
                scores(i + 1)
                through_wo(i)
                values(i + 1)
                masked_qkv(i)
                if not last:
                    pe.wait_ge(S["v_done"], i * 4 + 7)
                    turn_x(i + 2)
                similarity(i)

            step(0)
            with pe.Fori(1, PAIRS - 2) as i:
                step(i)
            step(PAIRS - 2, True)
            weights(PAIRS - 1, True)
            attend(PAIRS - 1)
            through_wo(PAIRS - 1)
            masked_qkv(PAIRS - 1, True)
            similarity(PAIRS - 1, True)

        @block.vector
        def _(dve):
            def bias_out(i):
                for half in range(2):
                    dve.wait_ge(S["q_ps"], i * 2 + half + 1)
                    dve.tensor_tensor(qT[:, 4 * half:4 * half + 4], bank[Q_BANK[half]][:].rearrange("p (m n) -> p m n", n=P),
                                      bc(bq[:, 4 * half:4 * half + 4], [P, 4, P]), ALU.add).then_inc(S["q_done"], 1)
                for half in range(2):
                    dve.wait_ge(S["k_ps"], i * 2 + half + 1)
                    for a in range(2):
                        r = slice(64 * a, 64 * a + 64)
                        src = bank[K_BANK[half]][r].rearrange("p (m q n) -> p m q n", q=2, n=L)
                        b4 = bc(bc(bk[r, 4 * half:4 * half + 4], [64, 4, 2]), [64, 4, 2, L])
                        m = dve.tensor_tensor(kblk[r, 4 * half:4 * half + 4, :, 1 + a * L:1 + (a + 1) * L], src, b4, ALU.add)
                    m.then_inc(S["k_done"], 1)

            def softmax(i):
                for half in range(2):
                    dve.wait_ge(S["s_ps"], i * 2 + half + 1)
                    dve.tensor_reduce(half_of(mx, half).rearrange("p (n s) -> p n s", s=SPB), slots(half), X,
                                      ALU.max).then_inc(S["max_done"], 1)
                    dve.wait_ge(S["max_done"], i * 2 + half + 1)
                    dve.wait_ge(S["acond_done"], i)
                    dve.tensor_tensor(prob4(half), slots(half),
                                      bc(half_of(mx, half).rearrange("p (n s) -> p n s", s=SPB), [P, 2, SPB, W0]),
                                      ALU.subtract).then_inc(S["sub_done"], 1)
                for half in range(2):
                    dve.wait_ge(S["exp_done"], i * 2 + half + 1)
                    dve.tensor_reduce(half_of(sm, half), prob[:, 8 * half:8 * half + 8], X, ALU.add).then_inc(S["sum_done"], 1)
                    dve.wait_ge(S["sum_done"], i * 2 + half + 1)
                    dve.reciprocal(half_of(sm, half), half_of(sm, half)).then_inc(S["inv_done"], 1)

            def sim_out(i):
                dve.wait_ge(S["sim_ps"], i + 1)
                dve.tensor_copy(sims[:, bass.ds(i, 1)].rearrange("p a b -> p (a b)"),
                                bank[SIM_BANK][:, 0:2 * H1]).then_inc(S["sim_done"], 1)

            bias_out(0)
            softmax(0)
            with dve.Fori(0, PAIRS - 1) as i:
                bias_out(i + 1)
                softmax(i + 1)
                sim_out(i)
            sim_out(PAIRS - 1)

        @block.scalar
        def _(act):
            def xT_out(i):
                act.wait_ge(S["xT_ps"], i + 1)
                act.wait_ge(S["k_ps"], i * 2)
                act.copy(xT[:].rearrange("p k n -> p (k n)"), bank[X_BANK][:, 0:KT * P]).then_inc(S["xT_done"], 1)

            def attend_out(i):
                for half in range(2):
                    act.wait_ge(S["pT_ps"], i * 2 + half + 1)
                    act.copy(probT[:, 4 * half:4 * half + 4].rearrange("p m n -> p (m n)"), bank[W_BANK[half]][:]).then_inc(S["pT_done"], 1)
                act.wait_ge(S["aT_ps"], i + 1)
                act.copy(acondT[:], bank[A_BANK][0:2 * H0, 0:P]).then_inc(S["aT_done"], 1)
                for half in range(2):
                    act.wait_ge(S["att_ps"], i * 2 + half + 1)
                    act.copy(attT[:, 4 * half:4 * half + 4].rearrange("p m n -> p (m n)"),
                             bank[ATT_BANK[half]][:]).then_inc(S["att_done"], 1)

            def y_out(i):
                act.wait_ge(S["y_ps"], i + 1)
                for n in range(KT):
                    m = act.activation(yT[:, n], bank[Y_BANK][:, n * P:(n + 1) * P], ACT.Identity, bias=bo[:, n:n + 1])
                m.then_inc(S["y_done"], 1)

            def exps(i):
                for half in range(2):
                    act.wait_ge(S["sub_done"], i * 2 + half + 1)
                    act.activation(prob[:, 8 * half:8 * half + 8], prob[:, 8 * half:8 * half + 8], ACT.Exp,
                                   scale=HD0 ** -0.5).then_inc(S["exp_done"], 1)

            def masked_out(i):
                act.wait_ge(S["f_ps"], i + 1)
                act.wait_ge(S["fq_kept"], i)
                act.wait_ge(S["sim_ps"], i)
                qp = bank[F_BANK][:, 0:KT * P].rearrange("p (k n) -> p k n", n=P)
                act.copy(qs[:], qp).then_inc(S["fq_done"], 1)
                act.activation(qq[:], qp, ACT.Square).then_inc(S["qq_done"], 1)
                act.copy(fk[:, :, bass.ds(i * P, P)], bank[F_BANK][:, KT * P:].rearrange("p (k n) -> p k n", n=P)).then_inc(S["fk_done"], 1)
                act.wait_ge(S["fv_ps"], i + 1)
                act.copy(fv[:, bass.ds(i, 1)].rearrange("p a b -> p (a b)"), bank[FV_BANK][:, 0:D]).then_inc(S["fv_done"], 1)

            def values_out(i):
                for n in range(4):
                    act.wait_ge(S["v_ps"], i * 4 + n + 1)
                    act.copy(vblk[:, 2 * n:2 * n + 2].rearrange("p m q n -> p (m q n)"), bank[V_BANK[n]][:]).then_inc(S["v_done"], 1)

            xT_out(0)
            exps(0)
            values_out(0)
            xT_out(1)

            def step(i, last=False):
                attend_out(i)
                exps(i + 1)
                y_out(i)
                values_out(i + 1)
                masked_out(i)
                if not last:
                    xT_out(i + 2)

            step(0)
            with act.Fori(1, PAIRS - 2) as i:
                step(i)
            step(PAIRS - 2, True)
            attend_out(PAIRS - 1)
            y_out(PAIRS - 1)
            masked_out(PAIRS - 1)

        upper_lower = [const("same_seq")[:, 64 * q:64 * q + 1] for q in range(2)]

        @block.gpsimd
        def _(pool):
            def condition_keys(i, first=False):
                if not first:
                    pool.wait_ge(S["v_ps"], i * 4)
                for a in range(2):
                    m = pool.tensor_tensor(kblk[:, :, :, a * (2 * L + 1)], akT[:, :, bass.ds(i * 2, 2)],
                                           bc(upper_lower[a].broadcast_to([P, HT]), [P, HT, 2]), ALU.mult)
                m.then_inc(S["ak_set"], 1)

            def normalise(i):
                for half in range(2):
                    pool.wait_ge(S["inv_done"], i * 2 + half + 1)
                    pool.wait_ge(S["pT_ps"], i * 2)
                    for a in range(2):
                        heads = slice(8 * half + a, 8 * half + 8, 2)
                        m = pool.tensor_tensor(pkey[:, heads], prob[:, heads, 1 - a:1 - a + L], bc(sm[:, heads], [P, 4, L]), ALU.mult)
                    m.then_inc(S["prob_done"], 1)
                pool.wait_ge(S["aT_ps"], i)
                for a in range(2):
                    m = pool.tensor_tensor(aw[:, a::2], prob[:, a::2, a * L], sm[:, a::2], ALU.mult)
                m.then_inc(S["aw_done"], 1)
                pool.wait_ge(S["aw_done"], i + 1)
                for q in range(2):
                    m = pool.tensor_tensor(acond[:, q * H0:(q + 1) * H0], aw[:], upper_lower[q].broadcast_to([P, H0]), ALU.mult)
                m.then_inc(S["acond_done"], 1)

            def keep_q(i):
                pool.wait_ge(S["fq_done"], i + 1)
                pool.tensor_copy(fq[:, :, bass.ds(i * P, P)], qs[:]).then_inc(S["fq_kept"], 1)

            condition_keys(0, True)
            normalise(0)
            with pool.Fori(0, PAIRS - 1) as i:
                condition_keys(i + 1)
                normalise(i + 1)
                keep_q(i)
            keep_q(PAIRS - 1)




def classes(nc, c, sbuf, sem, const, ident, sims, key_bias, reg_bias):
    n16 = [P, PAIRS, H1]
    root, inv = sbuf(c, "root", n16), sbuf(c, "inv", n16)
    sim, low, high, scaled, cls = (sbuf(c, n, [P, PAIRS]) for n in ("sim", "low", "high", "scaled", "cls"))
    ext, extT, both, span = sbuf(c, "ext", [P, 2]), sbuf(c, "extT", [2, P]), sbuf(c, "both", [P, 2]), sbuf(c, "span", [P, 2])
    ends, endrow = sbuf(c, "ends", [2, 1]), sbuf(c, "endrow", [2, 2])
    ones2 = sbuf(c, "ones2", [2, P])
    far = sbuf(c, "far", [P, 1])
    diag = sbuf(c, "diag", [P, PAIRS, L], BF16)
    seq_h = sbuf(c, "seq_h", [P, P], BF16)
    allow, slope, offset, tmp = (sbuf(c, n, [P, PAIRS, L]) for n in ("allow", "slope", "offset", "tmp"))
    first_h = sbuf(c, "first_h", [P, 2, P], BF16)
    ps = c.enter_context(nc.psum_tensor("cls_ps", [P, 4, 512], F32))
    ps_reg = c.enter_context(nc.psum_tensor("cls_reg", [P, 2, 512], F32))
    ps_s = c.enter_context(nc.psum_tensor("cls_s", [P, 512], F32))
    rooted, ext_done, extT_ps, end_set, end_ps, diag_done, key_ps, reg_ps, reg_done = (sem(c, "c_" + n) for n in (
        "rooted", "ext_done", "extT_ps", "end_set", "end_ps", "diag_done", "key_ps", "reg_ps", "reg_done"))
    step = sem(c, "c_step")
    block = c.enter_context(nc.Block())

    @block.scalar
    def _(act):
        act.activation(root[:], sims[:, :, H1:2 * H1], ACT.Sqrt).then_inc(rooted, 1)

    @block.tensor
    def _(pe):
        pe.wait_ge(ext_done, 1)
        pe.transpose(ps_s[0:2, 0:P], ext[:], ident).then_inc(extT_ps, 1)
        pe.wait_ge(end_set, 1)
        pe.matmul(ps_s[:, P:P + 2], ones2[:], endrow[:], start=True, stop=True).then_inc(end_ps, 1)
        pe.wait_ge(diag_done, 1)
        for n in range(4):
            m = pe.matmul(ps[:, n], seq_h[:], diag[:, 8 * n:8 * n + 8].rearrange("p a b -> p (a b)"), start=True, stop=True)
        m.then_inc(key_ps, 1)
        for n in range(8):
            if n >= 1:
                pe.wait_ge(reg_done, n)
            for q in range(2):
                m = pe.matmul(ps_reg[:, q, 0:4 * L], first_h[:, q],
                              diag[:, 4 * n:4 * n + 4].rearrange("p a b -> p (a b)"), start=True, stop=True)
            m.then_inc(reg_ps, 1)

    @block.vector
    def _(dve):
        done = 0

        def then(ins):
            nonlocal done
            done += 1
            ins.then_inc(step, 1)
            dve.wait_ge(step, done)

        dve.memset(endrow[:], 0.0)
        dve.memset(ones2[:], 1.0)
        dve.memset(allow[:], 0.0)
        dve.tensor_copy(seq_h[:], const("same_seq"))
        for q in range(2):
            then(dve.tensor_scalar(first_h[:, q], const("same_seq")[:, 64 * q:64 * q + 1].broadcast_to([P, P]), 1.0, None, ALU.mult))
        then(dve.tensor_scalar(far[:], const("is_tok"), -NEG, NEG, ALU.mult, ALU.add))
        dve.wait_ge(rooted, 1)
        then(dve.reciprocal(inv[:], root[:]))
        then(dve.tensor_tensor(root[:], sims[:, :, 0:H1], inv[:], ALU.mult))
        then(dve.tensor_reduce(low[:], root[:], X, ALU.add))
        then(dve.tensor_scalar(sim[:], low[:], 1.0 / H1, None, ALU.mult))
        then(dve.tensor_scalar(high[:], sim[:], far[:], None, ALU.add))
        then(dve.tensor_scalar(low[:], sim[:], -1.0, far[:], ALU.mult, ALU.add))
        dve.tensor_reduce(ext[:, 0:1], low[:], X, ALU.max)
        dve.tensor_reduce(ext[:, 1:2], high[:], X, ALU.max).then_inc(ext_done, 1)
        dve.wait_ge(extT_ps, 1)
        then(dve.tensor_reduce(ends[:], ps_s[0:2, 0:P], X, ALU.max))
        dve.tensor_tensor(endrow[:], ident[0:2, 0:2], ends[:].broadcast_to([2, 2]), ALU.mult).then_inc(end_set, 1)
        dve.wait_ge(end_ps, 1)
        then(dve.tensor_copy(both[:], ps_s[:, P:P + 2]))
        then(dve.tensor_tensor(span[:, 0:1], both[:, 0:1], both[:, 1:2], ALU.add))
        then(dve.reciprocal(span[:, 1:2], span[:, 0:1]))
        then(dve.tensor_scalar(scaled[:], sim[:], both[:, 0:1], span[:, 1:2], ALU.add, ALU.mult))
        then(dve.tensor_scalar(low[:], scaled[:], 0.9, const("is_tok"), ALU.is_gt, ALU.mult))
        dve.tensor_tensor(diag[:], bc(low[:], [P, PAIRS, L]),
                          const("key_diag").unsqueeze(1).broadcast_to([P, PAIRS, L]), ALU.mult).then_inc(diag_done, 1)
        then(dve.tensor_scalar(far[:], const("is_tok"), -1.0, 1.0, ALU.mult, ALU.add))
        then(dve.tensor_scalar(cls[:], low[:], far[:], None, ALU.add))
        dve.tensor_scalar(high[:], cls[:], -2.0, 1.0, ALU.mult, ALU.add)
        then(dve.tensor_tensor(offset[:], bc(cls[:], [P, PAIRS, L]),
                               const("tok_row").unsqueeze(1).broadcast_to([P, PAIRS, L]), ALU.mult))
        dve.wait_ge(key_ps, 1)
        then(dve.tensor_tensor(slope[:], ps[:].rearrange("p n (a b) -> p (n a) b", b=L), bc(high[:], [P, PAIRS, L]), ALU.mult))
        then(dve.tensor_tensor(tmp[:], slope[:], offset[:], ALU.add))
        dve.tensor_scalar(key_bias[:], tmp[:], NEG, None, ALU.mult)
        for n in range(8):
            dve.wait_ge(reg_ps, n + 1)
            dve.tensor_scalar(reg_bias[:, 4 * n:4 * n + 4].rearrange("p a q b -> p q a b"),
                              ps_reg[:, :, 0:4 * L].rearrange("p q (a b) -> p q a b", b=L), NEG, None,
                              ALU.mult).then_inc(reg_done, 1)


def masked_pass(nc, c, sbuf, sem, t, const, ident, ident_h, fq, fk, fv, key_bias, reg_bias, x1T, x1_d):
    wp = sbuf(c, "wp", [P, KT, D])
    bp = sbuf(c, "bp", [P, D])
    xrow = sbuf(c, "mxrow", [P, D])
    xb = sbuf(c, "xb", [P, D])
    x1 = sbuf(c, "x1", [P, D])
    q = sbuf(c, "q_pair", [P, KT, P])
    kp = sbuf(c, "k_pair", [P, KT, P])
    v = sbuf(c, "v_pair", [P, D])
    rq = sbuf(c, "rq", [P, KT, 2, L])
    kblk = sbuf(c, "mkblk", [P, KT, 2, 8, L])
    vblk = sbuf(c, "mvblk", [P, 2, 8, 2 * HD1])
    prob = sbuf(c, "mprob", [P, NSLOT, L])
    pkey = sbuf(c, "mpkey", [P, NSLOT, L])
    probT = sbuf(c, "mprobT", [P, NSLOT // 2, P])
    oT = sbuf(c, "oT", [P, KT, P])
    mx, sm = sbuf(c, "mmx", [P, NSLOT]), sbuf(c, "msm", [P, NSLOT])
    regh = sbuf(c, "regh", [P, 2 * KT, 8, REG])
    reg = sbuf(c, "reg", [P, KT, 2, REG])
    score = c.enter_context(nc.psum_tensor("mscore", [P, 3, 512], F32))
    pt = [c.enter_context(nc.psum_tensor(f"mpt{n}", [P, 512], F32)) for n in range(2)]
    pr = c.enter_context(nc.psum_tensor("mpr", [P, 512], F32))
    po = c.enter_context(nc.psum_tensor("mpo", [P, 512], F32))
    px = c.enter_context(nc.psum_tensor("mpx", [P, 512], F32))
    names = ("w_loaded x_loaded stored pads q_set k_set v_set rq_set kblk_set vblk_set s_ps max_done sub_done exp_done "
             "sum_done inv_done prob_done pT_ps pT_done o_ps o_done r_ps rmul_done rsum_done radd_done reg_done "
             "xb_done x_ps x1_done x1T_ps x1T_done")
    S = {n: sem(c, "m_" + n) for n in names.split()}
    block = c.enter_context(nc.Block())
    head8 = const("head8")
    sflat = score[:].rearrange("p n c -> p (n c)")[:, 0:NSLOT * L].rearrange("p (s k) -> p s k", k=L)

    @block.sync
    def _(sp):
        sp.dma_start(wp[:], t["L0_ffn_W_proj"].rearrange("(k p) n -> p k n", p=P)).then_inc(S["w_loaded"], 16)
        sp.dma_start(bp[:], t["L0_ffn_b_proj"].partition_broadcast(P)).then_inc(S["w_loaded"], 16)
        def step(i):
            sp.wait_ge(S["xb_done"], i)
            sp.dma_start(xrow[:], t["x"][bass.ds(i * 2, 2)].rearrange("b l d -> (b l) d")).then_inc(S["x_loaded"], 16)
            sp.wait_ge(S["x1_done"], i + 1)
            sp.dma_start(x1_d[bass.ds(i * 2, 2)].rearrange("b l d -> (b l) d"), x1[:]).then_inc(S["stored"], 16)

        step(0)
        with sp.Fori(1, PAIRS) as i:
            step(i)
        sp.wait_ge(S["stored"], 16 * PAIRS)

    def half_blocks(eng, i, k):
        for s in range(2):
            m = eng.tensor_tensor(kblk[:, k, s], bc(head8, [P, 8, L]),
                                  fk[:, k, bass.ds(i * P + s * L, L)].unsqueeze(1).broadcast_to([P, 8, L]), ALU.mult)
        m.then_inc(S["kblk_set"], 1)

    @block.gpsimd
    def _(pool):
        def stage(i):
            pool.wait_ge(S["s_ps"], i)
            for k in range(KT):
                for s in range(2):
                    m = pool.tensor_tensor(rq[:, k, s, 0:8 * REG].rearrange("p (h r) -> p h r", r=REG), bc(head8, [P, 8, REG]),
                                           fq[:, k, bass.ds(i * P + s * L, REG)].unsqueeze(1).broadcast_to([P, 8, REG]), ALU.mult)
            m.then_inc(S["rq_set"], 1)
            half_blocks(pool, i, 1)

        def normalise(i):
            pool.wait_ge(S["inv_done"], i + 1)
            pool.wait_ge(S["pT_ps"], i * 3)
            pool.tensor_tensor(pkey[:], prob[:], bc(sm[:], [P, NSLOT, L]), ALU.mult).then_inc(S["prob_done"], 1)

        def residual(i):
            pool.wait_ge(S["x_loaded"], i * 16 + 16)
            pool.wait_ge(S["x1_done"], i)
            pool.tensor_tensor(xb[:], xrow[:], bp[:], ALU.add).then_inc(S["xb_done"], 1)

        pool.memset(rq[:], 0.0).then_inc(S["pads"], 1)
        pool.memset(vblk[:], 0.0).then_inc(S["pads"], 1)
        pool.wait_ge(S["pads"], 2)
        pool.wait_ge(S["w_loaded"], 32)
        stage(0)
        stage(1)
        normalise(0)

        def step(i, last=False):
            if not last:
                stage(i + 2)
            residual(i)
            normalise(i + 1)

        step(0)
        step(1)
        with pool.Fori(2, PAIRS - 2) as i:
            step(i)
        step(PAIRS - 2, True)
        residual(PAIRS - 1)

    @block.tensor
    def _(pe):
        def scores(i):
            pe.wait_ge(S["sub_done"], i)
            for n in range(2):
                pe.matmul(score[:, n], ident_h[:], key_bias[:, bass.ds(i, 1)].broadcast_to([P, 8, L]), start=True, stop=True)
            pe.matmul(score[:, 2, 0:2 * L], ident_h[:], reg_bias[:, bass.ds(i, 1)].rearrange("p a q b -> p (a q b)"), start=True, stop=True)
            pe.wait_ge(S["rq_set"], i + 1)
            pe.wait_ge(S["k_set"], i + 1)
            for k in range(KT):
                for s in range(2):
                    pe.matmul(score[64 * k:64 * k + 64, 2, s * L:(s + 1) * L], rq[:, k, s], kp[:, k, s * L:(s + 1) * L],
                              start=False, stop=True, skip_group_check=True)
            pe.wait_ge(S["kblk_set"], i * 2 + 2)
            pe.wait_ge(S["q_set"], i + 1)
            for k in range(KT):
                for s in range(2):
                    m = pe.matmul(score[64 * s:64 * s + 64, k], q[:, k, s * L:(s + 1) * L],
                                  kblk[:, k, s].rearrange("p h n -> p (h n)"), start=False, stop=True, skip_group_check=True)
            m.then_inc(S["s_ps"], 1)

        def transposed(i):
            pe.wait_ge(S["prob_done"], i + 1)
            pe.wait_ge(S["rmul_done"], i)
            pe.wait_ge(S["pT_done"], i * 3)
            for n in range(NSLOT // 2):
                out = (pt[0], pt[1], pr)[n // 4]
                m = pe.transpose(out[:, (n % 4) * P:(n % 4 + 1) * P], pkey[:, 2 * n:2 * n + 2].rearrange("p a k -> p (a k)"), ident)
                if n in (3, 7, 8):
                    m.then_inc(S["pT_ps"], 1)

        def weigh(i):
            pe.wait_ge(S["pT_done"], i * 3 + 3)
            pe.wait_ge(S["vblk_set"], i + 1)
            pe.wait_ge(S["o_done"], i)
            for s in range(2):
                for p in range(8):
                    r = 32 * (p % 4)
                    m = pe.matmul(po[r:r + 32, (p // 4) * P + s * L:(p // 4) * P + (s + 1) * L], vblk[:, s, p],
                                  probT[:, p, s * L:(s + 1) * L], start=True, stop=True, tile_position=(0, r))
            m.then_inc(S["o_ps"], 1)
            for k in range(KT):
                for s in range(2):
                    out = (pr[:, 0:KT * L], pt[0][:, 0:KT * L])[s]
                    m = pe.matmul(out[:, k * L:(k + 1) * L], v[64 * s:64 * s + 64, k * P:(k + 1) * P],
                                  probT[64 * s:64 * s + 64, 8, k * L:(k + 1) * L], start=True, stop=True)
            m.then_inc(S["r_ps"], 1)

        def projected(i):
            pe.wait_ge(S["reg_done"], i + 1)
            pe.wait_ge(S["x1T_done"], i)
            for k in range(KT):
                m = pe.matmul(px[:, 0:D], oT[:, k], wp[:, k], start=(k == 0), stop=(k == KT - 1))
            m.then_inc(S["x_ps"], 1)

        def turned(i):
            pe.wait_ge(S["x1_done"], i + 1)
            for k in range(KT):
                m = pe.transpose(px[:, k * P:(k + 1) * P], x1[:, k * P:(k + 1) * P], ident)
            m.then_inc(S["x1T_ps"], 1)

        pe.wait_ge(S["w_loaded"], 32)
        scores(0)
        scores(1)

        def step(i, first=False, last=False):
            transposed(i)
            if not first:
                turned(i - 1)
            weigh(i)
            if not last:
                scores(i + 2)
            projected(i)

        step(0, first=True)
        step(1)
        with pe.Fori(2, PAIRS - 2) as i:
            step(i)
        step(PAIRS - 2, last=True)
        step(PAIRS - 1, last=True)
        turned(PAIRS - 1)

    @block.vector
    def _(dve):
        def blocks(i):
            dve.wait_ge(S["s_ps"], i)
            half_blocks(dve, i, 0)

        def softmax_max(i):
            dve.wait_ge(S["s_ps"], i + 1)
            dve.tensor_reduce(mx[:], sflat, X, ALU.max).then_inc(S["max_done"], 1)

        def softmax_sub(i):
            dve.wait_ge(S["max_done"], i + 1)
            dve.wait_ge(S["prob_done"], i)
            dve.tensor_tensor(prob[:], sflat, bc(mx[:], [P, NSLOT, L]), ALU.subtract).then_inc(S["sub_done"], 1)

        def softmax_sum(i):
            dve.wait_ge(S["exp_done"], i + 1)
            dve.tensor_reduce(sm[:], prob[:], X, ALU.add).then_inc(S["sum_done"], 1)
            dve.wait_ge(S["sum_done"], i + 1)
            dve.reciprocal(sm[:], sm[:]).then_inc(S["inv_done"], 1)

        def registers(i):
            dve.wait_ge(S["r_ps"], i + 1)
            for s, src in enumerate((pr[:, 0:KT * L], pt[0][:, 0:KT * L])):
                for k in range(KT):
                    m = dve.tensor_tensor(regh[:, 2 * k + s], src[:, k * L:k * L + 8 * REG].rearrange("p (h r) -> p h r", r=REG),
                                          bc(head8, [P, 8, REG]), ALU.mult)
            m.then_inc(S["rmul_done"], 1)
            dve.wait_ge(S["rmul_done"], i + 1)
            dve.tensor_reduce(reg[:].rearrange("p k s r -> p (k s) r"), regh[:].rearrange("p n h r -> p n r h"), X,
                              ALU.add).then_inc(S["rsum_done"], 1)
            dve.wait_ge(S["rsum_done"], i + 1)
            dve.wait_ge(S["o_done"], i + 1)
            o = oT[:].rearrange("p k (s n) -> p k s n", s=2)[:, :, :, 0:REG]
            dve.tensor_tensor(reg[:], reg[:], o, ALU.add).then_inc(S["radd_done"], 1)
            dve.wait_ge(S["radd_done"], i + 1)
            dve.tensor_scalar(o, reg[:], 0.5, None, ALU.mult).then_inc(S["reg_done"], 1)

        def residual(i):
            dve.wait_ge(S["x_ps"], i + 1)
            dve.wait_ge(S["xb_done"], i + 1)
            dve.wait_ge(S["x1T_ps"], i)
            dve.wait_ge(S["stored"], i * 16)
            dve.tensor_tensor(x1[:], px[:, 0:D], xb[:], ALU.add).then_inc(S["x1_done"], 1)

        blocks(0)
        softmax_max(0)
        softmax_sub(0)
        blocks(1)
        softmax_sum(0)

        def step(i, first=False, last=False):
            softmax_max(i + 1)
            if not first:
                residual(i - 1)
            softmax_sub(i + 1)
            if not last:
                blocks(i + 2)
            softmax_sum(i + 1)
            registers(i)

        step(0, first=True)
        step(1)
        with dve.Fori(2, PAIRS - 2) as i:
            step(i)
        step(PAIRS - 2, last=True)
        residual(PAIRS - 2)
        registers(PAIRS - 1)
        residual(PAIRS - 1)

    @block.scalar
    def _(act):
        def exps(i):
            act.wait_ge(S["sub_done"], i + 1)
            act.activation(prob[:], prob[:], ACT.Exp, scale=HD1 ** -0.5).then_inc(S["exp_done"], 1)

        def queries(i):
            act.wait_ge(S["s_ps"], i)
            act.copy(kp[:], fk[:, :, bass.ds(i * P, P)]).then_inc(S["k_set"], 1)
            act.copy(q[:], fq[:, :, bass.ds(i * P, P)]).then_inc(S["q_set"], 1)

        def stage_v(i):
            act.wait_ge(S["r_ps"], i)
            act.copy(v[:], fv[:, bass.ds(i, 1)].rearrange("p a b -> p (a b)")).then_inc(S["v_set"], 1)

        def values(i):
            act.wait_ge(S["v_set"], i + 1)
            for s in range(2):
                src = v[64 * s:64 * s + 64].rearrange("p (n a d) -> p n a d", a=2, d=HD1)
                for a in range(2):
                    m = act.copy(vblk[64 * a:64 * a + 64, s, :, a * HD1:(a + 1) * HD1], src[:, :, a])
            m.then_inc(S["vblk_set"], 1)

        def weights(i):
            for n in range(3):
                act.wait_ge(S["pT_ps"], i * 3 + n + 1)
                w = 4 if n < 2 else 1
                act.copy(probT[:, 4 * n:4 * n + w].rearrange("p m n -> p (m n)"),
                         (pt[0], pt[1], pr)[n][:, 0:w * P]).then_inc(S["pT_done"], 1)

        def out(i):
            act.wait_ge(S["o_ps"], i + 1)
            act.wait_ge(S["x_ps"], i)
            act.copy(oT[:].rearrange("p k n -> p (k n)"), po[:, 0:KT * P]).then_inc(S["o_done"], 1)

        def turned(i):
            act.wait_ge(S["x1T_ps"], i + 1)
            for k in range(KT):
                m = act.copy(x1T[:, k, :, bass.ds(i * 2, 2)].rearrange("p t s -> p s t"),
                             px[:, k * P:(k + 1) * P].rearrange("p (s t) -> p s t", s=2))
            m.then_inc(S["x1T_done"], 1)

        act.wait_ge(S["pads"], 2)
        queries(0)
        stage_v(0)
        values(0)
        queries(1)
        exps(0)

        def step(i, first=False, last=False):
            if not last:
                queries(i + 2)
            weights(i)
            exps(i + 1)
            if not first:
                turned(i - 1)
            out(i)
            stage_v(i + 1)
            values(i + 1)

        step(0, first=True)
        step(1)
        with act.Fori(2, PAIRS - 2) as i:
            step(i)
        step(PAIRS - 2, last=True)
        weights(PAIRS - 1)
        turned(PAIRS - 2)
        out(PAIRS - 1)
        turned(PAIRS - 1)


def recurrence(nc, c, sbuf, sem, t, const, ident, x1T, h_rows, logits, ytab_d, ew1, ew2, eb1, e_loaded):
    wx, wh = sbuf(c, "wx", [P, KT, D]), sbuf(c, "wh", [P, KT, D])
    b, ob1 = sbuf(c, "rb", [P, KT]), sbuf(c, "ob1", [P, FT])
    ow1, ow2 = sbuf(c, "ow1", [P, KT, HID]), sbuf(c, "ow2", [P, FT, D])
    rw = sbuf(c, "rw", [P, KT, E])
    rbias, ob2 = sbuf(c, "rbias", [P, E]), sbuf(c, "ob2", [P, D])
    cond = sbuf(c, "rcond", [B, D])
    h = [sbuf(c, f"h{u}", [P, KT, 2 * B]) for u in range(2)]
    hid = sbuf(c, "ohid", [P, FT, P])
    hid_hi, hid_lo = sbuf(c, "ohid_hi", [P, FT, P], F32R), sbuf(c, "ohid_lo", [P, FT, P], F32R)
    ow2_hi, ow2_lo = sbuf(c, "ow2_hi", [P, FT, D], F32R), sbuf(c, "ow2_lo", [P, FT, D], F32R)
    y = sbuf(c, "oy", [P, D])
    ph = [[c.enter_context(nc.psum_tensor(f"ph{u}{m}", [P, 512], F32)) for m in range(KT)] for u in range(2)]
    pm = [c.enter_context(nc.psum_tensor(f"pm{n}", [P, 512], F32)) for n in range(2)]
    py = c.enter_context(nc.psum_tensor("py", [P, 512], F32))
    pr = c.enter_context(nc.psum_tensor("prow", [P, 512], F32))
    names = ("loaded condT_ps h0_done h_ps h_done hid_ps hid_done hi_done lo_done ow2_hi_done ow2_lo_done y_ps y_done stored row_ps row_done logit_done")
    S = {n: sem(c, "r_" + n) for n in names.split()}
    block = c.enter_context(nc.Block())
    ytok = ytab_d[XROWS:].rearrange("(j p) d -> j p d", p=P)

    @block.sync
    def _(sp):
        loads = [
            (cond[:], t["cond_1024"]), (wx[:], t["L1_cond_Wx"].rearrange("(k p) n -> p k n", p=P)),
            (wh[:], t["L1_cond_Wh"].rearrange("(k p) n -> p k n", p=P)),
            (b[:], t["L1_cond_b"].rearrange("(m p) -> p m", p=P)),
            (ob1[:], t["L1_ffn_ob1"].rearrange("(m p) -> p m", p=P)),
            (rw[:], t["L1_ffn_router_w"].rearrange("(k p) n -> p k n", p=P)),
            (rbias[:], t["L1_ffn_router_b"].partition_broadcast(P)), (ob2[:], t["L1_ffn_ob2"].partition_broadcast(P)),
            (ow1[:], t["L1_ffn_ow1"].rearrange("(k p) n -> p k n", p=P)),
            (ow2[:], t["L1_ffn_ow2"].rearrange("(k p) n -> p k n", p=P)),
        ]
        for dst, src in loads:
            with nc.allow_non_contiguous_dma(reason="bias columns"):
                sp.dma_start(dst, src).then_inc(S["loaded"], 16)
        for e in range(2):
            load_expert(nc, sp, t, e, ew1[e], ew2[e], eb1[e], e_loaded[e])
        with sp.Fori(0, STEPS2) as j:
            sp.wait_ge(S["y_done"], j + 1)
            sp.dma_start(ytok[bass.ds(j, 1)].rearrange("a p d -> p (a d)"), y[:]).then_inc(S["stored"], 16)
        sp.wait_ge(S["stored"], 16 * STEPS2)

    @block.tensor
    def _(pe):
        def inputs(j, u):
            for m in range(KT):
                for k in range(KT):
                    pe.matmul(ph[u][m][:, 0:P], wx[:, k, m * P:(m + 1) * P],
                              x1T[:, k, bass.ds(j * 2, 2)].rearrange("p t b -> p (t b)"),
                              start=(k == 0), stop=(k == KT - 1), skip_group_check=True)

        def step(j, u, par, first=False):
            src, o = (h[1 - u], B) if par == 0 else (h[u], 0)
            if first:
                pe.wait_ge(S["h0_done"], 1)
            else:
                pe.wait_ge(S["h_done"], j * 4 + 2 * par)
            for k in range(KT):
                for m in range(KT):
                    ins = pe.matmul(ph[u][m][:, par * B:(par + 1) * B], wh[:, k, m * P:(m + 1) * P], src[:, k, o:o + B],
                                    start=False, stop=True, skip_group_check=True)
                    if k == KT - 1:
                        ins.then_inc(S["h_ps"], 1)

        def mlp_up(j, u):
            pe.wait_ge(S["h_done"], j * 4 + 4)
            pe.wait_ge(S["hid_done"], j * 8)
            for half in range(2):
                for n in range(4):
                    for k in range(KT):
                        f = 4 * half + n
                        m = pe.matmul(pm[half][:, n * P:(n + 1) * P], ow1[:, k, f * P:(f + 1) * P], h[u][:, k],
                                      start=(k == 0), stop=(k == KT - 1))
                m.then_inc(S["hid_ps"], 1)

        def rows_and_logits(j, u):
            pe.wait_ge(S["row_done"], j)
            pe.wait_ge(S["logit_done"], j)
            for k in range(KT):
                m = pe.transpose(pr[:, k * P:(k + 1) * P], h[u][:, k], ident)
            for k in range(KT):
                m = pe.matmul(pr[:, D:D + E], h[u][:, k], rw[:, k], start=(k == 0), stop=(k == KT - 1))
            m.then_inc(S["row_ps"], 1)

        def mlp_down(j):
            pe.wait_ge(S["y_done"], j)
            pe.wait_ge(S["hi_done"], j + 1)
            pe.wait_ge(S["lo_done"], j + 1)
            for f in range(FT):
                pe.matmul(py[:, 0:D], hid_lo[:, f], ow2_hi[:, f], start=(f == 0), stop=False)
                pe.matmul(py[:, 0:D], hid_hi[:, f], ow2_lo[:, f], start=False, stop=False)
                m = pe.matmul(py[:, 0:D], hid_hi[:, f], ow2_hi[:, f], start=False, stop=(f == FT - 1))
            m.then_inc(S["y_ps"], 1)

        pe.wait_ge(S["loaded"], 160)
        pe.wait_ge(S["ow2_lo_done"], 1)
        for k in range(KT):
            m = pe.transpose(py[:, k * B:(k + 1) * B], cond[:, k * P:(k + 1) * P], ident[0:B, 0:B])
        m.then_inc(S["condT_ps"], 1)
        inputs(0, 0)
        step(0, 0, 0, True)
        step(0, 0, 1)

        def pair(j, u, first=False):
            inputs(j, u)
            step(j, u, 0)
            mlp_up(j - 1, 1 - u)
            step(j, u, 1)
            rows_and_logits(j - 1, 1 - u)
            if not first:
                mlp_down(j - 2)

        pair(1, 1, True)
        with pe.Fori(1, STEPS2 // 2) as n:
            for u in range(2):
                pair(n * 2 + u, u)
        mlp_up(STEPS2 - 1, 1)
        rows_and_logits(STEPS2 - 1, 1)
        mlp_down(STEPS2 - 2)
        mlp_down(STEPS2 - 1)

    @block.scalar
    def _(act):
        act.wait_ge(S["loaded"], 160)
        act.copy(ow2_hi[:], ow2[:]).then_inc(S["ow2_hi_done"], 1)
        act.wait_ge(S["condT_ps"], 1)
        act.copy(h[1][:, :, B:], py[:, 0:KT * B].rearrange("p (k b) -> p k b", b=B)).then_inc(S["h0_done"], 1)
        def split(j):
            act.wait_ge(S["hid_done"], j * 8 + 8)
            act.wait_ge(S["y_ps"], j)
            act.copy(hid_hi[:], hid[:]).then_inc(S["hi_done"], 1)

        def tanh(n, u):
            for par in range(2):
                for m in range(KT):
                    act.wait_ge(S["h_ps"], n * 8 + (4 * u + 2 * par + m + 1))
                    act.activation(h[u][:, m, par * B:(par + 1) * B], ph[u][m][:, par * B:(par + 1) * B], ACT.Tanh,
                                   bias=b[:, m:m + 1]).then_inc(S["h_done"], 1)

        tanh(0, 0)
        tanh(0, 1)
        split(0)
        with act.Fori(1, STEPS2 // 2) as n:
            for u in range(2):
                tanh(n, u)
                split(n * 2 + u - 1)
        split(STEPS2 - 1)

    @block.vector
    def _(dve):
        dve.wait_ge(S["ow2_hi_done"], 1)
        dve.tensor_tensor(ow2_lo[:], ow2[:], ow2_hi[:].bitcast(F32), ALU.subtract).then_inc(S["ow2_lo_done"], 1)

        def two_steps(j):
            dve.wait_ge(S["lo_done"], j)
            for half in range(2):
                dve.wait_ge(S["hid_ps"], j * 2 + half + 1)
                for n in range(4):
                    f = 4 * half + n
                    dve.tensor_scalar(hid[:, f], pm[half][:, n * P:(n + 1) * P], ob1[:, f:f + 1], 0.0,
                                      ALU.add, ALU.max).then_inc(S["hid_done"], 1)
            dve.wait_ge(S["row_ps"], j + 1)
            dve.tensor_copy(h_rows[:, bass.ds(j, 1)].rearrange("p a d -> p (a d)"), pr[:, 0:D]).then_inc(S["row_done"], 1)
            dve.tensor_tensor(logits[:, bass.ds(j, 1)].rearrange("p a e -> p (a e)"), pr[:, D:D + E], rbias[:],
                              ALU.add).then_inc(S["logit_done"], 1)

        def low(j):
            dve.wait_ge(S["y_ps"], j)
            dve.wait_ge(S["hi_done"], j + 1)
            dve.tensor_tensor(hid_lo[:], hid[:], hid_hi[:].bitcast(F32), ALU.subtract).then_inc(S["lo_done"], 1)

        def out(j):
            dve.wait_ge(S["y_ps"], j + 1)
            dve.wait_ge(S["stored"], j * 16)
            dve.tensor_tensor(y[:], py[:, 0:D], ob2[:], ALU.add).then_inc(S["y_done"], 1)

        two_steps(0)
        low(0)
        with dve.Fori(1, STEPS2) as j:
            two_steps(j)
            out(j - 1)
            low(j)
        out(STEPS2 - 1)


def load_expert(nc, eng, t, e, w1, w2, b1, loaded):
    eng.dma_start(w1, t["L1_ffn_w1"][bass.ds(e, 1)].rearrange("a (k p) n -> p (a k) n", p=P)).then_inc(loaded, 16)
    eng.dma_start(w2, t["L1_ffn_w2"][bass.ds(e, 1)].rearrange("a (k p) n -> p (a k) n", p=P)).then_inc(loaded, 16)
    with nc.allow_non_contiguous_dma(reason="bias columns"):
        eng.dma_start(b1[:], t["L1_ffn_b1"][bass.ds(e, 1)].rearrange("a (m p) -> p (a m)", p=P)).then_inc(loaded, 16)


def experts(nc, c, sbuf, sem, t, const, ident, h_rows, logits, x1_d, xtab_d, ytab_d, ew1, ew2, eb1, e_loaded):
    big = [P, STEPS2, E]
    eq, cand, hot, count, rank = (sbuf(c, n, big) for n in ("eq", "cand", "hot", "count", "rank"))
    top, eid, pos, ok, slot, gap = (sbuf(c, n, [P, STEPS2]) for n in ("top", "eid", "pos", "ok", "slot", "gap"))
    ones = sbuf(c, "ones", [P, STEPS2])
    idx = sbuf(c, "idx", [P, STEPS2], U32)
    b2 = sbuf(c, "b2", [P, E, D])
    xe = [sbuf(c, f"xe{u}", [P, 3, D]) for u in range(2)]
    xeT = sbuf(c, "xeT", [P, KT, CAP])
    hT = sbuf(c, "ehT", [P, FT, CAP])
    ye = [sbuf(c, f"ye{u}", [P, 3, D]) for u in range(2)]
    got = [sbuf(c, f"got{u}", [P, 4, D]) for u in range(2)]
    res = [sbuf(c, f"res{u}", [P, 4, D]) for u in range(2)]
    pxT = c.enter_context(nc.psum_tensor("pxT", [P, KT, 512], F32))
    phid = [c.enter_context(nc.psum_tensor(f"phid{n}", [P, 512], F32)) for n in range(4)]
    pyo = [c.enter_context(nc.psum_tensor(f"pyo{n}", [P, 512], F32)) for n in range(2)]
    names = "b2_loaded hot_done rank_ps idx_done scattered xT_ps xT_done hid_ps hid_act hid_dve y_ps y_done"
    S = {n: sem(c, "e_" + n) for n in names.split()}
    step = sem(c, "e_step")
    x_loaded = [sem(c, f"e_x_loaded{u}") for u in range(2)]
    y_stored = [sem(c, f"e_y_stored{u}") for u in range(2)]
    res_loaded = [sem(c, f"e_res_loaded{u}") for u in range(2)]
    gathered = [sem(c, f"e_gathered{u}") for u in range(2)]
    out_stored = [sem(c, f"e_out_stored{u}") for u in range(2)]
    summed = sem(c, "e_summed")
    block = c.enter_context(nc.Block())
    GROUPS = STEPS2 // 4

    def by_parity(ap, g, par):
        return ap.rearrange("b (j r) d -> b j r d", r=2)[:, bass.ds(g * 4, 4), par]

    @block.sync
    def _(sp):
        sp.dma_start(b2[:].rearrange("p e d -> p (e d)"),
                     t["L1_ffn_b2"].rearrange("e d -> (e d)").partition_broadcast(P)).then_inc(S["b2_loaded"], 16)
        sp.wait_ge(S["scattered"], 16 * STEPS2)

        def load_rows(e, u):
            sp.dma_start(xe[u][:, 0:2], xtab_d[bass.ds(e * CAP, 2 * P)].rearrange("(n p) d -> p n d", p=P)).then_inc(x_loaded[u], 16)
            sp.dma_start(xe[u][0:64, 2], xtab_d[bass.ds(e * CAP + 2 * P, 64)]).then_inc(x_loaded[u], 16)

        def store(e, u):
            sp.wait_ge(S["y_done"], e * 3 + 3)
            sp.dma_start(ytab_d[bass.ds(e * CAP, 2 * P)].rearrange("(n p) d -> p n d", p=P), ye[u][:, 0:2]).then_inc(y_stored[u], 16)
            sp.dma_start(ytab_d[bass.ds(e * CAP + 2 * P, 64)], ye[u][0:64, 2]).then_inc(y_stored[u], 16)

        for u in range(2):
            load_rows(u, u)
        for u in range(2):
            for par in range(2):
                sp.dma_start(res[u][64 * par:64 * par + 64], by_parity(x1_d, u, par)).then_inc(res_loaded[u], 16)
        with sp.Fori(0, E // 2 - 1) as n:
            for u in range(2):
                e = n * 2 + u
                store(e, u)
                load_rows(e + 2, u)
                load_expert(nc, sp, t, e + 2, ew1[u], ew2[u], eb1[u], e_loaded[u])
        for u in range(2):
            store(E - 2 + u, u)
        with sp.Fori(0, GROUPS // 2 - 1) as n:
            for u in range(2):
                g = n * 2 + u
                sp.wait_ge(summed, g + 1)
                for par in range(2):
                    sp.dma_start(by_parity(t["out"], g, par), got[u][64 * par:64 * par + 64]).then_inc(out_stored[u], 16)
                for par in range(2):
                    sp.dma_start(res[u][64 * par:64 * par + 64], by_parity(x1_d, g + 2, par)).then_inc(res_loaded[u], 16)
        for u in range(2):
            g = GROUPS - 2 + u
            sp.wait_ge(summed, g + 1)
            for par in range(2):
                sp.dma_start(by_parity(t["out"], g, par), got[u][64 * par:64 * par + 64]).then_inc(out_stored[u], 16)
        for u in range(2):
            sp.wait_ge(out_stored[u], 32 * (GROUPS // 2))

    @block.gpsimd
    def _(pool):
        pool.wait_ge(S["idx_done"], 1)
        for j in range(STEPS2):
            pool.indirect_dma_start(xtab_d, bass.IndirectOffsetOnAxis(idx[:, j:j + 1], 0), h_rows[:, j], None).then_inc(S["scattered"], 16)
        for u in range(2):
            pool.wait_ge(y_stored[u], 32 * E // 2)
        for g in range(GROUPS):
            u = g % 2
            pool.wait_ge(out_stored[u], g // 2 * 32)
            for i in range(4):
                pool.indirect_dma_start(got[u][:, i], None, ytab_d,
                                        bass.IndirectOffsetOnAxis(idx[:, g * 4 + i:g * 4 + i + 1], 0)).then_inc(gathered[u], 16)

    @block.tensor
    def _(pe):
        pe.wait_ge(S["hot_done"], 1)
        flat = "p j e -> p (j e)"
        pe.matmul(pxT[:, 0, 0:STEPS2 * E], const("same_b"), count[:].rearrange(flat), start=True, stop=False)
        pe.matmul(pxT[:, 0, 0:STEPS2 * E], const("drop"), hot[:].rearrange(flat), start=False, stop=False)
        pe.matmul(pxT[:, 0, 0:STEPS2 * E], const("before"),
                  count[:, STEPS2 - 1].unsqueeze(1).broadcast_to(big), start=False, stop=True).then_inc(S["rank_ps"], 1)
        pe.wait_ge(S["idx_done"], 1)

        def turn(e, n, u):
            pe.wait_ge(x_loaded[u], n * 32 + 32)
            pe.wait_ge(S["xT_done"], e)
            for k in range(KT):
                for i, (o, w) in enumerate(CAPT):
                    m = pe.transpose(pxT[:, k, o:o + w], xe[u][0:w, i, k * P:(k + 1) * P], ident[0:w, 0:w])
            m.then_inc(S["xT_ps"], 1)

        def up(e, n, u):
            pe.wait_ge(S["xT_done"], e + 1)
            pe.wait_ge(e_loaded[u], n * 48 + 48)
            for f in range(FT):
                pe.wait_ge(S["hid_act"] if f % 2 == 0 else S["hid_dve"], e * 4 + max(f // 2 - 1, 0))
                for k in range(KT):
                    m = pe.matmul(phid[f % 4][:, 0:CAP], ew1[u][:, k, f * P:(f + 1) * P], xeT[:, k], start=(k == 0), stop=(k == KT - 1))
                m.then_inc(S["hid_ps"], 1)

        def down(e, u):
            pe.wait_ge(S["hid_act"], e * 4 + 4)
            pe.wait_ge(S["hid_dve"], e * 4 + 4)
            for i, (o, w) in enumerate(CAPT):
                pe.wait_ge(S["y_done"], e * 3 + max(i - 1, 0))
                for f in range(FT):
                    m = pe.matmul(pyo[0 if i != 1 else 1][0:w, 0:D], hT[:, f, o:o + w], ew2[u][:, f], start=(f == 0), stop=(f == FT - 1))
                m.then_inc(S["y_ps"], 1)

        turn(0, 0, 0)
        def two(n):
            for u in range(2):
                up(n * 2 + u, n, u)
                turn(n * 2 + u + 1, n + u, 1 - u)
                down(n * 2 + u, u)

        two(0)
        with pe.Fori(1, E // 2 - 1) as n:
            two(n)
        up(E - 2, E // 2 - 1, 0)
        turn(E - 1, E // 2 - 1, 1)
        down(E - 2, 0)
        up(E - 1, E // 2 - 1, 1)
        down(E - 1, 1)

    @block.scalar
    def _(act):
        def two(n):
            for u in range(2):
                e = n * 2 + u
                act.wait_ge(S["xT_ps"], e + 1)
                act.wait_ge(S["hid_ps"], e * FT)
                act.copy(xeT[:], pxT[:, :, 0:CAP]).then_inc(S["xT_done"], 1)
                for f in range(0, FT, 2):
                    act.wait_ge(S["hid_ps"], e * FT + (f + 1))
                    act.activation(hT[:, f], phid[f % 4][:, 0:CAP], ACT.Relu, bias=eb1[u][:, f:f + 1]).then_inc(S["hid_act"], 1)

        two(0)
        with act.Fori(1, E // 2) as n:
            two(n)

    @block.vector
    def _(dve):
        done = 0

        def then(ins):
            nonlocal done
            done += 1
            ins.then_inc(step, 1)
            dve.wait_ge(step, done)

        e_minus = const("e_minus").unsqueeze(1).broadcast_to(big)
        dve.memset(ones[:], 1.0)
        then(dve.tensor_reduce(top[:], logits[:], X, ALU.max))
        then(dve.tensor_tensor(eq[:], logits[:], bc(top[:], big), ALU.is_equal))
        then(dve.tensor_tensor(cand[:], eq[:], e_minus, ALU.mult))
        then(dve.tensor_reduce(eid[:], cand[:], X, ALU.min))
        then(dve.tensor_tensor(hot[:], e_minus, bc(eid[:], big), ALU.is_equal))
        for n in range(E):
            m = dve.tensor_tensor_scan(count[:, :, n], ones[:], hot[:, :, n], 0.0, ALU.mult, ALU.add)
        m.then_inc(S["hot_done"], 1)
        dve.wait_ge(S["rank_ps"], 1)
        then(dve.tensor_tensor(rank[:], hot[:], pxT[:, 0, 0:STEPS2 * E].rearrange("p (j e) -> p j e", e=E), ALU.mult))
        then(dve.tensor_reduce(pos[:], rank[:], X, ALU.add))
        then(dve.tensor_scalar(ok[:], pos[:], float(CAP), None, ALU.is_lt))
        then(dve.tensor_scalar(slot[:], eid[:], float(E), float(CAP), ALU.add, ALU.mult))
        then(dve.tensor_tensor(slot[:], slot[:], pos[:], ALU.add))
        then(dve.tensor_tensor(gap[:], slot[:], const("own"), ALU.subtract))
        then(dve.tensor_tensor(gap[:], gap[:], ok[:], ALU.mult))
        dve.tensor_tensor(idx[:], gap[:], const("own"), ALU.add).then_inc(S["idx_done"], 1)
        dve.wait_ge(S["b2_loaded"], 16)

        def two(n):
            for u in range(2):
                e = n * 2 + u
                for f in range(1, FT, 2):
                    dve.wait_ge(S["hid_ps"], e * FT + (f + 1))
                    dve.tensor_scalar(hT[:, f], phid[f % 4][:, 0:CAP], eb1[u][:, f:f + 1], 0.0, ALU.add, ALU.max).then_inc(S["hid_dve"], 1)
                for i, (o, w) in enumerate(CAPT):
                    dve.wait_ge(S["y_ps"], e * 3 + (i + 1))
                    dve.wait_ge(y_stored[u], n * 32)
                    dve.tensor_tensor(ye[u][0:w, i], pyo[0 if i != 1 else 1][0:w, 0:D],
                                      b2[0:w, bass.ds(e, 1)].rearrange("p a d -> p (a d)"), ALU.add).then_inc(S["y_done"], 1)

        two(0)
        with dve.Fori(1, E // 2) as n:
            two(n)
        with dve.Fori(0, GROUPS // 2) as n:
            for u in range(2):
                dve.wait_ge(gathered[u], n * 64 + 64)
                dve.wait_ge(res_loaded[u], n * 32 + 32)
                dve.tensor_tensor(got[u][:], got[u][:], res[u][:], ALU.add).then_inc(summed, 1)


_NAMES = ["x", "cond_1024", "L0_cond_WQ_w", "L0_cond_WQ_b", "L0_cond_WK_w", "L0_cond_WK_b", "L0_cond_WV_w",
          "L0_cond_WV_b", "L0_cond_WO_w", "L0_cond_WO_b", "L0_ffn_g_info", "L0_ffn_W_qkv", "L0_ffn_W_proj",
          "L0_ffn_b_proj", "L1_cond_Wx", "L1_cond_Wh", "L1_cond_b", "L1_ffn_router_w", "L1_ffn_router_b", "L1_ffn_w1",
          "L1_ffn_b1", "L1_ffn_w2", "L1_ffn_b2", "L1_ffn_ow1", "L1_ffn_ob1", "L1_ffn_ow2", "L1_ffn_ob2"]


def kernel(**inputs):
    import concourse.bacc as bacc
    from concourse.bass_utils import run_bass_kernel_spmd as run

    nc = bacc.Bacc("TRN2", target_bir_lowering=False, num_devices=1)
    arrays, tensors = {}, {}
    table, const_at = shape_constants()
    given = {n: np.ascontiguousarray(inputs[n]) for n in _NAMES}
    given["consts"] = table
    for name, a in given.items():
        arrays["in_" + name] = a
        tensors[name] = nc.dram_tensor("in_" + name, a.shape, mybir.dt.from_np(a.dtype), kind="ExternalInput").ap()
    tensors["out"] = nc.dram_tensor("out_0", (B, L, D), F32, kind="ExternalOutput").ap()
    build(nc, tensors, const_at)
    return run(nc, [arrays], core_ids=[0]).results[0]["out_0"]
```

```python
from contextlib import ExitStack

import numpy as np

import concourse.bass as bass
from concourse import mybir

ALU = mybir.AluOpType
ACT = mybir.ActivationFunctionType
F32 = mybir.dt.float32
F32R = mybir.dt.float32r
BF16 = mybir.dt.bfloat16
U32 = mybir.dt.uint32
X = mybir.AxisListType.X

P = 128
B, L, D = 64, 64, 256
KT = D // P
PAIRS = B // 2
H0, HD0 = 16, 64
HT = H0 * HD0 // P
H1, HD1 = 16, 16
REG = 5
W0 = L + 2
SPB = 4
NSLOT = H1 + 2
E, CAP, HID = 8, 320, 1024
FT = HID // P
STEPS2 = L // 2
LATE = 6
MAIN = STEPS2 - LATE
XROWS = E * CAP
NEG = -1.0e30
CAPT = [(0, 128), (128, 128), (256, 64)]


def shape_constants():
    p = np.arange(P)
    ident = np.eye(P, dtype=np.float32)
    band = np.full((P, 2, W0), NEG, np.float32)
    for q in range(P):
        for head, first, extra in ((0, 1, 0), (1, 0, L)):
            for j in (q % L - 1, q % L, q % L + 1):
                if 0 <= j < L:
                    band[q, head, first + j] = 0.0
            band[q, head, extra] = 0.0
            if q % L in (0, L - 1):
                band[q, head, L + 1] = 0.0
    band = band.reshape(P, -1)
    head8 = (p[:, None] // HD1 == np.arange(8)[None]).astype(np.float32)
    head16 = np.zeros((P, KT, H1), np.float32)
    for t in range(KT):
        head16[:, t, 8 * t:8 * t + 8] = head8
    same_head = (p[:, None] // HD1 == p[None] // HD1).astype(np.float32)
    same_seq = (p[:, None] // L == p[None] // L).astype(np.float32)
    key_diag = (p[:, None] % L == np.arange(L)[None]).astype(np.float32)
    tok_row = np.tile((np.arange(L) >= REG).astype(np.float32)[None], (P, 1))
    is_tok = ((p % L) >= REG).astype(np.float32)[:, None]
    par, b = p // B, p % B
    same_b = (b[:, None] == b[None]).astype(np.float32)
    drop = -same_b * ((par[:, None] == 1) | (par[None] == 0))
    before = (b[:, None] < b[None]).astype(np.float32)
    e_minus = np.tile(np.arange(E, dtype=np.float32)[None] - E, (P, 1))
    own = (XROWS + np.arange(STEPS2)[None] * P + p[:, None]).astype(np.float32)
    tok = (b[:, None] * L + par[:, None] + 2 * np.arange(STEPS2)[None]).astype(np.float32)
    free_id = (B * L + 4 * p[:, None] + np.arange(4)[None]).astype(np.float32)
    parts = dict(tok=tok, free_id=free_id, ident=ident, band=band, head8=head8, head16=head16.reshape(P, -1), same_head=same_head,
                 same_seq=same_seq, key_diag=key_diag, tok_row=tok_row, is_tok=is_tok, same_b=same_b,
                 drop=drop.astype(np.float32), before=before, e_minus=e_minus, own=own)
    at, cols = {}, 0
    for name, a in parts.items():
        at[name] = (cols, a.shape[1])
        cols += a.shape[1]
    return np.concatenate(list(parts.values()), 1), at


def bc(ap, shape):
    return ap.unsqueeze(len(ap.shape)).broadcast_to(shape)


def cut(room, at, shape):
    n = int(np.prod(shape))
    names = " ".join("abcd"[:len(shape)])
    return room[:, at:at + n].rearrange(f"p ({names}) -> p {names}", **dict(zip("abcd", shape)))


def build(nc, t, CONST_AT):
    with ExitStack() as outer:
        def sbuf(ctx, name, shape, dt=F32):
            return ctx.enter_context(nc.sbuf_tensor(name, shape, dt))

        def sem(ctx, name):
            return ctx.enter_context(nc.semaphore(name))

        consts = sbuf(outer, "consts", [P, sum(w for _, w in CONST_AT.values())])
        ident_h = sbuf(outer, "ident_h", [P, P], BF16)

        def const(name):
            o, w = CONST_AT[name]
            return consts[:, o:o + w]

        ident = const("ident")
        avw_d = nc.dram_tensor("avw_d", [B * H0, D], F32).ap()
        x1_d = nc.dram_tensor("x1_d", [B, L, D], F32).ap()
        xtab_d = nc.dram_tensor("xtab_d", [XROWS + B * L, D + 1], F32).ap()

        fq_room = sbuf(outer, "fq", [P, STEPS2 * (D + 1)])
        fq = fq_room[:, 0:KT * B * L].rearrange("p (k n) -> p k n", k=KT)
        fk = sbuf(outer, "fk", [P, KT, B * L])
        fv = sbuf(outer, "fv", [P, PAIRS, D])
        with ExitStack() as c:
            qgblk = sbuf(outer, "qgblk", [P, KT, H1])
            sims = sbuf(outer, "sims", [P, PAIRS, 2 * H1])
            star_pass(nc, c, sbuf, sem, t, const, ident, ident_h, consts, qgblk, fq, fk, fv, sims, avw_d, xtab_d)
        x1T = sbuf(outer, "x1T", [P, KT, L, B])
        room = sims[:].rearrange("p j h -> p (j h)")
        cond, wx = cut(room, 0, (D,))[0:B], cut(room, D, (KT, D))
        wh, ow1 = sbuf(outer, "wh", [P, KT, D]), sbuf(outer, "ow1", [P, KT, HID])
        b, rw = sbuf(outer, "rb", [P, KT]), sbuf(outer, "rw", [P, KT, E])
        start_loaded = sem(outer, "start_loaded")
        start = [(cond, t["cond_1024"]), (wx, t["L1_cond_Wx"].rearrange("(k p) n -> p k n", p=P)),
                 (wh[:], t["L1_cond_Wh"].rearrange("(k p) n -> p k n", p=P)),
                 (b[:], t["L1_cond_b"].rearrange("(m p) -> p m", p=P)),
                 (rw[:], t["L1_ffn_router_w"].rearrange("(k p) n -> p k n", p=P)),
                 (ow1[:], t["L1_ffn_ow1"].rearrange("(k p) n -> p k n", p=P))]
        with ExitStack() as l0:
            key_bias = sbuf(l0, "key_bias", [P, PAIRS, L], BF16)
            reg_bias = sbuf(l0, "reg_bias", [P, PAIRS, 2, L], BF16)
            with ExitStack() as c:
                classes(nc, c, sbuf, sem, const, ident, sims, key_bias, reg_bias)
            with ExitStack() as c:
                masked_pass(nc, c, sbuf, sem, t, const, ident, ident_h, fq, fk, fv, key_bias, reg_bias, x1T, x1_d,
                            start, start_loaded)
        h_rows = fq_room[:].rearrange("p (j d) -> p j d", d=D + 1)
        room = fk[:].rearrange("p k n -> p (k n)")
        ew1 = [room[:, u * 4096:u * 4096 + 2048].rearrange("p (k n) -> p k n", k=KT) for u in range(2)]
        ew2 = [room[:, u * 4096 + 2048:u * 4096 + 4096].rearrange("p (k n) -> p k n", k=FT) for u in range(2)]
        with ExitStack() as l1:
            logits = sbuf(l1, "logits", [P, STEPS2, E])
            eb1 = [sbuf(l1, f"eb1_{u}", [P, FT]) for u in range(2)]
            e_loaded = [sem(l1, f"e_loaded{u}") for u in range(2)]
            ob1 = sbuf(l1, "ob1", [P, FT])
            w2_parts = [sbuf(l1, f"w2_{n}", [P, FT, D], F32R) for n in ("hi", "lo")]
            hid_parts = [sbuf(l1, f"hid_{n}", [P, FT, CAP], F32R) for n in ("hi", "lo")]
            mlp = {n: sem(l1, "o_" + n) for n in "hid_ps hid_done hi_done lo_done y_ps y_done stored".split()}
            with ExitStack() as c:
                recurrence(nc, c, sbuf, sem, t, const, ident, cond, wx, wh, b, ow1, rw, start_loaded, x1T, h_rows, logits, x1_d, fv,
                           ob1, w2_parts, hid_parts, mlp, ew1, ew2, eb1, e_loaded)
            with ExitStack() as c:
                experts(nc, c, sbuf, sem, t, const, ident, h_rows, logits, x1_d, xtab_d, fv, x1T,
                        ob1, ow1, w2_parts, hid_parts, mlp,
                        ew1, ew2, eb1, e_loaded)


def star_pass(nc, c, sbuf, sem, t, const, ident, ident_h, consts, qgblk, fq, fk, fv, sims, avw_d, xtab_d):
    wq = sbuf(c, "wq", [P, KT, H0 * HD0])
    wk = sbuf(c, "wk", [P, KT, H0 * HD0])
    wo_hi, wo_lo = (sbuf(c, n, [P, HT, D], F32R) for n in ("wo_hi", "wo_lo"))
    wqkv = sbuf(c, "wqkv", [P, KT, 3 * D])
    bq, bk, bv = (sbuf(c, n, [P, HT]) for n in ("bq", "bk", "bv"))
    bo = sbuf(c, "bo", [P, KT])
    akT = sbuf(c, "akT", [P, HT, B])
    headones = const("head16").rearrange("p (t h) -> p t h", t=KT)
    band_h = sbuf(c, "band_h", [P, SPB // 2, 2 * W0], BF16)
    xrow = sbuf(c, "xrow", [P, D])
    avw = sbuf(c, "avw", [2 * H0, D])
    kblk = sbuf(c, "kblk", [P, HT, 2, 2 * (L + 1)])
    prob = sbuf(c, "prob", [P, H0, W0])
    pkey = sbuf(c, "pkey", [P, H0, L])
    acond = sbuf(c, "acond", [P, 2 * H0])
    mx, sm, aw = (sbuf(c, n, [P, H0]) for n in ("mx", "sm", "aw"))

    x_loaded = sem(c, "a_x_loaded")
    avw_stored, rest_loaded = sem(c, "p_avw_stored"), sem(c, "p_rest_loaded")
    with ExitStack() as s:
        cond = sbuf(s, "cond", [B, D])
        condT = sbuf(s, "condT", [P, KT, B])
        avT = sbuf(s, "avT", [P, HT, B])
        wv = fk[:, :, 0:H0 * HD0]
        wo = fk[:, 0, H0 * HD0:H0 * HD0 + HT * D].rearrange("p (m n) -> p m n", n=D)
        avw_rows = fv[0:B, 0:H0]
        g, g2, gn = (sbuf(s, n, [P, KT]) for n in ("g", "g2", "gn"))
        unused = sbuf(s, "unused", [P, 4, D + 1])
        pst = s.enter_context(nc.psum_tensor("pst", [P, 2, 512], F32))
        psa = s.enter_context(nc.psum_tensor("psa", [P, 2, 512], F32))
        psv = s.enter_context(nc.psum_tensor("psv", [B, 4, 512], F32))
        key_loaded, wv_loaded, wo_loaded, unused_zero, unused_set, filled = (sem(s, n) for n in (
            "p_key_loaded", "p_wv_loaded", "p_wo_loaded", "p_unused_zero", "p_unused_set",
            "p_filled"))
        condT_ps, condT_done, ak_ps, ak_done, av_ps, av_done, avw_ps, avw_done = (sem(s, n) for n in (
            "p_condT_ps", "p_condT_done", "p_ak_ps", "p_ak_done", "p_av_ps", "p_av_done", "p_avw_ps", "p_avw_done"))
        wo_hi_done = sem(s, "p_wo_hi_done")
        g2_done, gs_ps, gs_root, gs_inv, gn_done = (sem(s, n) for n in (
            "p_g2_done", "p_gs_ps", "p_gs_root", "p_gs_inv", "p_gn_done"))
        block = s.enter_context(nc.Block())
        def column(name):
            return t[name].rearrange("(m p) -> p m", p=P)

        def rows(name):
            return t[name].rearrange("(k p) n -> p k n", p=P)

        loads = [
            (key_loaded, [(consts[:], t["consts"]), (cond[:], t["cond_1024"]), (bk[:], column("L0_cond_WK_b")),
                          (wk[:], rows("L0_cond_WK_w"))]),
            (wv_loaded, [(bv[:], column("L0_cond_WV_b")), (g[:], t["L0_ffn_g_info"][0, 0].rearrange("(m p) -> p m", p=P)),
                         (wv, rows("L0_cond_WV_w"))]),
            (wo_loaded, [(wo, rows("L0_cond_WO_w"))]),
            (rest_loaded, [(bq[:], column("L0_cond_WQ_b")), (bo[:], column("L0_cond_WO_b")),
                           (wq[:], rows("L0_cond_WQ_w")), (wqkv[:], rows("L0_ffn_W_qkv"))]),
        ]

        @block.sync
        def _(sp):
            for done, pieces in loads:
                for dst, src in pieces:
                    with nc.allow_non_contiguous_dma(reason="bias columns"):
                        sp.dma_start(dst, src).then_inc(done, 16)
            sp.dma_start(xrow[:], t["x"][0:2].rearrange("b l d -> (b l) d")).then_inc(x_loaded, 16)
            sp.wait_ge(unused_set, 1)
            parts = XROWS // P // 4
            for n in range(parts):
                sp.dma_start(xtab_d[n * 4 * P:(n + 1) * 4 * P].rearrange("(p r) d -> p (r d)", p=P),
                             unused[:].rearrange("p r d -> p (r d)")).then_inc(filled, 16)
            sp.wait_ge(avw_done, H0 // 2)
            sp.dma_start(avw_d.rearrange("(b h) d -> b h d", h=H0), avw_rows).then_inc(avw_stored, 16)
            sp.wait_ge(filled, 16 * parts)

        @block.tensor
        def _(pe):
            pe.wait_ge(key_loaded, 64)
            for k in range(KT):
                m = pe.transpose(pst[:, 0, k * B:(k + 1) * B], cond[:, k * P:(k + 1) * P], ident[0:B, 0:B])
            m.then_inc(condT_ps, 1)
            pe.wait_ge(condT_done, 1)
            for w, out, ready in ((wk, psa[:, 0], ak_ps), (wv, psa[:, 1], av_ps)):
                if w is wv:
                    pe.wait_ge(wv_loaded, 48)
                for n in range(HT):
                    for k in range(KT):
                        m = pe.matmul(out[:, n * B:(n + 1) * B], w[:, k, n * P:(n + 1) * P], condT[:, k],
                                      start=(k == 0), stop=(k == KT - 1))
                m.then_inc(ready, 1)
            pe.wait_ge(g2_done, 1)
            pe.matmul(pst[:, 1, 0:KT], const("same_head"), g2[:], start=True, stop=True).then_inc(gs_ps, 1)
            pe.wait_ge(av_done, 1)
            pe.wait_ge(wo_loaded, 16)
            for n in range(H0 // 2):
                if n >= 2:
                    pe.wait_ge(avw_done, n - 1)
                for a in range(2):
                    m = pe.matmul(psv[:, 2 * (n % 2) + a, 0:D], avT[64 * a:64 * a + 64, n],
                                  wo[64 * a:64 * a + 64, n], start=True, stop=True)
                m.then_inc(avw_ps, 1)

        @block.vector
        def _(dve):
            dve.memset(unused[:], 0.0).then_inc(unused_zero, 1)
            dve.memset(kblk[:], 0.0)
            dve.memset(acond[:], 0.0)
            dve.wait_ge(key_loaded, 64)
            dve.wait_ge(unused_zero, 1)
            dve.tensor_copy(unused[:, :, D].bitcast(U32), const("free_id")).then_inc(unused_set, 1)
            dve.tensor_copy(ident_h[:], ident)
            for n in range(SPB // 2):
                dve.tensor_copy(band_h[:, n], const("band"))
            dve.wait_ge(condT_ps, 1)
            dve.tensor_copy(condT[:].rearrange("p k b -> p (k b)"), pst[:, 0, 0:KT * B]).then_inc(condT_done, 1)
            dve.wait_ge(ak_ps, 1)
            dve.tensor_tensor(akT[:], psa[:, 0].rearrange("p (m b) -> p m b", b=B), bc(bk[:], [P, HT, B]),
                              ALU.add).then_inc(ak_done, 1)
            dve.wait_ge(wv_loaded, 48)
            dve.tensor_tensor(g2[:], g[:], g[:], ALU.mult).then_inc(g2_done, 1)
            dve.wait_ge(av_ps, 1)
            dve.tensor_tensor(avT[:], psa[:, 1].rearrange("p (m b) -> p m b", b=B), bc(bv[:], [P, HT, B]),
                              ALU.add).then_inc(av_done, 1)
            dve.wait_ge(gs_root, 1)
            dve.reciprocal(g2[:], gn[:]).then_inc(gs_inv, 1)
            dve.wait_ge(gs_inv, 1)
            dve.tensor_tensor(gn[:], g2[:], g[:], ALU.mult).then_inc(gn_done, 1)
            dve.wait_ge(gn_done, 1)
            dve.tensor_tensor(qgblk[:], headones, bc(gn[:], [P, KT, H1]), ALU.mult)
            dve.wait_ge(wo_hi_done, 1)
            dve.tensor_tensor(wo_lo[:], wo, wo_hi[:].bitcast(F32), ALU.subtract)
            for n in range(H0 // 2):
                dve.wait_ge(avw_ps, n + 1)
                dve.tensor_copy(avw_rows[:, 2 * n:2 * n + 2], psv[:, 2 * (n % 2):2 * (n % 2) + 2, 0:D]).then_inc(avw_done, 1)

        @block.scalar
        def _(act):
            act.wait_ge(wo_loaded, 16)
            act.copy(wo_hi[:], wo).then_inc(wo_hi_done, 1)
            act.wait_ge(gs_ps, 1)
            act.activation(gn[:], pst[:, 1, 0:KT], ACT.Sqrt).then_inc(gs_root, 1)

    with ExitStack() as s:
        xT = sbuf(s, "xT", [P, KT, P])
        qT = sbuf(s, "qT", [P, HT, P])
        vblk = sbuf(s, "vblk", [P, HT, 2, P])
        probT = sbuf(s, "probT", [P, HT, P])
        acondT = sbuf(s, "acondT", [2 * H0, P])
        att_hi, att_lo = (sbuf(s, n, [P, HT, P], F32R) for n in ("att_hi", "att_lo"))
        yrow = sbuf(s, "yrow", [P, D])
        yT = sbuf(s, "yT", [P, KT, P])
        qs = sbuf(s, "qs", [P, KT, P])
        qq = sbuf(s, "qq", [P, KT, P])
        score = s.enter_context(nc.psum_tensor("score", [P, 4, 512], F32))
        bank = [s.enter_context(nc.psum_tensor(f"bank{n}", [P, 512], F32)) for n in range(4)]
        names = ("avw_loaded xT_ps xT_done q_ps q_done k_ps k_done ak_set s_ps max_done sub_done exp_done "
                 "sum_done inv_done prob_done aw_done acond_done pT_ps pT_done aT_ps aT_done att_ps att_hi att_done y_ps yrow_done yT_ps y_done "
                 "f_ps fq_done qq_done fv_ps fv_done v_ps v_done sim_ps sim_done fq_kept")
        S = {n: sem(s, "a_" + n) for n in names.split()}
        S["x_loaded"] = x_loaded
        block = s.enter_context(nc.Block())
        s4 = score[:].rearrange("p n c -> p (n c)")

        def slots(half):
            return score[:, 2 * half:2 * half + 2, 0:SPB * W0].rearrange("p n (s w) -> p n s w", w=W0)

        def half_of(ap, half):
            return ap[:, 8 * half:8 * half + 8]

        def prob4(half):
            return prob[:, 8 * half:8 * half + 8].rearrange("p (n s) w -> p n s w", s=SPB)

        @block.sync
        def _(sp):
            def load(i, first=False):
                if not first:
                    sp.wait_ge(S["xT_ps"], i)
                    sp.dma_start(xrow[:], t["x"][bass.ds(i * 2, 2)].rearrange("b l d -> (b l) d")).then_inc(S["x_loaded"], 16)
                if first:
                    sp.wait_ge(avw_stored, 16)
                else:
                    sp.wait_ge(S["y_ps"], i)
                sp.dma_start(avw[:], avw_d[bass.ds(i * 2 * H0, 2 * H0)]).then_inc(S["avw_loaded"], 16)
            load(0, True)
            with sp.Fori(1, PAIRS) as i:
                load(i)

        Q_BANK, K_BANK = (1, 3), (2, 0)
        W_BANK, A_BANK, ATT_BANK, Y_BANK = (1, 3), 2, (1, 3), 0
        V_BANK, F_BANK, FV_BANK, X_BANK, SIM_BANK = (2, 1, 3, 2), 0, 1, 3, 2

        @block.tensor
        def _(pe):
            def turn_x(i):
                pe.wait_ge(S["x_loaded"], i * 16 + 16)
                for k in range(KT):
                    m = pe.transpose(bank[X_BANK][:, k * P:(k + 1) * P], xrow[:, k * P:(k + 1) * P], ident)
                m.then_inc(S["xT_ps"], 1)

            def project(i, first=False):
                pe.wait_ge(S["xT_done"], i + 1)
                if not first:
                    pe.wait_ge(S["fv_done"], i - 1)
                for half in range(2):
                    for n in range(4):
                        for k in range(KT):
                            m = pe.matmul(bank[Q_BANK[half]][:, n * P:(n + 1) * P],
                                          wq[:, k, (4 * half + n) * P:(4 * half + n + 1) * P],
                                          xT[:, k], start=(k == 0), stop=(k == KT - 1))
                    m.then_inc(S["q_ps"], 1)
                if not first:
                    pe.wait_ge(S["sim_done"], i - 1)
                for half in range(2):
                    for n in range(4):
                        for k in range(KT):
                            m = pe.matmul(bank[K_BANK[half]][:, n * P:(n + 1) * P],
                                          wk[:, k, (4 * half + n) * P:(4 * half + n + 1) * P],
                                          xT[:, k], start=(k == 0), stop=(k == KT - 1))
                    m.then_inc(S["k_ps"], 1)

            def weights(i, last=False):
                if last:
                    pe.wait_ge(S["xT_done"], i + 1)
                    pe.wait_ge(S["fv_done"], i)
                    pe.wait_ge(S["sim_done"], i)
                else:
                    pe.wait_ge(S["q_done"], i * 2 + 4)
                for half in range(2):
                    pe.wait_ge(S["prob_done"], i * 2 + half + 1)
                    for n in range(4):
                        p = 4 * half + n
                        m = pe.transpose(bank[W_BANK[half]][:, n * P:(n + 1) * P],
                                         pkey[:, 2 * p:2 * p + 2].rearrange("p a k -> p (a k)"), ident)
                    m.then_inc(S["pT_ps"], 1)
                pe.wait_ge(S["acond_done"], i + 1)
                if not last:
                    pe.wait_ge(S["k_done"], i * 2 + 3)
                pe.transpose(bank[A_BANK][0:2 * H0, 0:P], acond[:], ident).then_inc(S["aT_ps"], 1)

            def attend(i):
                pe.wait_ge(S["v_done"], i * 4 + 4)
                for half in range(2):
                    pe.wait_ge(S["pT_done"], i * 2 + half + 1)
                    for n in range(4):
                        p = 4 * half + n
                        for q in range(2):
                            for a in range(2):
                                m = pe.matmul(bank[ATT_BANK[half]][64 * a:64 * a + 64, n * P + q * L:n * P + (q + 1) * L],
                                              vblk[:, p, q, 64 * a:64 * a + 64], probT[:, p, q * L:(q + 1) * L],
                                              start=True, stop=True)
                    m.then_inc(S["att_ps"], 1)

            def mask_scores(i):
                pe.wait_ge(S["sub_done"], i * 2)
                for n in range(4):
                    pe.matmul(score[:, n, 0:SPB * W0], ident_h[:], band_h[:].rearrange("p n w -> p (n w)"),
                              start=True, stop=True)

            def scores(i):
                pe.wait_ge(S["q_done"], i * 2 + 2)
                pe.wait_ge(S["k_done"], i * 2 + 2)
                pe.wait_ge(S["ak_set"], i + 1)
                for p in range(HT):
                    for q in range(2):
                        o = (p % 2) * 2 * W0
                        out = score[64 * q:64 * q + 64, p // 2, o:o + 2 * W0].rearrange("p (s w) -> p s w", w=W0)[:, :, 0:L + 1]
                        m = pe.matmul(out, qT[:, p, q * L:(q + 1) * L], kblk[:, p, q].rearrange("p (s w) -> p s w", s=2),
                                      start=False, stop=True, skip_group_check=True)
                    if p % 4 == 3:
                        m.then_inc(S["s_ps"], 1)

            def through_wo(i):
                pe.wait_ge(S["att_done"], i * 2 + 2)
                pe.wait_ge(S["aT_done"], i + 1)
                pe.wait_ge(S["avw_loaded"], i * 16 + 16)
                out = bank[Y_BANK][:, 0:D]
                pe.matmul(out, acondT[:], avw[:], start=True, stop=False)
                for p in range(HT):
                    pe.matmul(out, att_lo[:, p], wo_hi[:, p], start=False, stop=False)
                    pe.matmul(out, att_hi[:, p], wo_lo[:, p], start=False, stop=False)
                    m = pe.matmul(out, att_hi[:, p], wo_hi[:, p], start=False, stop=(p == HT - 1))
                m.then_inc(S["y_ps"], 1)

            def turn_y(i):
                pe.wait_ge(S["yrow_done"], i + 1)
                for k in range(KT):
                    m = pe.transpose(bank[Y_BANK][:, k * P:(k + 1) * P], yrow[:, k * P:(k + 1) * P], ident)
                m.then_inc(S["yT_ps"], 1)

            def values(i, banks, first=False):
                for n in banks:
                    if n == 3 or first:
                        pe.wait_ge(S["v_done"], i * 4 + (1 if n == 3 else 0))
                    for j in range(4):
                        p, q = 2 * n + j // 2, j % 2
                        m = pe.transpose(bank[V_BANK[n]][:, j * P:(j + 1) * P], kblk[:, p, q, 1:1 + 2 * L], ident)
                    m.then_inc(S["v_ps"], 1)

            def masked_qkv(i, last=False):
                pe.wait_ge(S["y_done"], i + 1)
                for n in range(4):
                    for k in range(KT):
                        m = pe.matmul(bank[F_BANK][:, n * P:(n + 1) * P], wqkv[:, k, n * P:(n + 1) * P], yT[:, k],
                                      start=(k == 0), stop=(k == KT - 1))
                m.then_inc(S["f_ps"], 1)
                if not last:
                    pe.wait_ge(S["v_done"], i * 4 + 6)
                for k in range(KT):
                    m = pe.matmul(bank[FV_BANK][:, 0:D], yT[:, k], wqkv[:, k, 2 * D:3 * D],
                                  start=(k == 0), stop=(k == KT - 1))
                m.then_inc(S["fv_ps"], 1)

            def similarity(i, last=False):
                pe.wait_ge(S["fq_done"], i + 1)
                pe.wait_ge(S["qq_done"], i + 1)
                if not last:
                    pe.wait_ge(S["v_done"], i * 4 + 8)
                for o, src, w in ((0, qs, qgblk), (H1, qq, headones)):
                    for k in range(KT):
                        m = pe.matmul(bank[SIM_BANK][:, o:o + H1], src[:, k], w[:, k], start=(k == 0), stop=(k == KT - 1))
                m.then_inc(S["sim_ps"], 1)

            pe.wait_ge(rest_loaded, 64)
            turn_x(0)
            project(0, True)
            mask_scores(0)
            scores(0)
            pe.wait_ge(S["q_done"], 2)
            values(0, range(4), True)
            pe.wait_ge(S["v_done"], 3)
            turn_x(1)
            pe.wait_ge(S["v_done"], 4)

            def step(i, last=False):
                project(i + 1, isinstance(i, int) and i == 0)
                weights(i)
                mask_scores(i + 1)
                attend(i)
                scores(i + 1)
                through_wo(i)
                values(i + 1, range(0, 2))
                turn_y(i)
                values(i + 1, range(2, 4))
                masked_qkv(i)
                if not last:
                    pe.wait_ge(S["v_done"], i * 4 + 7)
                    turn_x(i + 2)
                similarity(i)

            step(0)
            with pe.Fori(1, PAIRS - 2) as i:
                step(i)
            step(PAIRS - 2, True)
            weights(PAIRS - 1, True)
            attend(PAIRS - 1)
            through_wo(PAIRS - 1)
            turn_y(PAIRS - 1)
            masked_qkv(PAIRS - 1, True)
            similarity(PAIRS - 1, True)

        @block.vector
        def _(dve):
            def bias_out(i):
                for half in range(2):
                    dve.wait_ge(S["q_ps"], i * 2 + half + 1)
                    dve.tensor_tensor(qT[:, 4 * half:4 * half + 4], bank[Q_BANK[half]][:].rearrange("p (m n) -> p m n", n=P),
                                      bc(bq[:, 4 * half:4 * half + 4], [P, 4, P]), ALU.add).then_inc(S["q_done"], 1)
                for half in range(2):
                    dve.wait_ge(S["k_ps"], i * 2 + half + 1)
                    for a in range(2):
                        r = slice(64 * a, 64 * a + 64)
                        src = bank[K_BANK[half]][r].rearrange("p (m q n) -> p m q n", q=2, n=L)
                        b4 = bc(bc(bk[r, 4 * half:4 * half + 4], [64, 4, 2]), [64, 4, 2, L])
                        m = dve.tensor_tensor(kblk[r, 4 * half:4 * half + 4, :, 1 + a * L:1 + (a + 1) * L], src, b4, ALU.add)
                    m.then_inc(S["k_done"], 1)

            def softmax(i):
                for half in range(2):
                    dve.wait_ge(S["s_ps"], i * 2 + half + 1)
                    dve.tensor_reduce(half_of(mx, half).rearrange("p (n s) -> p n s", s=SPB), slots(half), X,
                                      ALU.max).then_inc(S["max_done"], 1)
                    dve.wait_ge(S["max_done"], i * 2 + half + 1)
                    dve.wait_ge(S["acond_done"], i)
                    dve.tensor_tensor(prob4(half), slots(half),
                                      bc(half_of(mx, half).rearrange("p (n s) -> p n s", s=SPB), [P, 2, SPB, W0]),
                                      ALU.subtract).then_inc(S["sub_done"], 1)
                for half in range(2):
                    dve.wait_ge(S["exp_done"], i * 2 + half + 1)
                    dve.tensor_reduce(half_of(sm, half), prob[:, 8 * half:8 * half + 8], X, ALU.add).then_inc(S["sum_done"], 1)
                    dve.wait_ge(S["sum_done"], i * 2 + half + 1)
                    dve.reciprocal(half_of(sm, half), half_of(sm, half)).then_inc(S["inv_done"], 1)

            def sim_out(i):
                dve.wait_ge(S["sim_ps"], i + 1)
                dve.tensor_copy(sims[:, bass.ds(i, 1)].rearrange("p a b -> p (a b)"),
                                bank[SIM_BANK][:, 0:2 * H1]).then_inc(S["sim_done"], 1)

            def attention_low(i):
                for half in range(2):
                    part = slice(4 * half, 4 * half + 4)
                    dve.wait_ge(S["att_hi"], i * 2 + half + 1)
                    dve.tensor_tensor(att_lo[:, part].rearrange("p m n -> p (m n)"), bank[ATT_BANK[half]][:],
                                      att_hi[:, part].bitcast(F32).rearrange("p m n -> p (m n)"), ALU.subtract).then_inc(S["att_done"], 1)

            bias_out(0)
            softmax(0)
            with dve.Fori(0, PAIRS - 1) as i:
                bias_out(i + 1)
                attention_low(i)
                softmax(i + 1)
                sim_out(i)
            attention_low(PAIRS - 1)
            sim_out(PAIRS - 1)

        @block.scalar
        def _(act):
            def xT_out(i):
                act.wait_ge(S["xT_ps"], i + 1)
                act.wait_ge(S["k_ps"], i * 2)
                act.copy(xT[:].rearrange("p k n -> p (k n)"), bank[X_BANK][:, 0:KT * P]).then_inc(S["xT_done"], 1)

            def attend_out(i):
                for half in range(2):
                    act.wait_ge(S["pT_ps"], i * 2 + half + 1)
                    act.copy(probT[:, 4 * half:4 * half + 4].rearrange("p m n -> p (m n)"), bank[W_BANK[half]][:]).then_inc(S["pT_done"], 1)
                act.wait_ge(S["aT_ps"], i + 1)
                act.copy(acondT[:], bank[A_BANK][0:2 * H0, 0:P]).then_inc(S["aT_done"], 1)
                for half in range(2):
                    act.wait_ge(S["att_ps"], i * 2 + half + 1)
                    act.copy(att_hi[:, 4 * half:4 * half + 4].rearrange("p m n -> p (m n)"),
                             bank[ATT_BANK[half]][:]).then_inc(S["att_hi"], 1)

            def yrow_out(i):
                act.wait_ge(S["y_ps"], i + 1)
                act.copy(yrow[:], bank[Y_BANK][:, 0:D]).then_inc(S["yrow_done"], 1)

            def y_out(i):
                act.wait_ge(S["yT_ps"], i + 1)
                for n in range(KT):
                    m = act.activation(yT[:, n], bank[Y_BANK][:, n * P:(n + 1) * P], ACT.Identity, bias=bo[:, n:n + 1])
                m.then_inc(S["y_done"], 1)

            def exps(i):
                for half in range(2):
                    act.wait_ge(S["sub_done"], i * 2 + half + 1)
                    act.activation(prob[:, 8 * half:8 * half + 8], prob[:, 8 * half:8 * half + 8], ACT.Exp,
                                   scale=HD0 ** -0.5).then_inc(S["exp_done"], 1)

            def masked_out(i):
                act.wait_ge(S["f_ps"], i + 1)
                act.wait_ge(S["fq_kept"], i)
                act.wait_ge(S["sim_ps"], i)
                qp = bank[F_BANK][:, 0:KT * P].rearrange("p (k n) -> p k n", n=P)
                act.copy(qs[:], qp).then_inc(S["fq_done"], 1)
                act.activation(qq[:], qp, ACT.Square).then_inc(S["qq_done"], 1)
                act.copy(fk[:, :, bass.ds(i * P, P)], bank[F_BANK][:, KT * P:].rearrange("p (k n) -> p k n", n=P))
                act.wait_ge(S["fv_ps"], i + 1)
                act.copy(fv[:, bass.ds(i, 1)].rearrange("p a b -> p (a b)"), bank[FV_BANK][:, 0:D]).then_inc(S["fv_done"], 1)

            def values_out(i, banks):
                for n in banks:
                    act.wait_ge(S["v_ps"], i * 4 + n + 1)
                    act.copy(vblk[:, 2 * n:2 * n + 2].rearrange("p m q n -> p (m q n)"), bank[V_BANK[n]][:]).then_inc(S["v_done"], 1)

            xT_out(0)
            exps(0)
            values_out(0, range(4))
            xT_out(1)

            def step(i, last=False):
                attend_out(i)
                exps(i + 1)
                yrow_out(i)
                values_out(i + 1, range(0, 1))
                y_out(i)
                values_out(i + 1, range(1, 4))
                masked_out(i)
                if not last:
                    xT_out(i + 2)

            step(0)
            with act.Fori(1, PAIRS - 2) as i:
                step(i)
            step(PAIRS - 2, True)
            attend_out(PAIRS - 1)
            yrow_out(PAIRS - 1)
            y_out(PAIRS - 1)
            masked_out(PAIRS - 1)

        upper_lower = [const("same_seq")[:, 64 * q:64 * q + 1] for q in range(2)]

        @block.gpsimd
        def _(pool):
            def condition_keys(i, first=False):
                if not first:
                    pool.wait_ge(S["v_ps"], i * 4)
                for a in range(2):
                    m = pool.tensor_tensor(kblk[:, :, :, a * (2 * L + 1)], akT[:, :, bass.ds(i * 2, 2)],
                                           bc(upper_lower[a].broadcast_to([P, HT]), [P, HT, 2]), ALU.mult)
                m.then_inc(S["ak_set"], 1)

            def normalise(i):
                for half in range(2):
                    pool.wait_ge(S["inv_done"], i * 2 + half + 1)
                    pool.wait_ge(S["pT_ps"], i * 2)
                    for a in range(2):
                        heads = slice(8 * half + a, 8 * half + 8, 2)
                        m = pool.tensor_tensor(pkey[:, heads], prob[:, heads, 1 - a:1 - a + L], bc(sm[:, heads], [P, 4, L]), ALU.mult)
                    m.then_inc(S["prob_done"], 1)
                pool.wait_ge(S["aT_ps"], i)
                for a in range(2):
                    m = pool.tensor_tensor(aw[:, a::2], prob[:, a::2, a * L], sm[:, a::2], ALU.mult)
                m.then_inc(S["aw_done"], 1)
                pool.wait_ge(S["aw_done"], i + 1)
                for q in range(2):
                    m = pool.tensor_tensor(acond[:, q * H0:(q + 1) * H0], aw[:], upper_lower[q].broadcast_to([P, H0]), ALU.mult)
                m.then_inc(S["acond_done"], 1)

            def keep_q(i):
                pool.wait_ge(S["fq_done"], i + 1)
                pool.tensor_copy(fq[:, :, bass.ds(i * P, P)], qs[:]).then_inc(S["fq_kept"], 1)

            condition_keys(0, True)
            normalise(0)
            with pool.Fori(0, PAIRS - 1) as i:
                condition_keys(i + 1)
                normalise(i + 1)
                keep_q(i)
            keep_q(PAIRS - 1)




def classes(nc, c, sbuf, sem, const, ident, sims, key_bias, reg_bias):
    n16 = [P, PAIRS, H1]
    root, inv = sbuf(c, "root", n16), sbuf(c, "inv", n16)
    sim, low, high, scaled, cls = (sbuf(c, n, [P, PAIRS]) for n in ("sim", "low", "high", "scaled", "cls"))
    ext, extT, both, span = sbuf(c, "ext", [P, 2]), sbuf(c, "extT", [2, P]), sbuf(c, "both", [P, 2]), sbuf(c, "span", [P, 2])
    ends, endrow = sbuf(c, "ends", [2, 1]), sbuf(c, "endrow", [2, 2])
    ones2 = sbuf(c, "ones2", [2, P])
    far = sbuf(c, "far", [P, 1])
    diag = sbuf(c, "diag", [P, PAIRS, L], BF16)
    seq_h = sbuf(c, "seq_h", [P, P], BF16)
    slope, offset, tmp = (sbuf(c, n, [P, PAIRS, L]) for n in ("slope", "offset", "tmp"))
    first_h = sbuf(c, "first_h", [P, 2, P], BF16)
    ps = c.enter_context(nc.psum_tensor("cls_ps", [P, 4, 512], F32))
    ps_reg = c.enter_context(nc.psum_tensor("cls_reg", [P, 2, 512], F32))
    ps_s = c.enter_context(nc.psum_tensor("cls_s", [P, 512], F32))
    rooted, ext_done, extT_ps, end_set, end_ps, diag_done, key_ps, reg_ps, reg_done = (sem(c, "c_" + n) for n in (
        "rooted", "ext_done", "extT_ps", "end_set", "end_ps", "diag_done", "key_ps", "reg_ps", "reg_done"))
    step = sem(c, "c_step")
    block = c.enter_context(nc.Block())

    @block.scalar
    def _(act):
        act.activation(root[:], sims[:, :, H1:2 * H1], ACT.Sqrt).then_inc(rooted, 1)
        for n in range(8):
            act.wait_ge(reg_ps, n + 1)
            act.activation(reg_bias[:, 4 * n:4 * n + 4].rearrange("p a q b -> p q a b"),
                           ps_reg[:, n % 2].rearrange("p (q a b) -> p q a b", q=2, b=L), ACT.Identity,
                           scale=NEG).then_inc(reg_done, 1)

    @block.tensor
    def _(pe):
        pe.wait_ge(ext_done, 1)
        pe.transpose(ps_s[0:2, 0:P], ext[:], ident).then_inc(extT_ps, 1)
        pe.wait_ge(end_set, 1)
        pe.matmul(ps_s[:, P:P + 2], ones2[:], endrow[:], start=True, stop=True).then_inc(end_ps, 1)
        pe.wait_ge(diag_done, 1)
        for n in range(4):
            m = pe.matmul(ps[:, n], seq_h[:], diag[:, 8 * n:8 * n + 8].rearrange("p a b -> p (a b)"), start=True, stop=True)
        m.then_inc(key_ps, 1)
        for n in range(8):
            if n >= 2:
                pe.wait_ge(reg_done, n - 1)
            for q in range(2):
                m = pe.matmul(ps_reg[:, n % 2, q * 4 * L:(q + 1) * 4 * L], first_h[:, q],
                              diag[:, 4 * n:4 * n + 4].rearrange("p a b -> p (a b)"), start=True, stop=True)
            m.then_inc(reg_ps, 1)

    @block.vector
    def _(dve):
        done = 0

        def then(ins):
            nonlocal done
            done += 1
            ins.then_inc(step, 1)
            dve.wait_ge(step, done)

        dve.memset(endrow[:], 0.0)
        dve.memset(ones2[:], 1.0)
        dve.tensor_copy(seq_h[:], const("same_seq"))
        for q in range(2):
            then(dve.tensor_scalar(first_h[:, q], const("same_seq")[:, 64 * q:64 * q + 1].broadcast_to([P, P]), 1.0, None, ALU.mult))
        then(dve.tensor_scalar(far[:], const("is_tok"), -NEG, NEG, ALU.mult, ALU.add))
        dve.wait_ge(rooted, 1)
        then(dve.reciprocal(inv[:], root[:]))
        then(dve.tensor_tensor(root[:], sims[:, :, 0:H1], inv[:], ALU.mult))
        then(dve.tensor_reduce(low[:], root[:], X, ALU.add))
        then(dve.tensor_scalar(sim[:], low[:], 1.0 / H1, None, ALU.mult))
        then(dve.tensor_scalar(high[:], sim[:], far[:], None, ALU.add))
        then(dve.tensor_scalar(low[:], sim[:], -1.0, far[:], ALU.mult, ALU.add))
        dve.tensor_reduce(ext[:, 0:1], low[:], X, ALU.max)
        dve.tensor_reduce(ext[:, 1:2], high[:], X, ALU.max).then_inc(ext_done, 1)
        dve.wait_ge(extT_ps, 1)
        then(dve.tensor_reduce(ends[:], ps_s[0:2, 0:P], X, ALU.max))
        dve.tensor_tensor(endrow[:], ident[0:2, 0:2], ends[:].broadcast_to([2, 2]), ALU.mult).then_inc(end_set, 1)
        dve.wait_ge(end_ps, 1)
        then(dve.tensor_copy(both[:], ps_s[:, P:P + 2]))
        then(dve.tensor_tensor(span[:, 0:1], both[:, 0:1], both[:, 1:2], ALU.add))
        then(dve.reciprocal(span[:, 1:2], span[:, 0:1]))
        then(dve.tensor_scalar(scaled[:], sim[:], both[:, 0:1], span[:, 1:2], ALU.add, ALU.mult))
        then(dve.tensor_scalar(low[:], scaled[:], 0.9, const("is_tok"), ALU.is_gt, ALU.mult))
        dve.tensor_tensor(diag[:], bc(low[:], [P, PAIRS, L]),
                          const("key_diag").unsqueeze(1).broadcast_to([P, PAIRS, L]), ALU.mult).then_inc(diag_done, 1)
        then(dve.tensor_scalar(far[:], const("is_tok"), -1.0, 1.0, ALU.mult, ALU.add))
        then(dve.tensor_scalar(cls[:], low[:], far[:], None, ALU.add))
        dve.tensor_scalar(high[:], cls[:], -2.0, 1.0, ALU.mult, ALU.add)
        then(dve.tensor_tensor(offset[:], bc(cls[:], [P, PAIRS, L]),
                               const("tok_row").unsqueeze(1).broadcast_to([P, PAIRS, L]), ALU.mult))
        dve.wait_ge(key_ps, 1)
        then(dve.tensor_tensor(slope[:], ps[:].rearrange("p n (a b) -> p (n a) b", b=L), bc(high[:], [P, PAIRS, L]), ALU.mult))
        then(dve.tensor_tensor(tmp[:], slope[:], offset[:], ALU.add))
        dve.tensor_scalar(key_bias[:], tmp[:], NEG, None, ALU.mult)


def masked_pass(nc, c, sbuf, sem, t, const, ident, ident_h, fq, fk, fv, key_bias, reg_bias, x1T, x1_d, start,
                start_loaded):
    wp = sbuf(c, "wp", [P, KT, D])
    bp = sbuf(c, "bp", [P, D])
    xrow = sbuf(c, "mxrow", [P, D])
    xb = sbuf(c, "xb", [P, D])
    x1 = sbuf(c, "x1", [P, D])
    q = sbuf(c, "q_pair", [P, KT, P])
    kp = sbuf(c, "k_pair", [P, KT, P])
    v = sbuf(c, "v_pair", [P, D])
    rq = sbuf(c, "rq", [P, KT, 2, L])
    kblk = sbuf(c, "mkblk", [P, KT, 2, 8, L])
    vblk = sbuf(c, "mvblk", [P, 2, 8, 2 * HD1])
    prob = sbuf(c, "mprob", [P, NSLOT, L])
    pkey = sbuf(c, "mpkey", [P, NSLOT, L])
    probT = sbuf(c, "mprobT", [P, NSLOT // 2, P])
    oT = sbuf(c, "oT", [P, KT, P])
    mx, sm = sbuf(c, "mmx", [P, NSLOT]), sbuf(c, "msm", [P, NSLOT])
    regh = sbuf(c, "regh", [P, 2 * KT, 8, REG])
    reg = sbuf(c, "reg", [P, KT, 2, REG])
    score = c.enter_context(nc.psum_tensor("mscore", [P, 3, 512], F32))
    pt = [c.enter_context(nc.psum_tensor(f"mpt{n}", [P, 512], F32)) for n in range(2)]
    pr = c.enter_context(nc.psum_tensor("mpr", [P, 512], F32))
    po = c.enter_context(nc.psum_tensor("mpo", [P, 512], F32))
    px = c.enter_context(nc.psum_tensor("mpx", [P, 512], F32))
    names = ("w_loaded x_loaded stored pads qk_set v_set rq_set kblk_set vblk_set s_ps max_done sub_done exp_done "
             "sum_done inv_done prob_done pT_ps pT_done o_ps o_done r_ps rmul_done rsum_done radd_done reg_done "
             "xb_done x_ps x1_done x1T_ps x1T_done")
    S = {n: sem(c, "m_" + n) for n in names.split()}
    block = c.enter_context(nc.Block())
    head8 = const("head8")
    sflat = score[:].rearrange("p n c -> p (n c)")[:, 0:NSLOT * L].rearrange("p (s k) -> p s k", k=L)

    @block.sync
    def _(sp):
        sp.dma_start(wp[:], t["L0_ffn_W_proj"].rearrange("(k p) n -> p k n", p=P)).then_inc(S["w_loaded"], 16)
        sp.dma_start(bp[:], t["L0_ffn_b_proj"].partition_broadcast(P)).then_inc(S["w_loaded"], 16)
        def step(i):
            sp.wait_ge(S["xb_done"], i)
            sp.dma_start(xrow[:], t["x"][bass.ds(i * 2, 2)].rearrange("b l d -> (b l) d")).then_inc(S["x_loaded"], 16)
            sp.wait_ge(S["x1_done"], i + 1)
            sp.dma_start(x1_d[bass.ds(i * 2, 2)].rearrange("b l d -> (b l) d"), x1[:]).then_inc(S["stored"], 16)

        step(0)
        for dst, src in start:
            with nc.allow_non_contiguous_dma(reason="bias columns"):
                sp.dma_start(dst, src).then_inc(start_loaded, 16)
        with sp.Fori(1, PAIRS) as i:
            step(i)
        sp.wait_ge(S["stored"], 16 * PAIRS)

    def half_blocks(eng, i, k):
        for s in range(2):
            m = eng.tensor_tensor(kblk[:, k, s], bc(head8, [P, 8, L]),
                                  fk[:, k, bass.ds(i * P + s * L, L)].unsqueeze(1).broadcast_to([P, 8, L]), ALU.mult)
        m.then_inc(S["kblk_set"], 1)

    @block.gpsimd
    def _(pool):
        def stage(i):
            pool.wait_ge(S["s_ps"], i)
            for k in range(KT):
                for s in range(2):
                    m = pool.tensor_tensor(rq[:, k, s, 0:8 * REG].rearrange("p (h r) -> p h r", r=REG), bc(head8, [P, 8, REG]),
                                           fq[:, k, bass.ds(i * P + s * L, REG)].unsqueeze(1).broadcast_to([P, 8, REG]), ALU.mult)
            m.then_inc(S["rq_set"], 1)
            half_blocks(pool, i, 1)

        def normalise(i):
            pool.wait_ge(S["inv_done"], i + 1)
            pool.wait_ge(S["pT_ps"], i * 3)
            pool.tensor_tensor(pkey[:], prob[:], bc(sm[:], [P, NSLOT, L]), ALU.mult).then_inc(S["prob_done"], 1)

        def residual(i):
            pool.wait_ge(S["x_loaded"], i * 16 + 16)
            pool.wait_ge(S["x1_done"], i)
            pool.tensor_tensor(xb[:], xrow[:], bp[:], ALU.add).then_inc(S["xb_done"], 1)

        pool.memset(rq[:], 0.0).then_inc(S["pads"], 1)
        pool.memset(vblk[:], 0.0).then_inc(S["pads"], 1)
        pool.wait_ge(S["pads"], 2)
        stage(0)
        stage(1)
        normalise(0)
        pool.wait_ge(S["w_loaded"], 32)

        def step(i, last=False):
            if not last:
                stage(i + 2)
            residual(i)
            normalise(i + 1)

        step(0)
        step(1)
        with pool.Fori(2, PAIRS - 2) as i:
            step(i)
        step(PAIRS - 2, True)
        residual(PAIRS - 1)

    @block.tensor
    def _(pe):
        def scores(i):
            pe.wait_ge(S["sub_done"], i)
            for n in range(2):
                pe.matmul(score[:, n], ident_h[:], key_bias[:, bass.ds(i, 1)].broadcast_to([P, 8, L]), start=True, stop=True)
            pe.matmul(score[:, 2, 0:2 * L], ident_h[:], reg_bias[:, bass.ds(i, 1)].rearrange("p a q b -> p (a q b)"), start=True, stop=True)
            pe.wait_ge(S["rq_set"], i + 1)
            pe.wait_ge(S["qk_set"], i + 1)
            for k in range(KT):
                for s in range(2):
                    pe.matmul(score[64 * k:64 * k + 64, 2, s * L:(s + 1) * L], rq[:, k, s], kp[:, k, s * L:(s + 1) * L],
                              start=False, stop=True, skip_group_check=True)
            pe.wait_ge(S["kblk_set"], i * 2 + 2)
            for k in range(KT):
                for s in range(2):
                    m = pe.matmul(score[64 * s:64 * s + 64, k], q[:, k, s * L:(s + 1) * L],
                                  kblk[:, k, s].rearrange("p h n -> p (h n)"), start=False, stop=True, skip_group_check=True)
            m.then_inc(S["s_ps"], 1)

        def transposed(i):
            pe.wait_ge(S["prob_done"], i + 1)
            pe.wait_ge(S["rmul_done"], i)
            pe.wait_ge(S["pT_done"], i * 3)
            for n in range(NSLOT // 2):
                out = (pt[0], pt[1], pr)[n // 4]
                m = pe.transpose(out[:, (n % 4) * P:(n % 4 + 1) * P], pkey[:, 2 * n:2 * n + 2].rearrange("p a k -> p (a k)"), ident)
                if n in (3, 7, 8):
                    m.then_inc(S["pT_ps"], 1)

        def weigh(i):
            pe.wait_ge(S["pT_done"], i * 3 + 3)
            pe.wait_ge(S["vblk_set"], i + 1)
            pe.wait_ge(S["o_done"], i)
            for s in range(2):
                for p in range(8):
                    r = 32 * (p % 4)
                    m = pe.matmul(po[r:r + 32, (p // 4) * P + s * L:(p // 4) * P + (s + 1) * L], vblk[:, s, p],
                                  probT[:, p, s * L:(s + 1) * L], start=True, stop=True, tile_position=(0, r))
            m.then_inc(S["o_ps"], 1)
            for k in range(KT):
                for s in range(2):
                    out = (pr[:, 0:KT * L], pt[0][:, 0:KT * L])[s]
                    m = pe.matmul(out[:, k * L:(k + 1) * L], v[64 * s:64 * s + 64, k * P:(k + 1) * P],
                                  probT[64 * s:64 * s + 64, 8, k * L:(k + 1) * L], start=True, stop=True)
            m.then_inc(S["r_ps"], 1)

        def projected(i):
            pe.wait_ge(S["reg_done"], i + 1)
            pe.wait_ge(S["x1T_done"], i)
            for k in range(KT):
                m = pe.matmul(px[:, 0:D], oT[:, k], wp[:, k], start=(k == 0), stop=(k == KT - 1))
            m.then_inc(S["x_ps"], 1)

        def turned(i):
            pe.wait_ge(S["x1_done"], i + 1)
            for k in range(KT):
                m = pe.transpose(px[:, k * P:(k + 1) * P], x1[:, k * P:(k + 1) * P], ident)
            m.then_inc(S["x1T_ps"], 1)

        scores(0)
        scores(1)
        pe.wait_ge(S["w_loaded"], 32)

        def step(i, first=False, last=False):
            transposed(i)
            if not first:
                turned(i - 1)
            weigh(i)
            if not last:
                scores(i + 2)
            projected(i)

        step(0, first=True)
        step(1)
        with pe.Fori(2, PAIRS - 2) as i:
            step(i)
        step(PAIRS - 2, last=True)
        step(PAIRS - 1, last=True)
        turned(PAIRS - 1)

    @block.vector
    def _(dve):
        def blocks(i):
            dve.wait_ge(S["s_ps"], i)
            half_blocks(dve, i, 0)

        def softmax_max(i):
            dve.wait_ge(S["s_ps"], i + 1)
            dve.tensor_reduce(mx[:], sflat, X, ALU.max).then_inc(S["max_done"], 1)

        def softmax_sub(i):
            dve.wait_ge(S["max_done"], i + 1)
            dve.wait_ge(S["prob_done"], i)
            dve.tensor_tensor(prob[:], sflat, bc(mx[:], [P, NSLOT, L]), ALU.subtract).then_inc(S["sub_done"], 1)

        def softmax_sum(i):
            dve.wait_ge(S["exp_done"], i + 1)
            dve.tensor_reduce(sm[:], prob[:], X, ALU.add).then_inc(S["sum_done"], 1)
            dve.wait_ge(S["sum_done"], i + 1)
            dve.reciprocal(sm[:], sm[:]).then_inc(S["inv_done"], 1)

        def registers(i):
            dve.wait_ge(S["r_ps"], i + 1)
            for s, src in enumerate((pr[:, 0:KT * L], pt[0][:, 0:KT * L])):
                for k in range(KT):
                    m = dve.tensor_tensor(regh[:, 2 * k + s], src[:, k * L:k * L + 8 * REG].rearrange("p (h r) -> p h r", r=REG),
                                          bc(head8, [P, 8, REG]), ALU.mult)
            m.then_inc(S["rmul_done"], 1)
            dve.wait_ge(S["rmul_done"], i + 1)
            dve.tensor_reduce(reg[:].rearrange("p k s r -> p (k s) r"), regh[:].rearrange("p n h r -> p n r h"), X,
                              ALU.add).then_inc(S["rsum_done"], 1)
            dve.wait_ge(S["rsum_done"], i + 1)
            dve.wait_ge(S["o_done"], i + 1)
            o = oT[:].rearrange("p k (s n) -> p k s n", s=2)[:, :, :, 0:REG]
            dve.tensor_tensor(reg[:], reg[:], o, ALU.add).then_inc(S["radd_done"], 1)
            dve.wait_ge(S["radd_done"], i + 1)
            dve.tensor_scalar(o, reg[:], 0.5, None, ALU.mult).then_inc(S["reg_done"], 1)

        def residual(i):
            dve.wait_ge(S["x_ps"], i + 1)
            dve.wait_ge(S["xb_done"], i + 1)
            dve.wait_ge(S["x1T_ps"], i)
            dve.wait_ge(S["stored"], i * 16)
            dve.tensor_tensor(x1[:], px[:, 0:D], xb[:], ALU.add).then_inc(S["x1_done"], 1)

        blocks(0)
        softmax_max(0)
        softmax_sub(0)
        blocks(1)
        softmax_sum(0)

        def step(i, first=False, last=False):
            softmax_max(i + 1)
            if not first:
                residual(i - 1)
            softmax_sub(i + 1)
            if not last:
                blocks(i + 2)
            softmax_sum(i + 1)
            registers(i)

        step(0, first=True)
        step(1)
        with dve.Fori(2, PAIRS - 2) as i:
            step(i)
        step(PAIRS - 2, last=True)
        residual(PAIRS - 2)
        registers(PAIRS - 1)
        residual(PAIRS - 1)

    @block.scalar
    def _(act):
        def exps(i):
            act.wait_ge(S["sub_done"], i + 1)
            act.activation(prob[:], prob[:], ACT.Exp, scale=HD1 ** -0.5).then_inc(S["exp_done"], 1)

        def queries(i):
            act.wait_ge(S["s_ps"], i)
            act.copy(kp[:], fk[:, :, bass.ds(i * P, P)])
            act.copy(q[:], fq[:, :, bass.ds(i * P, P)]).then_inc(S["qk_set"], 1)

        def stage_v(i):
            act.wait_ge(S["r_ps"], i)
            act.copy(v[:], fv[:, bass.ds(i, 1)].rearrange("p a b -> p (a b)")).then_inc(S["v_set"], 1)

        def values(i):
            act.wait_ge(S["v_set"], i + 1)
            for s in range(2):
                src = v[64 * s:64 * s + 64].rearrange("p (n a d) -> p n a d", a=2, d=HD1)
                for a in range(2):
                    m = act.copy(vblk[64 * a:64 * a + 64, s, :, a * HD1:(a + 1) * HD1], src[:, :, a])
            m.then_inc(S["vblk_set"], 1)

        def weights(i):
            for n in range(3):
                act.wait_ge(S["pT_ps"], i * 3 + n + 1)
                w = 4 if n < 2 else 1
                act.copy(probT[:, 4 * n:4 * n + w].rearrange("p m n -> p (m n)"),
                         (pt[0], pt[1], pr)[n][:, 0:w * P]).then_inc(S["pT_done"], 1)

        def out(i):
            act.wait_ge(S["o_ps"], i + 1)
            act.wait_ge(S["x_ps"], i)
            act.copy(oT[:].rearrange("p k n -> p (k n)"), po[:, 0:KT * P]).then_inc(S["o_done"], 1)

        def turned(i):
            act.wait_ge(S["x1T_ps"], i + 1)
            for k in range(KT):
                m = act.copy(x1T[:, k, :, bass.ds(i * 2, 2)].rearrange("p t s -> p s t"),
                             px[:, k * P:(k + 1) * P].rearrange("p (s t) -> p s t", s=2))
            m.then_inc(S["x1T_done"], 1)

        act.wait_ge(S["pads"], 2)
        queries(0)
        stage_v(0)
        values(0)
        queries(1)
        exps(0)

        def step(i, first=False, last=False):
            if not last:
                queries(i + 2)
            weights(i)
            exps(i + 1)
            if not first:
                turned(i - 1)
            out(i)
            stage_v(i + 1)
            values(i + 1)

        step(0, first=True)
        step(1)
        with act.Fori(2, PAIRS - 2) as i:
            step(i)
        step(PAIRS - 2, last=True)
        weights(PAIRS - 1)
        turned(PAIRS - 2)
        out(PAIRS - 1)
        turned(PAIRS - 1)


def layer1_room(x1T):
    room = x1T[:].rearrange("p k t b -> p (k t b)")
    at = L * B
    assert FT * P + D + 5 * STEPS2 * E <= MAIN * 2 * B
    first = at + FT * P + D
    routing = [cut(room, first + n * STEPS2 * E, (STEPS2, E)) for n in range(5)]
    return cut(room, at, (FT, P)), cut(room, at + FT * P, (D,)), routing


def by_parity(ap, par, j, n):
    return ap.rearrange("b (j r) d -> b j r d", r=2)[:, bass.ds(j, n), par]


def recurrence(nc, c, sbuf, sem, t, const, ident, cond, wx, wh, b, ow1, rw, start_loaded, x1T, h_rows, logits, x1_d, x1_rows, ob1, w2_parts, hid_parts, mlp,
               ew1, ew2, eb1, e_loaded):
    ow2 = sbuf(c, "ow2", [P, FT, D])
    rbias, ob2 = sbuf(c, "rbias", [P, E]), sbuf(c, "ob2", [P, D])
    h = [sbuf(c, f"h{u}", [P, KT, 2 * B]) for u in range(2)]
    hid = sbuf(c, "ohid", [P, FT, P])
    hid_hi, hid_lo = (part[:, :, 0:P] for part in hid_parts)
    ow2_hi, ow2_lo = w2_parts
    y = sbuf(c, "oy", [P, D])
    ph = [[c.enter_context(nc.psum_tensor(f"ph{u}{m}", [P, 512], F32)) for m in range(KT)] for u in range(2)]
    pm = [c.enter_context(nc.psum_tensor(f"pm{n}", [P, 512], F32)) for n in range(2)]
    py = c.enter_context(nc.psum_tensor("py", [P, 512], F32))
    pr = c.enter_context(nc.psum_tensor("prow", [P, 512], F32))
    names = ("rest_loaded base_done condT_ps h0_done h_ps h_done kept ow2_hi_done ow2_lo_done row_ps row_done logit_done")
    S = {n: sem(c, "r_" + n) for n in names.split()}
    x1_loaded = [sem(c, f"r_x1_loaded{n}") for n in range(4)]
    block = c.enter_context(nc.Block())
    CHUNK = STEPS2 // 4

    @block.sync
    def _(sp):
        rest = [
            (rbias[:], t["L1_ffn_router_b"].partition_broadcast(P)), (ob2[:], t["L1_ffn_ob2"].partition_broadcast(P)),
            (ow2[:], t["L1_ffn_ow2"].rearrange("(k p) n -> p k n", p=P)),
            (ob1[:], t["L1_ffn_ob1"].rearrange("(m p) -> p m", p=P)),
        ]
        for dst, src in rest:
            with nc.allow_non_contiguous_dma(reason="bias columns"):
                sp.dma_start(dst, src).then_inc(S["rest_loaded"], 16)
        for n in range(4):
            for par in range(2):
                sp.dma_start(x1_rows[64 * par:64 * par + 64, n * CHUNK:(n + 1) * CHUNK],
                             by_parity(x1_d, par, n * CHUNK, CHUNK)).then_inc(x1_loaded[n], 16)
        for e in range(2):
            load_expert(nc, sp, t, e, ew1[e], ew2[e], eb1[e], e_loaded[e])
        with sp.Fori(0, MAIN) as j:
            sp.wait_ge(mlp["y_done"], j + 1)
            for par in range(2):
                sp.dma_start(by_parity(t["out"], par, j, 1).rearrange("b j d -> b (j d)"),
                             y[64 * par:64 * par + 64]).then_inc(mlp["stored"], 16)
        sp.wait_ge(mlp["stored"], 32 * MAIN)

    @block.gpsimd
    def _(pool):
        pool.wait_ge(S["rest_loaded"], 64)
        for n in range(4):
            pool.wait_ge(x1_loaded[n], 32)
            with pool.Fori(n * CHUNK, (n + 1) * CHUNK) as j:
                row = x1_rows[:, bass.ds(j, 1)].rearrange("p a d -> p (a d)")
                pool.tensor_tensor(row, row, ob2[:], ALU.add).then_inc(S["base_done"], 1)
        with pool.Fori(MAIN // 2, STEPS2 // 2) as n:
            for u in range(2):
                pool.wait_ge(S["h_done"], n * 8 + (4 * u + 4))
                pool.tensor_copy(x1T[:, :, bass.ds(n * 4 + 2 * u, 2)],
                                 h[u][:].rearrange("p k (t b) -> p k t b", b=B)).then_inc(S["kept"], 1)

    @block.tensor
    def _(pe):
        def inputs(j, u):
            for m in range(KT):
                for k in range(KT):
                    pe.matmul(ph[u][m][:, 0:P], wx[:, k, m * P:(m + 1) * P],
                              x1T[:, k, bass.ds(j * 2, 2)].rearrange("p t b -> p (t b)"),
                              start=(k == 0), stop=(k == KT - 1), skip_group_check=True)

        def step(j, u, par, first=False):
            src, o = (h[1 - u], B) if par == 0 else (h[u], 0)
            if first:
                pe.wait_ge(S["h0_done"], 1)
            else:
                pe.wait_ge(S["h_done"], j * 4 + 2 * par)
            for k in range(KT):
                for m in range(KT):
                    ins = pe.matmul(ph[u][m][:, par * B:(par + 1) * B], wh[:, k, m * P:(m + 1) * P], src[:, k, o:o + B],
                                    start=False, stop=True, skip_group_check=True)
                    if k == KT - 1:
                        ins.then_inc(S["h_ps"], 1)

        def mlp_up(j, u):
            pe.wait_ge(S["h_done"], j * 4 + 4)
            pe.wait_ge(mlp["hid_done"], j * 8)
            for half in range(2):
                for n in range(4):
                    for k in range(KT):
                        f = 4 * half + n
                        m = pe.matmul(pm[half][:, n * P:(n + 1) * P], ow1[:, k, f * P:(f + 1) * P], h[u][:, k],
                                      start=(k == 0), stop=(k == KT - 1))
                m.then_inc(mlp["hid_ps"], 1)

        def rows_and_logits(j, u):
            pe.wait_ge(S["h_done"], j * 4 + 4)
            pe.wait_ge(S["row_done"], j)
            pe.wait_ge(S["logit_done"], j)
            for k in range(KT):
                m = pe.transpose(pr[:, k * P:(k + 1) * P], h[u][:, k], ident)
            for k in range(KT):
                m = pe.matmul(pr[:, D:D + E], h[u][:, k], rw[:, k], start=(k == 0), stop=(k == KT - 1))
            m.then_inc(S["row_ps"], 1)

        def mlp_down(j):
            pe.wait_ge(mlp["y_done"], j)
            pe.wait_ge(mlp["hi_done"], j + 1)
            pe.wait_ge(mlp["lo_done"], j + 1)
            for f in range(FT):
                pe.matmul(py[:, 0:D], hid_lo[:, f], ow2_hi[:, f], start=(f == 0), stop=False)
                pe.matmul(py[:, 0:D], hid_hi[:, f], ow2_lo[:, f], start=False, stop=False)
                m = pe.matmul(py[:, 0:D], hid_hi[:, f], ow2_hi[:, f], start=False, stop=(f == FT - 1))
            m.then_inc(mlp["y_ps"], 1)

        pe.wait_ge(start_loaded, 96)
        for k in range(KT):
            m = pe.transpose(py[:, k * B:(k + 1) * B], cond[:, k * P:(k + 1) * P], ident[0:B, 0:B])
        m.then_inc(S["condT_ps"], 1)
        inputs(0, 0)
        step(0, 0, 0, True)
        step(0, 0, 1)

        def pair(j, u, first=False):
            inputs(j, u)
            step(j, u, 0)
            mlp_up(j - 1, 1 - u)
            step(j, u, 1)
            rows_and_logits(j - 1, 1 - u)
            if not first:
                mlp_down(j - 2)

        pair(1, 1, True)
        pe.wait_ge(S["ow2_lo_done"], 1)
        with pe.Fori(1, MAIN // 2) as n:
            for u in range(2):
                pair(n * 2 + u, u)
        pair(MAIN, 0)
        inputs(MAIN + 1, 1)
        step(MAIN + 1, 1, 0)
        mlp_down(MAIN - 1)
        rows_and_logits(MAIN, 0)
        step(MAIN + 1, 1, 1)
        with pe.Fori(MAIN // 2 + 1, STEPS2 // 2) as n:
            for u in range(2):
                j = n * 2 + u
                inputs(j, u)
                step(j, u, 0)
                rows_and_logits(j - 1, 1 - u)
                step(j, u, 1)
        rows_and_logits(STEPS2 - 1, 1)

    @block.scalar
    def _(act):
        act.wait_ge(start_loaded, 96)
        act.wait_ge(S["condT_ps"], 1)
        act.copy(h[1][:, :, B:], py[:, 0:KT * B].rearrange("p (k b) -> p k b", b=B)).then_inc(S["h0_done"], 1)
        def split(j):
            act.wait_ge(mlp["hid_done"], j * 8 + 8)
            act.wait_ge(mlp["y_ps"], j)
            act.copy(hid_hi, hid[:]).then_inc(mlp["hi_done"], 1)

        def tanh(n, u):
            for par in range(2):
                for m in range(KT):
                    act.wait_ge(S["h_ps"], n * 8 + (4 * u + 2 * par + m + 1))
                    act.activation(h[u][:, m, par * B:(par + 1) * B], ph[u][m][:, par * B:(par + 1) * B], ACT.Tanh,
                                   bias=b[:, m:m + 1]).then_inc(S["h_done"], 1)

        tanh(0, 0)
        act.wait_ge(S["rest_loaded"], 64)
        act.copy(ow2_hi[:], ow2[:]).then_inc(S["ow2_hi_done"], 1)
        tanh(0, 1)
        split(0)
        with act.Fori(1, MAIN // 2) as n:
            for u in range(2):
                tanh(n, u)
                split(n * 2 + u - 1)
        tanh(MAIN // 2, 0)
        split(MAIN - 1)
        tanh(MAIN // 2, 1)
        with act.Fori(MAIN // 2 + 1, STEPS2 // 2) as n:
            for u in range(2):
                act.wait_ge(S["kept"], n * 2 + (u - MAIN - 1))
                tanh(n, u)

    @block.vector
    def _(dve):
        def hidden(j):
            dve.wait_ge(mlp["lo_done"], j)
            for half in range(2):
                dve.wait_ge(mlp["hid_ps"], j * 2 + half + 1)
                for n in range(4):
                    f = 4 * half + n
                    dve.tensor_scalar(hid[:, f], pm[half][:, n * P:(n + 1) * P], ob1[:, f:f + 1], 0.0,
                                      ALU.add, ALU.max).then_inc(mlp["hid_done"], 1)

        def rows(j):
            dve.wait_ge(S["row_ps"], j + 1)
            dve.tensor_copy(h_rows[:, bass.ds(j, 1), 0:D].rearrange("p a d -> p (a d)"), pr[:, 0:D]).then_inc(S["row_done"], 1)
            dve.tensor_tensor(logits[:, bass.ds(j, 1)].rearrange("p a e -> p (a e)"), pr[:, D:D + E], rbias[:],
                              ALU.add).then_inc(S["logit_done"], 1)

        def low(j):
            dve.wait_ge(mlp["y_ps"], j)
            dve.wait_ge(mlp["hi_done"], j + 1)
            dve.tensor_tensor(hid_lo, hid[:], hid_hi.bitcast(F32), ALU.subtract).then_inc(mlp["lo_done"], 1)

        def out(j):
            dve.wait_ge(mlp["y_ps"], j + 1)
            dve.wait_ge(mlp["stored"], j * 32)
            dve.wait_ge(S["base_done"], j + 1)
            dve.tensor_tensor(y[:], py[:, 0:D], x1_rows[:, bass.ds(j, 1)].rearrange("p a d -> p (a d)"),
                              ALU.add).then_inc(mlp["y_done"], 1)

        dve.tensor_copy(h_rows[:, :, D].bitcast(U32), const("tok"))
        dve.wait_ge(S["rest_loaded"], 64)
        dve.wait_ge(S["ow2_hi_done"], 1)
        dve.tensor_tensor(ow2_lo[:], ow2[:], ow2_hi[:].bitcast(F32), ALU.subtract).then_inc(S["ow2_lo_done"], 1)
        hidden(0)
        rows(0)
        low(0)
        with dve.Fori(1, MAIN) as j:
            hidden(j)
            rows(j)
            out(j - 1)
            low(j)
        out(MAIN - 1)
        with dve.Fori(MAIN, STEPS2) as j:
            rows(j)


def load_expert(nc, eng, t, e, w1, w2, b1, loaded):
    eng.dma_start(w1, t["L1_ffn_w1"][bass.ds(e, 1)].rearrange("a (k p) n -> p (a k) n", p=P)).then_inc(loaded, 16)
    eng.dma_start(w2, t["L1_ffn_w2"][bass.ds(e, 1)].rearrange("a (k p) n -> p (a k) n", p=P)).then_inc(loaded, 16)
    with nc.allow_non_contiguous_dma(reason="bias columns"):
        eng.dma_start(b1[:], t["L1_ffn_b1"][bass.ds(e, 1)].rearrange("a (m p) -> p (a m)", p=P)).then_inc(loaded, 16)


def experts(nc, c, sbuf, sem, t, const, ident, h_rows, logits, x1_d, xtab_d, fv, x1T, ob1, ow1, w2_parts, hid_parts, mlp,
            ew1, ew2, eb1, e_loaded):
    big = [P, STEPS2, E]
    hid, y, (eq, cand, hot, count, rank) = layer1_room(x1T)
    top, eid, pos, ok, slot, gap = (sbuf(c, n, [P, STEPS2]) for n in ("top", "eid", "pos", "ok", "slot", "gap"))
    ones = sbuf(c, "ones", [P, STEPS2])
    idx, ids = sbuf(c, "idx", [P, STEPS2], U32), sbuf(c, "ids", [P, E, 3], U32)
    v_room, x_room = fv[:].rearrange("p j d -> p (j d)"), x1T[:].rearrange("p k t b -> p (k t b)")
    b2 = cut(v_room, 0, (E, D))
    ye = [cut(v_room, (E + 3 * u) * D, (3, D)) for u in range(2)]
    hT = cut(v_room, (E + 6) * D, (FT, CAP))
    xe = [cut(x_room, 3 * u * (D + 1), (3, D + 1)) for u in range(2)]
    base = [cut(x_room, 6 * (D + 1) + 3 * u * D, (3, D)) for u in range(2)]
    w1_hi, w1_lo = (sbuf(c, n, [P, KT, HID], F32R) for n in ("ew1_hi", "ew1_lo"))
    w2_hi, w2_lo = w2_parts
    xT_hi, xT_lo = sbuf(c, "xeT_hi", [P, KT, CAP], F32R), sbuf(c, "xeT_lo", [P, KT, CAP], F32R)
    hT_hi, hT_lo = hid_parts
    pxT = c.enter_context(nc.psum_tensor("pxT", [P, KT, 512], F32))
    phid = [c.enter_context(nc.psum_tensor(f"phid{n}", [P, 512], F32)) for n in range(4)]
    pyo = [c.enter_context(nc.psum_tensor(f"pyo{n}", [P, 512], F32)) for n in range(2)]
    names = ("b2_loaded hot_done rank_ps idx_done base_zero ids_kept scattered xT_ps xT_hi xT_lo hid_ps hid_act hid_dve "
             "hid_hi hid_lo w1_hi w1_lo w2_hi w2_lo y_ps b2_done y_done")
    S = {n: sem(c, "e_" + n) for n in names.split()}
    step = sem(c, "e_step")
    x_loaded = [sem(c, f"e_x_loaded{u}") for u in range(2)]
    base_loaded = [sem(c, f"e_base_loaded{u}") for u in range(2)]
    y_stored = [sem(c, f"e_y_stored{u}") for u in range(2)]
    block = c.enter_context(nc.Block())
    x1_table, out_table = (a.rearrange("b l d -> (b l) d") for a in (x1_d, t["out"]))

    @block.sync
    def _(sp):
        sp.dma_start(b2.rearrange("p e d -> p (e d)"),
                     t["L1_ffn_b2"].rearrange("e d -> (e d)").partition_broadcast(P)).then_inc(S["b2_loaded"], 16)

        def store_late(j):
            sp.wait_ge(mlp["y_done"], j + 1)
            for par in range(2):
                sp.dma_start(by_parity(t["out"], par, j, 1).rearrange("b j d -> b (j d)"),
                             y[64 * par:64 * par + 64]).then_inc(mlp["stored"], 16)

        with sp.Fori(MAIN, STEPS2 - 1) as j:
            store_late(j)
        sp.wait_ge(S["scattered"], 16 * STEPS2)

        def load_rows(e, u):
            sp.dma_start(xe[u][:, 0:2], xtab_d[bass.ds(e * CAP, 2 * P)].rearrange("(n p) d -> p n d", p=P)).then_inc(x_loaded[u], 16)
            sp.dma_start(xe[u][0:64, 2], xtab_d[bass.ds(e * CAP + 2 * P, 64)]).then_inc(x_loaded[u], 16)

        for u in range(2):
            load_rows(u, u)
        store_late(STEPS2 - 1)
        with sp.Fori(0, E // 2 - 1) as n:
            for u in range(2):
                e = n * 2 + u
                sp.wait_ge(S["w1_lo"], e + 1)
                sp.wait_ge(S["w2_lo"], e + 1)
                sp.wait_ge(S["hid_act"], e * 4 + 4)
                sp.wait_ge(S["hid_dve"], e * 4 + 4)
                load_expert(nc, sp, t, e + 2, ew1[u], ew2[u], eb1[u], e_loaded[u])
                sp.wait_ge(S["xT_ps"], e + 1)
                sp.wait_ge(S["ids_kept"], e * 2 + 2)
                load_rows(e + 2, u)

    @block.gpsimd
    def _(pool):
        last_token = pool.to_reg(B * L - 1)

        def low_second(e, u):
            pool.wait_ge(S["w2_hi"], e + 1)
            pool.tensor_tensor(w2_lo[:], ew2[u], w2_hi[:].bitcast(F32), ALU.subtract).then_inc(S["w2_lo"], 1)

        def token(e, i, w):
            return bass.IndirectOffsetOnAxis(ids[0:w, e, i:i + 1], 0)

        def residual(e):
            u = e % 2
            pool.wait_ge(S["ids_kept"], e * 2 + 2)
            pool.wait_ge(S["y_done"], max(e - 1, 0) * 3)
            for i, (o, w) in enumerate(CAPT):
                pool.indirect_dma_start(base[u][0:w, i], None, x1_table, token(e, i, w), bounds_check=last_token,
                                        oob_is_err=False).then_inc(base_loaded[u], 16)

        def rows_out(e):
            u = e % 2
            for i, (o, w) in enumerate(CAPT):
                pool.wait_ge(S["y_done"], 3 * e + i + 1)
                pool.indirect_dma_start(out_table, token(e, i, w), ye[u][0:w, i], None, bounds_check=last_token,
                                        oob_is_err=False).then_inc(y_stored[u], 16)

        for u in range(2):
            pool.memset(base[u], 0.0).then_inc(S["base_zero"], 1)
        pool.wait_ge(S["idx_done"], 1)
        for j in range(STEPS2):
            pool.indirect_dma_start(xtab_d, bass.IndirectOffsetOnAxis(idx[:, j:j + 1], 0), h_rows[:, j], None).then_inc(S["scattered"], 16)
        low_second(0, 0)
        pool.wait_ge(S["base_zero"], 2)
        residual(0)
        residual(1)
        for e in range(1, E):
            low_second(e, e % 2)
            if e == 1:
                pool.wait_ge(mlp["stored"], 32 * STEPS2)
            rows_out(e - 1)
            if e + 1 < E:
                residual(e + 1)
        rows_out(E - 1)
        for u in range(2):
            pool.wait_ge(y_stored[u], 48 * (E // 2))

    @block.tensor
    def _(pe):
        pe.wait_ge(S["hot_done"], 1)
        flat = "p j e -> p (j e)"
        pe.matmul(pxT[:, 0, 0:STEPS2 * E], const("same_b"), count.rearrange(flat), start=True, stop=False)
        pe.matmul(pxT[:, 0, 0:STEPS2 * E], const("drop"), hot.rearrange(flat), start=False, stop=False)
        pe.matmul(pxT[:, 0, 0:STEPS2 * E], const("before"),
                  count[:, STEPS2 - 1].unsqueeze(1).broadcast_to(big), start=False, stop=True).then_inc(S["rank_ps"], 1)

        def late_up(j):
            pe.wait_ge(mlp["hid_done"], j * FT)
            for half in range(2):
                for n in range(4):
                    f = 4 * half + n
                    for k in range(KT):
                        m = pe.matmul(phid[half][:, n * P:(n + 1) * P], ow1[:, k, f * P:(f + 1) * P],
                                      x1T[:, k, bass.ds(j * 2, 2)].rearrange("p t b -> p (t b)"),
                                      start=(k == 0), stop=(k == KT - 1))
                m.then_inc(mlp["hid_ps"], 1)

        def late_down(j):
            pe.wait_ge(mlp["y_done"], j)
            pe.wait_ge(mlp["hi_done"], j + 1)
            pe.wait_ge(mlp["lo_done"], j + 1)
            for f in range(FT):
                hi, lo = hT_hi[:, f, 0:P], hT_lo[:, f, 0:P]
                pe.matmul(pyo[0][:, 0:D], lo, w2_hi[:, f], start=(f == 0), stop=False)
                pe.matmul(pyo[0][:, 0:D], hi, w2_lo[:, f], start=False, stop=False)
                m = pe.matmul(pyo[0][:, 0:D], hi, w2_hi[:, f], start=False, stop=(f == FT - 1))
            m.then_inc(mlp["y_ps"], 1)

        late_up(MAIN)
        with pe.Fori(MAIN + 1, STEPS2) as j:
            late_up(j)
            late_down(j - 1)
        late_down(STEPS2 - 1)
        pe.wait_ge(S["idx_done"], 1)
        pe.wait_ge(mlp["y_done"], STEPS2)

        def turn(e, n, u):
            pe.wait_ge(x_loaded[u], n * 32 + 32)
            pe.wait_ge(S["xT_lo"], e)
            for k in range(KT):
                for i, (o, w) in enumerate(CAPT):
                    m = pe.transpose(pxT[:, k, o:o + w], xe[u][0:w, i, k * P:(k + 1) * P], ident[0:w, 0:w])
            m.then_inc(S["xT_ps"], 1)

        def up(e, n, u):
            for part in ("xT_hi", "xT_lo", "w1_hi", "w1_lo"):
                pe.wait_ge(S[part], e + 1)
            for f in range(FT):
                pe.wait_ge(S["hid_act"] if f % 2 == 0 else S["hid_dve"], e * 4 + max(f // 2 - 1, 0))
                for k in range(KT):
                    hi, lo = w1_hi[:, k, f * P:(f + 1) * P], w1_lo[:, k, f * P:(f + 1) * P]
                    pe.matmul(phid[f % 4][:, 0:CAP], lo, xT_hi[:, k], start=(k == 0), stop=False)
                    pe.matmul(phid[f % 4][:, 0:CAP], hi, xT_lo[:, k], start=False, stop=False)
                    m = pe.matmul(phid[f % 4][:, 0:CAP], hi, xT_hi[:, k], start=False, stop=(k == KT - 1))
                m.then_inc(S["hid_ps"], 1)

        def down(e, u):
            pe.wait_ge(S["w2_hi"], e + 1)
            pe.wait_ge(S["w2_lo"], e + 1)
            for i, (o, w) in enumerate(CAPT):
                pe.wait_ge(S["b2_done"], e * 3 + max(i - 1, 0))
                out = pyo[0 if i != 1 else 1][0:w, 0:D]
                for f in range(FT):
                    if i == 0:
                        pe.wait_ge(S["hid_hi"], e * FT + f + 1)
                        pe.wait_ge(S["hid_lo"], e * FT + f + 1)
                    hi, lo = hT_hi[:, f, o:o + w], hT_lo[:, f, o:o + w]
                    pe.matmul(out, lo, w2_hi[:, f], start=(f == 0), stop=False)
                    pe.matmul(out, hi, w2_lo[:, f], start=False, stop=False)
                    m = pe.matmul(out, hi, w2_hi[:, f], start=False, stop=(f == FT - 1))
                m.then_inc(S["y_ps"], 1)

        turn(0, 0, 0)
        def two(n):
            for u in range(2):
                up(n * 2 + u, n, u)
                turn(n * 2 + u + 1, n + u, 1 - u)
                down(n * 2 + u, u)

        two(0)
        with pe.Fori(1, E // 2 - 1) as n:
            two(n)
        up(E - 2, E // 2 - 1, 0)
        turn(E - 1, E // 2 - 1, 1)
        down(E - 2, 0)
        up(E - 1, E // 2 - 1, 1)
        down(E - 1, 1)

    @block.scalar
    def _(act):
        def high_first(e, u, n):
            act.wait_ge(e_loaded[u], n * 48 + 48)
            act.wait_ge(S["hid_ps"], e * FT)
            act.copy(w1_hi[:], ew1[u]).then_inc(S["w1_hi"], 1)

        def high_rows(e):
            act.wait_ge(S["xT_ps"], e + 1)
            act.copy(xT_hi[:], pxT[:, :, 0:CAP]).then_inc(S["xT_hi"], 1)

        def high_second(e, u):
            act.wait_ge(mlp["y_ps"], STEPS2)
            act.wait_ge(S["y_ps"], e * 3)
            act.copy(w2_hi[:], ew2[u]).then_inc(S["w2_hi"], 1)

        def hidden(e, u):
            for f in range(FT):
                if f % 2 == 0:
                    act.wait_ge(S["hid_ps"], e * FT + (f + 1))
                    act.activation(hT[:, f], phid[f % 4][:, 0:CAP], ACT.Relu, bias=eb1[u][:, f:f + 1]).then_inc(S["hid_act"], 1)
                    act.wait_ge(S["hid_act"], e * 4 + (f // 2 + 1))
                else:
                    act.wait_ge(S["hid_dve"], e * 4 + (f // 2 + 1))
                act.copy(hT_hi[:, f], hT[:, f]).then_inc(S["hid_hi"], 1)

        def one(n, u, last=False):
            e = n * 2 + u
            hidden(e, u)
            if not last:
                high_first(e + 1, 1 - u, n + u)
                high_rows(e + 1)
                high_second(e + 1, 1 - u)

        def late_high(j):
            act.wait_ge(mlp["hid_done"], j * FT + FT)
            act.wait_ge(mlp["y_ps"], j)
            act.copy(hT_hi[:, :, 0:P], hid).then_inc(mlp["hi_done"], 1)

        high_first(0, 0, 0)
        with act.Fori(MAIN, STEPS2) as j:
            late_high(j)
        high_second(0, 0)
        high_rows(0)
        with act.Fori(0, E // 2 - 1) as n:
            one(n, 0)
            one(n, 1)
        one(E // 2 - 1, 0)
        one(E // 2 - 1, 1, True)

    @block.vector
    def _(dve):
        done = 0

        def then(ins):
            nonlocal done
            done += 1
            ins.then_inc(step, 1)
            dve.wait_ge(step, done)

        e_minus = const("e_minus").unsqueeze(1).broadcast_to(big)
        dve.memset(ones[:], 1.0)
        then(dve.tensor_reduce(top[:], logits[:], X, ALU.max))
        then(dve.tensor_tensor(eq, logits[:], bc(top[:], big), ALU.is_equal))
        then(dve.tensor_tensor(cand, eq, e_minus, ALU.mult))
        then(dve.tensor_reduce(eid[:], cand, X, ALU.min))
        then(dve.tensor_tensor(hot, e_minus, bc(eid[:], big), ALU.is_equal))
        for n in range(E):
            m = dve.tensor_tensor_scan(count[:, :, n], ones[:], hot[:, :, n], 0.0, ALU.mult, ALU.add)
        m.then_inc(S["hot_done"], 1)
        dve.wait_ge(S["rank_ps"], 1)
        then(dve.tensor_tensor(rank, hot, pxT[:, 0, 0:STEPS2 * E].rearrange("p (j e) -> p j e", e=E), ALU.mult))
        then(dve.tensor_reduce(pos[:], rank, X, ALU.add))
        then(dve.tensor_scalar(ok[:], pos[:], float(CAP), None, ALU.is_lt))
        then(dve.tensor_scalar(slot[:], eid[:], float(E), float(CAP), ALU.add, ALU.mult))
        then(dve.tensor_tensor(slot[:], slot[:], pos[:], ALU.add))
        then(dve.tensor_tensor(gap[:], slot[:], const("own"), ALU.subtract))
        then(dve.tensor_tensor(gap[:], gap[:], ok[:], ALU.mult))
        dve.tensor_tensor(idx[:], gap[:], const("own"), ALU.add).then_inc(S["idx_done"], 1)
        dve.wait_ge(S["b2_loaded"], 16)

        def low_rows(e, u):
            dve.wait_ge(S["xT_hi"], e + 1)
            dve.tensor_tensor(xT_lo[:], pxT[:, :, 0:CAP], xT_hi[:].bitcast(F32), ALU.subtract).then_inc(S["xT_lo"], 1)
            for i, w in ((slice(0, 2), P), (slice(2, 3), 64)):
                dve.tensor_copy(ids[0:w, bass.ds(e, 1), i].rearrange("p a i -> p (a i)"),
                                xe[u][0:w, i, D].bitcast(U32)).then_inc(S["ids_kept"], 1)

        def one(n, u, last=False):
            e = n * 2 + u
            for f in range(FT):
                if f % 2 == 1:
                    dve.wait_ge(S["hid_ps"], e * FT + (f + 1))
                    dve.tensor_scalar(hT[:, f], phid[f % 4][:, 0:CAP], eb1[u][:, f:f + 1], 0.0, ALU.add, ALU.max).then_inc(S["hid_dve"], 1)
                if f > 0:
                    low(e, f - 1)
            low(e, FT - 1)
            if not last:
                low_first(e + 1, 1 - u)
            for i, (o, w) in enumerate(CAPT):
                if i == 1 and not last:
                    low_rows(e + 1, 1 - u)
                dve.wait_ge(S["y_ps"], e * 3 + (i + 1))
                dve.wait_ge(y_stored[u], n * 48)
                dve.tensor_tensor(ye[u][0:w, i], pyo[0 if i != 1 else 1][0:w, 0:D],
                                  b2[0:w, bass.ds(e, 1)].rearrange("p a d -> p (a d)"), ALU.add).then_inc(S["b2_done"], 1)
                dve.wait_ge(S["b2_done"], e * 3 + (i + 1))
                dve.wait_ge(base_loaded[u], n * 48 + 48)
                dve.tensor_tensor(ye[u][0:w, i], ye[u][0:w, i], base[u][0:w, i], ALU.add).then_inc(S["y_done"], 1)

        def low(e, f):
            dve.wait_ge(S["hid_hi"], e * FT + (f + 1))
            dve.tensor_tensor(hT_lo[:, f], hT[:, f], hT_hi[:, f].bitcast(F32), ALU.subtract).then_inc(S["hid_lo"], 1)

        def low_first(e, u):
            dve.wait_ge(S["w1_hi"], e + 1)
            dve.tensor_tensor(w1_lo[:], ew1[u], w1_hi[:].bitcast(F32), ALU.subtract).then_inc(S["w1_lo"], 1)

        def late_hidden(j):
            dve.wait_ge(mlp["lo_done"], j)
            for half in range(2):
                dve.wait_ge(mlp["hid_ps"], j * 2 + half + 1)
                for n in range(4):
                    f = 4 * half + n
                    dve.tensor_scalar(hid[:, f], phid[half][:, n * P:(n + 1) * P], ob1[:, f:f + 1], 0.0,
                                      ALU.add, ALU.max).then_inc(mlp["hid_done"], 1)

        def late_low(j):
            dve.wait_ge(mlp["y_ps"], j)
            dve.wait_ge(mlp["hi_done"], j + 1)
            dve.tensor_tensor(hT_lo[:, :, 0:P], hid, hT_hi[:, :, 0:P].bitcast(F32), ALU.subtract).then_inc(mlp["lo_done"], 1)

        def late_out(j):
            dve.wait_ge(mlp["y_ps"], j + 1)
            dve.wait_ge(mlp["stored"], j * 32)
            dve.tensor_tensor(y, pyo[0][:, 0:D], fv[:, bass.ds(j, 1)].rearrange("p a d -> p (a d)"),
                              ALU.add).then_inc(mlp["y_done"], 1)

        late_hidden(MAIN)
        late_low(MAIN)
        with dve.Fori(MAIN + 1, STEPS2) as j:
            late_hidden(j)
            late_out(j - 1)
            late_low(j)
        late_out(STEPS2 - 1)
        low_first(0, 0)
        low_rows(0, 0)
        one(0, 0)
        one(0, 1)
        with dve.Fori(1, E // 2 - 1) as n:
            one(n, 0)
            one(n, 1)
        one(E // 2 - 1, 0)
        one(E // 2 - 1, 1, True)


_NAMES = ["x", "cond_1024", "L0_cond_WQ_w", "L0_cond_WQ_b", "L0_cond_WK_w", "L0_cond_WK_b", "L0_cond_WV_w",
          "L0_cond_WV_b", "L0_cond_WO_w", "L0_cond_WO_b", "L0_ffn_g_info", "L0_ffn_W_qkv", "L0_ffn_W_proj",
          "L0_ffn_b_proj", "L1_cond_Wx", "L1_cond_Wh", "L1_cond_b", "L1_ffn_router_w", "L1_ffn_router_b", "L1_ffn_w1",
          "L1_ffn_b1", "L1_ffn_w2", "L1_ffn_b2", "L1_ffn_ow1", "L1_ffn_ob1", "L1_ffn_ow2", "L1_ffn_ob2"]


def kernel(**inputs):
    import concourse.bacc as bacc
    from concourse.bass_utils import run_bass_kernel_spmd as run

    nc = bacc.Bacc("TRN2", target_bir_lowering=False, num_devices=1)
    arrays, tensors = {}, {}
    table, const_at = shape_constants()
    given = {n: np.ascontiguousarray(inputs[n]) for n in _NAMES}
    given["consts"] = table
    for name, a in given.items():
        arrays["in_" + name] = a
        tensors[name] = nc.dram_tensor("in_" + name, a.shape, mybir.dt.from_np(a.dtype), kind="ExternalInput").ap()
    tensors["out"] = nc.dram_tensor("out_0", (B, L, D), F32, kind="ExternalOutput").ap()
    build(nc, tensors, const_at)
    return run(nc, [arrays], core_ids=[0]).results[0]["out_0"]
```
